# Optimizing a Trainium2 kernel written in Bass

```python
import numpy as np
import jax
import jax.numpy as jnp

def _softmax(x, axis=-1):
    return jax.nn.softmax(x, axis=axis)

def _gelu(x):
    return jax.nn.gelu(x, approximate=True)

def _silu(x):
    return jax.nn.silu(x)

def _sigmoid(x):
    return jax.nn.sigmoid(x)

def _layernorm(x, axis=-1, eps=1e-05):
    m = jnp.mean(x, axis=axis, keepdims=True)
    v = jnp.var(x, axis=axis, keepdims=True)
    return (x - m) / jnp.sqrt(v + eps)

def _scatter_add(tgt, idx, src, axis=0):
    return tgt.at[idx].add(src)

def _segment_sum(src, seg, n):
    return jax.ops.segment_sum(src, seg, n)
kernel_name = 'mk_xattn_ffn_d4_seqx_r8_65de11'

def setup_inputs(seed: int=0):
    np.random.seed(seed)
    _w = jnp.asarray

    def _rec_inputs():
        import jax
        import jax.numpy as jnp
        _rk = jax.random.key(seed)
        x = -0.000125 + 0.9999 * jax.random.normal(jax.random.fold_in(_rk, 1), (2, 256, 512), jnp.float32)
        _lenS = 256 - jax.random.randint(jax.random.fold_in(_rk, 7), (2,), 0, max(1, 256 // 4) + 1, jnp.int32)
        _lenS2 = 512 - jax.random.randint(jax.random.fold_in(_rk, 8), (2,), 0, max(1, 512 // 4) + 1, jnp.int32)
        _ctx_4096P = jax.random.normal(jax.random.fold_in(_rk, 11), (2, 16, 512), jnp.float32)
        _ctx_4096c = jax.random.dirichlet(jax.random.fold_in(_rk, 511), 0.3 * jnp.ones((16,), jnp.float32), (2, 512))
        _ctx_4096t = jnp.einsum('bsk,bkd->bsd', _ctx_4096c, _ctx_4096P)
        _ctx_4096t = _ctx_4096t * jax.lax.rsqrt(jnp.mean(jnp.square(_ctx_4096t)) + 1e-12) * 0.953939
        ctx_4096 = -5.72187e-05 + 0.999849 * (_ctx_4096t + 0.3 * jax.random.normal(jax.random.fold_in(_rk, 611), (2, 512, 512), jnp.float32))
        _validS = jnp.arange(256)[None, :] < _lenS[:, None]
        _validS2 = jnp.arange(512)[None, :] < _lenS2[:, None]
        _causal = jnp.tril(jnp.ones((256, 256), dtype=bool))
        mask_1x1xSxS2_ff0 = jnp.where(jnp.ones((1, 1, 256, 512), dtype=bool), 0.0, -1000000000.0).astype(jnp.float32)
        return (x, ctx_4096, mask_1x1xSxS2_ff0)
    x, ctx_4096, mask_1x1xSxS2_ff0 = _rec_inputs()

    def _L0_xattn_setup():
        import jax, jax.numpy as jnp
        import numpy as np
        QMIN = 0.0
        QMAX = 255.0

        def fake_quant(x, scale, zp):
            s = scale.reshape(())
            z = zp.reshape(())
            q = jnp.clip(jnp.round(x / s + z), QMIN, QMAX)
            return (q - z) * s
        key = jax.random.key(seed)
        k1, k2 = jax.random.split(key)
        B, M, K, N = (4, 256, 512, 512)
        x1 = jax.random.normal(k1, (B, M, K), dtype=jnp.float32)
        x2 = jax.random.normal(k2, (B, K, N), dtype=jnp.float32)
        x1_scale = jnp.full((1,), 8.0 / 255.0, dtype=jnp.float32)
        x1_zp = jnp.full((1,), 128.0, dtype=jnp.float32)
        x2_scale = jnp.full((1,), 8.0 / 255.0, dtype=jnp.float32)
        x2_zp = jnp.full((1,), 128.0, dtype=jnp.float32)
        return {'x1': x1, 'x2': x2, 'x1_scale': x1_scale, 'x1_zp': x1_zp, 'x2_scale': x2_scale, 'x2_zp': x2_zp}
    _L0_xattn_all = _L0_xattn_setup()
    _L0_xattn_in = {k: v for k, v in _L0_xattn_all.items() if k in ('x1_scale', 'x1_zp', 'x2_scale', 'x2_zp')}
    del _L0_xattn_all

    def _L0_ffn_setup():
        import jax, jax.numpy as jnp
        import numpy as np
        B_L, B_H = (4, 8)
        LIN_SLOPE, LIN_INTER, EST_T = (1.0, 0.0, 64.0)
        BATCH, SEQ, IN_F, OUT_F = (4, 256, 512, 512)
        MAX_BITS = 8

        def dequant_kbit(qweight, lut, bit):
            O, I32 = (qweight.shape[1], qweight.shape[2])
            shifts = jnp.arange(32, dtype=jnp.int32)
            idx = jnp.zeros((O, I32 * 32), dtype=jnp.int32)
            for p in range(bit):
                bits = (qweight[p][:, :, None] >> shifts & 1).reshape(O, I32 * 32)
                idx = idx | bits << p
            return jnp.take_along_axis(lut, idx, axis=1)
        key = jax.random.key(seed)
        k = jax.random.split(key, 5)
        x = jax.random.normal(k[0], (BATCH, SEQ, IN_F), dtype=jnp.float32)
        qweight = jax.random.randint(k[1], (MAX_BITS, OUT_F, IN_F // 32), 0, 2147483647, dtype=jnp.int32)
        lut4 = jax.random.normal(k[2], (OUT_F, 2 ** B_L), dtype=jnp.float32) * 0.02
        lut8 = jax.random.normal(k[3], (OUT_F, 2 ** B_H), dtype=jnp.float32) * 0.02
        bias = jax.random.normal(k[4], (OUT_F,), dtype=jnp.float32) * 0.01
        return {'x': x, 'qweight': qweight, 'lut4': lut4, 'lut8': lut8, 'bias': bias}
    _L0_ffn_all = _L0_ffn_setup()
    _L0_ffn_in = {k: v for k, v in _L0_ffn_all.items() if k in ('qweight', 'lut4', 'lut8', 'bias')}
    del _L0_ffn_all

    def _L1_xattn_setup():
        import jax, jax.numpy as jnp
        import numpy as np
        B, N, NKV = (2, 256, 256)
        E = 512
        H = 16
        HD = E // H
        LQ = E // 8
        LKV = E // 16
        key = jax.random.key(seed)
        ks = jax.random.split(key, 6)
        Q = jax.random.normal(ks[0], (B, N, E), dtype=jnp.float32)
        K = jax.random.normal(ks[1], (B, NKV, E), dtype=jnp.float32)
        Wq_d = jax.random.normal(ks[2], (E, LQ), dtype=jnp.float32) / np.sqrt(E)
        W_qk = jax.random.normal(ks[3], (LQ, H * LKV), dtype=jnp.float32) / np.sqrt(LQ)
        Wkv_d = jax.random.normal(ks[4], (E, LKV), dtype=jnp.float32) / np.sqrt(E)
        Wv_u = jax.random.normal(ks[5], (LKV, H * HD), dtype=jnp.float32) / np.sqrt(LKV)
        return {'Q': Q, 'K': K, 'Wq_d': Wq_d, 'W_qk': W_qk, 'Wkv_d': Wkv_d, 'Wv_u': Wv_u}
    _L1_xattn_all = _L1_xattn_setup()
    _L1_xattn_in = {k: v for k, v in _L1_xattn_all.items() if k in ('Wq_d', 'W_qk', 'Wkv_d', 'Wv_u')}
    del _L1_xattn_all

    def _L1_ffn_setup():
        import jax, jax.numpy as jnp
        import numpy as np
        import math
        SQRT7 = math.sqrt(7.0)
        EPS = 1e-05

        def int4_quant(x):
            beta = jnp.mean(jnp.abs(x), axis=-1, keepdims=True)
            x_q = jnp.clip(jnp.round(x * SQRT7 / (beta + EPS)), -8, 7)
            return x_q * (beta * SQRT7) / SQRT7

        def int8_quant(x):
            gamma = jnp.max(jnp.abs(x), axis=-1, keepdims=True)
            x_q = jnp.clip(jnp.round(x * 127.0 / (gamma + EPS)), -128, 127)
            return x_q * gamma / 127.0

        def bitlinear(x, w, scale):
            w_mean = jnp.mean(jnp.abs(w))
            w_q = jnp.clip(jnp.round(w / (w_mean + EPS)), -1.0, 1.0)
            w_eff = w_q * w_mean * scale
            return jnp.einsum('...i,oi->...o', x, w_eff)
        key = jax.random.key(seed)
        ks = jax.random.split(key, 4)
        H, I = (512, 1376)
        B, S = (2, 256)
        x = jax.random.normal(ks[0], (B, S, H), dtype=jnp.float32)
        w_gate = jax.random.uniform(ks[1], (I, H), jnp.float32, -1.0, 1.0) / np.sqrt(H)
        w_up = jax.random.uniform(ks[2], (I, H), jnp.float32, -1.0, 1.0) / np.sqrt(H)
        w_down = jax.random.uniform(ks[3], (H, I), jnp.float32, -1.0, 1.0) / np.sqrt(I)
        ones = jnp.ones((1,), jnp.float32)
        return {'x': x, 'w_gate': w_gate, 'w_up': w_up, 'w_down': w_down, 's_gate': ones, 's_up': ones, 's_down': ones}
    _L1_ffn_all = _L1_ffn_setup()
    _L1_ffn_in = {k: v for k, v in _L1_ffn_all.items() if k in ('w_gate', 'w_up', 'w_down', 's_gate', 's_up', 's_down')}
    del _L1_ffn_all

    def _L2_xattn_setup():
        import jax, jax.numpy as jnp
        import numpy as np
        NUM_HEADS = 32
        NUM_KV_HEADS = 8
        HEAD_DIM = 128
        HIDDEN = 512
        EPS = 1e-05

        def rmsnorm(x, w, eps=EPS):
            xf = x.astype(jnp.float32)
            var = jnp.mean(xf * xf, axis=-1, keepdims=True)
            return w * (xf * jax.lax.rsqrt(var + eps)).astype(x.dtype)
        key = jax.random.key(seed)
        ks = jax.random.split(key, 10)
        B, Q, KV = (1, 128, 6404)
        s = 1.0 / np.sqrt(HIDDEN)
        return {'hidden_states': jax.random.normal(ks[0], (B, Q, HIDDEN), jnp.float32), 'cross_attention_states': jax.random.normal(ks[1], (B, KV, HIDDEN), jnp.float32), 'attention_mask': jnp.zeros((B, 1, Q, KV), jnp.float32), 'q_proj_w': jax.random.normal(ks[2], (NUM_HEADS * HEAD_DIM, HIDDEN), jnp.float32) * s, 'k_proj_w': jax.random.normal(ks[3], (NUM_KV_HEADS * HEAD_DIM, HIDDEN), jnp.float32) * s, 'v_proj_w': jax.random.normal(ks[4], (NUM_KV_HEADS * HEAD_DIM, HIDDEN), jnp.float32) * s, 'o_proj_w': jax.random.normal(ks[5], (HIDDEN, NUM_HEADS * HEAD_DIM), jnp.float32) * s, 'q_norm_w': jnp.ones((HEAD_DIM,), jnp.float32), 'k_norm_w': jnp.ones((HEAD_DIM,), jnp.float32)}
    _L2_xattn_all = _L2_xattn_setup()
    _L2_xattn_in = {k: v for k, v in _L2_xattn_all.items() if k in ('q_proj_w', 'k_proj_w', 'v_proj_w', 'o_proj_w', 'q_norm_w', 'k_norm_w')}
    del _L2_xattn_all

    def _L2_ffn_setup():
        import jax, jax.numpy as jnp
        import numpy as np
        K_TOP = 8
        key = jax.random.key(seed)
        k1, k2, k3 = jax.random.split(key, 3)
        B, S, H, E = (4, 512, 512, 64)
        hidden_states = jax.random.normal(k1, (B, S, H), dtype=jnp.float32)
        router_weight = jax.random.normal(k2, (E, H), dtype=jnp.float32)
        router_bias = jnp.zeros((E,), dtype=jnp.float32)
        expert_bias = jax.random.normal(k3, (E, H), dtype=jnp.float32) * 0.1
        return {'hidden_states': hidden_states, 'router_weight': router_weight, 'router_bias': router_bias, 'expert_bias': expert_bias}
    _L2_ffn_all = _L2_ffn_setup()
    _L2_ffn_in = {k: v for k, v in _L2_ffn_all.items() if k in ('router_weight', 'router_bias', 'expert_bias')}
    del _L2_ffn_all

    def _L3_xattn_setup():
        import jax, jax.numpy as jnp
        import numpy as np
        import math
        EPS = 1e-05
        LAMBDA = 0.6

        def _crucial_k(C):
            f = math.floor(LAMBDA * C)
            return f + f % 2

        def _conv1d(y, w):
            return jax.lax.conv_general_dilated(y, w, window_strides=(1,), padding=((3, 3),), dimension_numbers=('NCH', 'OIH', 'NCH'))

        def _norm_active(z, gamma, beta):
            mu = jnp.mean(z, axis=(0, 2), keepdims=True)
            var = jnp.mean((z - mu) ** 2, axis=(0, 2), keepdims=True)
            zn = (z - mu) * jax.lax.rsqrt(var + EPS)
            zn = zn * gamma.reshape(1, -1, 1) + beta.reshape(1, -1, 1)
            return jax.nn.sigmoid(jax.nn.relu(zn))
        key = jax.random.key(seed)
        k1, k2, k3 = jax.random.split(key, 3)
        B, C, L = (32, 32, 512)
        x = jax.random.normal(k1, (B, C, L), dtype=jnp.float32)
        channel_map = jax.random.normal(k2, (B, C, L), dtype=jnp.float32)
        fan_in = 2 * 7
        bound = 1.0 / math.sqrt(fan_in)
        conv_w = jax.random.uniform(k3, (1, 2, 7), jnp.float32, -bound, bound)
        bn_gamma = jnp.ones((1,), jnp.float32)
        bn_beta = jnp.zeros((1,), jnp.float32)
        return {'x': x, 'channel_map': channel_map, 'conv_w': conv_w, 'bn_gamma': bn_gamma, 'bn_beta': bn_beta}
    _L3_xattn_all = _L3_xattn_setup()
    _L3_xattn_in = {k: v for k, v in _L3_xattn_all.items() if k in ('conv_w', 'bn_gamma', 'bn_beta')}
    del _L3_xattn_all

    def _L3_ffn_setup():
        import jax, jax.numpy as jnp
        import numpy as np
        E = 8
        R = 16
        TOP_K = 2
        SCALING = 32.0 / 16.0
        D_IN = 512
        D_OUT = 512
        key = jax.random.key(seed)
        ks = jax.random.split(key, 6)
        x = jax.random.normal(ks[0], (4, 256, D_IN), jnp.float32)
        Wb = jax.random.normal(ks[1], (D_OUT, D_IN), jnp.float32) * 0.02
        bias = jax.random.normal(ks[2], (D_OUT,), jnp.float32) * 0.02
        Wr = jax.random.normal(ks[3], (E, D_IN), jnp.float32) * 0.01
        A = jax.random.normal(ks[4], (E, R, D_IN), jnp.float32) * (1.0 / np.sqrt(D_IN))
        Bm = jax.random.normal(ks[5], (E, D_OUT, R), jnp.float32) * 0.01
        return {'x': x, 'Wb': Wb, 'bias': bias, 'Wr': Wr, 'A': A, 'Bm': Bm}
    _L3_ffn_all = _L3_ffn_setup()
    _L3_ffn_in = {k: v for k, v in _L3_ffn_all.items() if k in ('Wb', 'bias', 'Wr', 'A', 'Bm')}
    del _L3_ffn_all
    return {'x': x, 'ctx_4096': ctx_4096, 'mask_1x1xSxS2_ff0': mask_1x1xSxS2_ff0, 'L0_xattn_x1_scale': _L0_xattn_in['x1_scale'], 'L0_xattn_x1_zp': _L0_xattn_in['x1_zp'], 'L0_xattn_x2_scale': _L0_xattn_in['x2_scale'], 'L0_xattn_x2_zp': _L0_xattn_in['x2_zp'], 'L0_ffn_qweight': _L0_ffn_in['qweight'], 'L0_ffn_lut4': _L0_ffn_in['lut4'], 'L0_ffn_lut8': _L0_ffn_in['lut8'], 'L0_ffn_bias': _L0_ffn_in['bias'], 'L1_xattn_Wq_d': _L1_xattn_in['Wq_d'], 'L1_xattn_W_qk': _L1_xattn_in['W_qk'], 'L1_xattn_Wkv_d': _L1_xattn_in['Wkv_d'], 'L1_xattn_Wv_u': _L1_xattn_in['Wv_u'], 'L1_ffn_w_gate': _L1_ffn_in['w_gate'], 'L1_ffn_w_up': _L1_ffn_in['w_up'], 'L1_ffn_w_down': _L1_ffn_in['w_down'], 'L1_ffn_s_gate': _L1_ffn_in['s_gate'], 'L1_ffn_s_up': _L1_ffn_in['s_up'], 'L1_ffn_s_down': _L1_ffn_in['s_down'], 'L2_xattn_q_proj_w': _L2_xattn_in['q_proj_w'], 'L2_xattn_k_proj_w': _L2_xattn_in['k_proj_w'], 'L2_xattn_v_proj_w': _L2_xattn_in['v_proj_w'], 'L2_xattn_o_proj_w': _L2_xattn_in['o_proj_w'], 'L2_xattn_q_norm_w': _L2_xattn_in['q_norm_w'], 'L2_xattn_k_norm_w': _L2_xattn_in['k_norm_w'], 'L2_ffn_router_weight': _L2_ffn_in['router_weight'], 'L2_ffn_router_bias': _L2_ffn_in['router_bias'], 'L2_ffn_expert_bias': _L2_ffn_in['expert_bias'], 'L3_xattn_conv_w': _L3_xattn_in['conv_w'], 'L3_xattn_bn_gamma': _L3_xattn_in['bn_gamma'], 'L3_xattn_bn_beta': _L3_xattn_in['bn_beta'], 'L3_ffn_Wb': _L3_ffn_in['Wb'], 'L3_ffn_bias': _L3_ffn_in['bias'], 'L3_ffn_Wr': _L3_ffn_in['Wr'], 'L3_ffn_A': _L3_ffn_in['A'], 'L3_ffn_Bm': _L3_ffn_in['Bm']}

def reference(x, ctx_4096, mask_1x1xSxS2_ff0, L0_xattn_x1_scale, L0_xattn_x1_zp, L0_xattn_x2_scale, L0_xattn_x2_zp, L0_ffn_qweight, L0_ffn_lut4, L0_ffn_lut8, L0_ffn_bias, L1_xattn_Wq_d, L1_xattn_W_qk, L1_xattn_Wkv_d, L1_xattn_Wv_u, L1_ffn_w_gate, L1_ffn_w_up, L1_ffn_w_down, L1_ffn_s_gate, L1_ffn_s_up, L1_ffn_s_down, L2_xattn_q_proj_w, L2_xattn_k_proj_w, L2_xattn_v_proj_w, L2_xattn_o_proj_w, L2_xattn_q_norm_w, L2_xattn_k_norm_w, L2_ffn_router_weight, L2_ffn_router_bias, L2_ffn_expert_bias, L3_xattn_conv_w, L3_xattn_bn_gamma, L3_xattn_bn_beta, L3_ffn_Wb, L3_ffn_bias, L3_ffn_Wr, L3_ffn_A, L3_ffn_Bm):
    import jax
    import jax.numpy as jnp

    def _L0_xattn_ref(x1, x2, x1_scale, x1_zp, x2_scale, x2_zp):
        import jax, jax.numpy as jnp
        import numpy as np
        QMIN = 0.0
        QMAX = 255.0

        def fake_quant(x, scale, zp):
            s = scale.reshape(())
            z = zp.reshape(())
            q = jnp.clip(jnp.round(x / s + z), QMIN, QMAX)
            return (q - z) * s
        q1 = fake_quant(x1, x1_scale, x1_zp)
        q2 = fake_quant(x2, x2_scale, x2_zp)
        return jnp.matmul(q1, q2)

    def _L0_ffn_ref(x, qweight, lut4, lut8, bias):
        import jax, jax.numpy as jnp
        import numpy as np
        B_L, B_H = (4, 8)
        LIN_SLOPE, LIN_INTER, EST_T = (1.0, 0.0, 64.0)
        BATCH, SEQ, IN_F, OUT_F = (4, 256, 512, 512)
        MAX_BITS = 8

        def dequant_kbit(qweight, lut, bit):
            O, I32 = (qweight.shape[1], qweight.shape[2])
            shifts = jnp.arange(32, dtype=jnp.int32)
            idx = jnp.zeros((O, I32 * 32), dtype=jnp.int32)
            for p in range(bit):
                bits = (qweight[p][:, :, None] >> shifts & 1).reshape(O, I32 * 32)
                idx = idx | bits << p
            return jnp.take_along_axis(lut, idx, axis=1)
        e = jnp.linalg.norm(x, axis=-1) * LIN_SLOPE + LIN_INTER
        mask = e > EST_T
        w_l = dequant_kbit(qweight, lut4, B_L)
        w_h = dequant_kbit(qweight, lut8, B_H)
        y_l = jnp.einsum('bsi,oi->bso', x, w_l)
        y_h = jnp.einsum('bsi,oi->bso', x, w_h)
        y = jnp.where(mask[..., None], y_h, y_l) + bias
        return y

    def _L1_xattn_ref(Q, K, Wq_d, W_qk, Wkv_d, Wv_u):
        import jax, jax.numpy as jnp
        import numpy as np
        B, N, NKV = (2, 256, 256)
        E = 512
        H = 16
        HD = E // H
        LQ = E // 8
        LKV = E // 16
        b, n, _ = Q.shape
        nkv = K.shape[1]
        C_q = Q @ Wq_d
        C_kv = K @ Wkv_d
        CqWqk = (C_q @ W_qk).reshape(b, n, H, LKV)
        scores = jnp.einsum('bnhl,bkl->bhnk', CqWqk, C_kv) / jnp.sqrt(jnp.asarray(LKV, dtype=Q.dtype))
        attn = jax.nn.softmax(scores, axis=-1)
        V_up = (C_kv @ Wv_u).reshape(b, nkv, H, HD)
        out = jnp.einsum('bhnk,bkhd->bnhd', attn, V_up)
        return out.reshape(b, n, H * HD)

    def _L1_ffn_ref(x, w_gate, w_up, w_down, s_gate, s_up, s_down):
        import jax, jax.numpy as jnp
        import numpy as np
        import math
        SQRT7 = math.sqrt(7.0)
        EPS = 1e-05

        def int4_quant(x):
            beta = jnp.mean(jnp.abs(x), axis=-1, keepdims=True)
            x_q = jnp.clip(jnp.round(x * SQRT7 / (beta + EPS)), -8, 7)
            return x_q * (beta * SQRT7) / SQRT7

        def int8_quant(x):
            gamma = jnp.max(jnp.abs(x), axis=-1, keepdims=True)
            x_q = jnp.clip(jnp.round(x * 127.0 / (gamma + EPS)), -128, 127)
            return x_q * gamma / 127.0

        def bitlinear(x, w, scale):
            w_mean = jnp.mean(jnp.abs(w))
            w_q = jnp.clip(jnp.round(w / (w_mean + EPS)), -1.0, 1.0)
            w_eff = w_q * w_mean * scale
            return jnp.einsum('...i,oi->...o', x, w_eff)
        xq = int4_quant(x)
        gate = bitlinear(xq, w_gate, s_gate)
        up = bitlinear(xq, w_up, s_up)
        gate = jnp.square(jax.nn.relu(gate))
        inter = int8_quant(up * gate)
        return bitlinear(inter, w_down, s_down)

    def _L2_xattn_ref(hidden_states, cross_attention_states, attention_mask, q_proj_w, k_proj_w, v_proj_w, o_proj_w, q_norm_w, k_norm_w):
        import jax, jax.numpy as jnp
        import numpy as np
        NUM_HEADS = 32
        NUM_KV_HEADS = 8
        HEAD_DIM = 128
        HIDDEN = 512
        EPS = 1e-05

        def rmsnorm(x, w, eps=EPS):
            xf = x.astype(jnp.float32)
            var = jnp.mean(xf * xf, axis=-1, keepdims=True)
            return w * (xf * jax.lax.rsqrt(var + eps)).astype(x.dtype)
        B, Q, _ = hidden_states.shape
        KV = cross_attention_states.shape[1]
        n_rep = NUM_HEADS // NUM_KV_HEADS
        q = (hidden_states @ q_proj_w.T).reshape(B, Q, NUM_HEADS, HEAD_DIM).transpose(0, 2, 1, 3)
        k = (cross_attention_states @ k_proj_w.T).reshape(B, KV, NUM_KV_HEADS, HEAD_DIM).transpose(0, 2, 1, 3)
        v = (cross_attention_states @ v_proj_w.T).reshape(B, KV, NUM_KV_HEADS, HEAD_DIM).transpose(0, 2, 1, 3)
        q = rmsnorm(q, q_norm_w)
        k = jnp.repeat(k, n_rep, axis=1)
        v = jnp.repeat(v, n_rep, axis=1)
        k = rmsnorm(k, k_norm_w)
        scale = 1.0 / np.sqrt(HEAD_DIM)
        scores = jnp.einsum('bhqd,bhkd->bhqk', q, k) * scale + attention_mask
        attn = jax.nn.softmax(scores.astype(jnp.float32), axis=-1).astype(q.dtype)
        out = jnp.einsum('bhqk,bhkd->bhqd', attn, v)
        out = out.transpose(0, 2, 1, 3).reshape(B, Q, NUM_HEADS * HEAD_DIM)
        return out @ o_proj_w.T

    def _L2_ffn_ref(hidden_states, router_weight, router_bias, expert_bias):
        import jax, jax.numpy as jnp
        import numpy as np
        K_TOP = 8
        B, S, H = hidden_states.shape
        E = router_weight.shape[0]
        T = B * S
        flat = hidden_states.reshape(T, H)
        logits = jnp.einsum('th,eh->te', flat, router_weight) + router_bias
        scores = jax.nn.softmax(logits, axis=-1)
        topk_w, topk_idx = jax.lax.top_k(scores, K_TOP)
        w_sum = topk_w.sum(axis=-1, keepdims=True)
        w_dense = jnp.zeros((T, E), dtype=scores.dtype).at[jnp.arange(T)[:, None], topk_idx].add(topk_w)
        bias_mix = jnp.einsum('te,eh->th', w_dense, expert_bias)
        out = flat * w_sum + bias_mix
        return out.reshape(B, S, H)

    def _L3_xattn_ref(x, channel_map, conv_w, bn_gamma, bn_beta):
        import jax, jax.numpy as jnp
        import numpy as np
        import math
        EPS = 1e-05
        LAMBDA = 0.6

        def _crucial_k(C):
            f = math.floor(LAMBDA * C)
            return f + f % 2

        def _conv1d(y, w):
            return jax.lax.conv_general_dilated(y, w, window_strides=(1,), padding=((3, 3),), dimension_numbers=('NCH', 'OIH', 'NCH'))

        def _norm_active(z, gamma, beta):
            mu = jnp.mean(z, axis=(0, 2), keepdims=True)
            var = jnp.mean((z - mu) ** 2, axis=(0, 2), keepdims=True)
            zn = (z - mu) * jax.lax.rsqrt(var + EPS)
            zn = zn * gamma.reshape(1, -1, 1) + beta.reshape(1, -1, 1)
            return jax.nn.sigmoid(jax.nn.relu(zn))
        B, C, L = x.shape
        k = _crucial_k(C)
        cm = jnp.moveaxis(channel_map, 1, 2)
        _, topk_idx = jax.lax.top_k(cm, k)
        b_idx = jnp.arange(B)[:, None, None]
        l_idx = jnp.arange(L)[None, :, None]
        mask = jnp.zeros((B, L, C), x.dtype).at[b_idx, l_idx, topk_idx].set(1.0)
        crucial_channels = jnp.moveaxis(mask, 2, 1)
        subcrucial_channels = 1.0 - crucial_channels
        crucial_features = crucial_channels * x
        subcrucial_features = subcrucial_channels * x
        c_max = jnp.max(crucial_features, axis=1, keepdims=True)
        c_avg = jnp.mean(crucial_features, axis=1, keepdims=True) * (C / k)
        s_max = jnp.max(subcrucial_features, axis=1, keepdims=True)
        s_avg = jnp.mean(subcrucial_features, axis=1, keepdims=True) * (C / (C - k))
        crucial_x = jnp.concatenate([c_max, c_avg], axis=1)
        subcrucial_x = jnp.concatenate([s_max, s_avg], axis=1)
        A_S1 = _norm_active(_conv1d(crucial_x, conv_w), bn_gamma, bn_beta)
        A_S2 = _norm_active(_conv1d(subcrucial_x, conv_w), bn_gamma, bn_beta)
        return crucial_features * A_S1 + subcrucial_features * A_S2

    def _L3_ffn_ref(x, Wb, bias, Wr, A, Bm):
        import jax, jax.numpy as jnp
        import numpy as np
        E = 8
        R = 16
        TOP_K = 2
        SCALING = 32.0 / 16.0
        D_IN = 512
        D_OUT = 512
        xf = x.reshape(-1, x.shape[-1])
        T = xf.shape[0]
        logits = xf @ Wr.T
        probs = jax.nn.softmax(logits, axis=-1)
        topk_p, topk_i = jax.lax.top_k(probs, TOP_K)
        topk_p = topk_p / jnp.sum(topk_p, axis=-1, keepdims=True)
        w = jnp.zeros((T, E), xf.dtype).at[jnp.arange(T)[:, None], topk_i].add(topk_p)
        h = jnp.einsum('ti,eri->ter', xf, A)
        lora = jnp.einsum('ter,te,eor->to', h, w, Bm) * SCALING
        base = xf @ Wb.T + bias
        out = (base + lora).reshape(*x.shape[:-1], D_OUT)
        return out
    x = x + _L0_xattn_ref(_layernorm(x, axis=-1), ctx_4096, L0_xattn_x1_scale, L0_xattn_x1_zp, L0_xattn_x2_scale, L0_xattn_x2_zp)
    x = x + _L0_ffn_ref(_layernorm(x, axis=-1), L0_ffn_qweight, L0_ffn_lut4, L0_ffn_lut8, L0_ffn_bias)
    x = x + _L1_xattn_ref(_layernorm(x, axis=-1), ctx_4096, L1_xattn_Wq_d, L1_xattn_W_qk, L1_xattn_Wkv_d, L1_xattn_Wv_u)
    x = x + _L1_ffn_ref(_layernorm(x, axis=-1), L1_ffn_w_gate, L1_ffn_w_up, L1_ffn_w_down, L1_ffn_s_gate, L1_ffn_s_up, L1_ffn_s_down)
    x = x + _L2_xattn_ref(_layernorm(x, axis=-1), ctx_4096, mask_1x1xSxS2_ff0, L2_xattn_q_proj_w, L2_xattn_k_proj_w, L2_xattn_v_proj_w, L2_xattn_o_proj_w, L2_xattn_q_norm_w, L2_xattn_k_norm_w)
    x = x + _L2_ffn_ref(_layernorm(x, axis=-1), L2_ffn_router_weight, L2_ffn_router_bias, L2_ffn_expert_bias)
    x = x + _L3_xattn_ref(_layernorm(x, axis=-1), ctx_4096, L3_xattn_conv_w, L3_xattn_bn_gamma, L3_xattn_bn_beta)
    x = x + _L3_ffn_ref(_layernorm(x, axis=-1), L3_ffn_Wb, L3_ffn_bias, L3_ffn_Wr, L3_ffn_A, L3_ffn_Bm)
    return x

_drawn_inputs = setup_inputs


def setup_inputs(seed=0):
    import zlib

    import numpy as np

    out = dict(_drawn_inputs(seed))
    spreads = {'L2_xattn_q_norm_w': (1.0, 0.6),
     'L2_xattn_k_norm_w': (1.0, 0.6),
     'L2_ffn_router_bias': (0.0, 2.0)}
    factors = {'L0_ffn_bias': 64.0,
     'L1_xattn_Wq_d': 4.187,
     'L1_xattn_W_qk': 4.174,
     'L2_ffn_router_weight': 8.0,
     'L2_ffn_expert_bias': 8.0,
     'L3_xattn_conv_w': 60.044,
     'L3_ffn_Wb': 2.698,
     'L3_ffn_bias': 62.271,
     'L3_ffn_Wr': 8.0,
     'L3_ffn_A': 8.0,
     'L3_ffn_Bm': 8.0}
    for name, (base, spread) in spreads.items():
        noise = np.random.default_rng([zlib.crc32(name.encode()), seed]).standard_normal(out[name].shape)
        drawn = base * np.exp(spread * noise) if base else spread * noise
        out[name] = jnp.asarray(drawn.astype(out[name].dtype))
    for name, factor in factors.items():
        out[name] = (out[name] * factor).astype(out[name].dtype)
    return out
```

```python
from contextlib import ExitStack

import numpy as np

import concourse.bass as bass
from concourse import mybir

F32, BF16, I32, F32R = mybir.dt.float32, mybir.dt.bfloat16, mybir.dt.int32, mybir.dt.float32r
ALU = mybir.AluOpType
ACT = mybir.ActivationFunctionType
AX = mybir.AxisListType

P = 128
B, SEQ, D = 2, 256, 512
CTX = 512
TILES = B * SEQ // P
TPB = SEQ // P
KT = D // P
CTILES = B * CTX // P
CPB = CTX // P
EPS = 1e-5
ROUND = 1.5 * 2.0 ** 23
BANKS = 8


class Own:

    def __init__(self, engine, semaphore):
        self.engine, self.semaphore, self.count = engine, semaphore, 0

    def __call__(self, instruction):
        instruction.then_inc(self.semaphore, 1)
        self.count += 1

    def wait(self):
        self.engine.wait_ge(self.semaphore, self.count)


class Core:

    def __init__(self, nc, stack):
        self.nc, self.stack, self.norms, self.turned, self.label = nc, stack, 0, 0, ""
        sb = self.sbuf
        self.x = sb("x", [P, TILES, D], F32)
        self.xn = sb("xn", [P, TILES, D], F32)
        self.xnT = sb("xnT", [P, KT, TILES * P], F32)
        self.ctxT = sb("ctxT", [P, KT, B * CTX], F32)
        self.ident = sb("ident", [P, P], F32)
        self.ident16 = sb("ident16", [P, P], BF16)
        self.ones = sb("ones", [P, P], F32)
        self.ones16 = sb("ones16", [P, 1], BF16)
        self.minus_half = sb("minus_half", [P, 16], F32)
        self.stats = sb("stats", [P, TILES, 6], F32)
        self.meanvar = sb("meanvar", [P, TILES, 2], F32)
        self.varep = sb("varep", [P, TILES], F32)
        self.rstd = sb("rstd", [P, TILES], F32)
        bisection_buffers(self)
        self.bank = [stack.enter_context(nc.psum_tensor(f"bank{i}", [P, 512], F32)) for i in range(BANKS)]
        self.vown = Own(nc.vector, self.sem("vector_own"))
        self.pown = Own(nc.gpsimd, self.sem("gpsimd_own"))
        self.aown = Own(nc.scalar, self.sem("scalar_own"))
        self.variance_ready = self.sem("variance_ready")
        self.rstd_ready = self.sem("rstd_ready")
        self.xn_ready = self.sem("xn_ready")
        self.xnT_in_psum = self.sem("xnT_in_psum")
        self.xnT_ready = self.sem("xnT_ready")
        self.x_loaded = self.sem("x_loaded")
        self.ctxT_loaded = self.sem("ctxT_loaded")

    def sbuf(self, name, shape, dtype, stack=None):
        return (stack or self.stack).enter_context(self.nc.sbuf_tensor(self.label + name, shape, dtype))

    def sem(self, name):
        return self.stack.enter_context(self.nc.semaphore(name))



def norm_vector(k, n):
    v = k.nc.vector
    for t in range(TILES):
        k.vown(v.bn_stats(k.stats[:, t, :], k.x[:, t, :]))
    k.vown.wait()
    for t in range(TILES):
        k.vown(v.bn_aggr(k.meanvar[:, t, :], k.stats[:, t, :]))
    k.vown.wait()
    v.tensor_scalar(k.varep[:, :], k.meanvar[:, :, 1], EPS, None, ALU.add).then_inc(k.variance_ready, 1)
    v.wait_ge(k.rstd_ready, n + 1)
    for t in range(TILES):
        v.tensor_scalar(k.xn[:, t, :], k.x[:, t, :], k.meanvar[:, t, 0:1], k.rstd[:, t:t + 1],
                        ALU.subtract, ALU.mult).then_inc(k.xn_ready, 1)


def norm_gpsimd(k, n):
    g = k.nc.gpsimd
    g.wait_ge(k.variance_ready, n + 1)
    g.tensor_tensor(k.rstd[:, :], k.varep[:, :], k.minus_half[:, 0:TILES], ALU.pow).then_inc(k.rstd_ready, 1)


def norm_tensor(k, n, m, banks):
    pe = k.nc.tensor
    for t in range(TILES):
        pe.wait_ge(k.xn_ready, TILES * n + t + 1)
        if t >= 2:
            pe.wait_ge(k.xnT_ready, TILES * m + t - 1)
        for f in range(KT):
            last = pe.transpose(banks[t % 2][:, f * P:(f + 1) * P], k.xn[:, t, f * P:(f + 1) * P], k.ident[:, :])
        last.then_inc(k.xnT_in_psum, 1)


def norm_scalar(k, m, banks):
    a = k.nc.scalar
    for t in range(TILES):
        a.wait_ge(k.xnT_in_psum, TILES * m + t + 1)
        a.copy(k.xnT[:, :, t * P:(t + 1) * P],
               banks[t % 2][:, :].rearrange("p (f c) -> p f c", f=KT)).then_inc(k.xnT_ready, 1)



def prologue(k, dram):
    nc = k.nc
    identity_zeroed = k.sem("identity_zeroed")
    with nc.Block(no_gpsimd_drain=True) as block:

        @block.sync
        def _(sp):
            sp.dma_start(k.x[:, :, :], dram["x"].rearrange("b (t p) d -> p (b t) d", p=P)).then_inc(k.x_loaded, 16)
            sp.dma_start(k.ctxT[:, :, :], dram["ctxT"].rearrange("(f p) r -> p f r", p=P)).then_inc(k.ctxT_loaded, 16)
            sp.wait_ge(k.x_loaded, 16)

        @block.gpsimd
        def _(g):
            g.memset(k.ident[:, :], 0.0).then_inc(identity_zeroed, 1)
            g.memset(k.ident16[:, :], 0.0).then_inc(identity_zeroed, 1)
            k.pown(g.memset(k.ones[:, :], 1.0))
            k.pown(g.memset(k.ones16[:, :], 1.0))
            k.pown(g.memset(k.minus_half[:, :], -0.5))
            g.wait_ge(identity_zeroed, 2)
            for m in (k.ident, k.ident16):
                k.pown(g.affine_select(out=m[:, :], in_=m[:, :], compare_op=ALU.not_equal, fill=1.0,
                                       base=0, pattern=[[-1, P]], channel_multiplier=1))
            k.pown.wait()



def layer0_attention(k, dram):
    nc, n = k.nc, k.norms
    k.norms += 1
    MIDDLE = 128.0
    with ExitStack() as s:
        ctx = k.sbuf("ctx", [P, CTILES, D], F32, s)
        q2 = k.sbuf("q2", [P, CTILES, D], BF16, s)
        q1 = k.sbuf("q1", [P, TILES, D], BF16, s)
        q1T = k.sbuf("q1T", [P, KT, TILES * P], BF16, s)
        t1 = k.sbuf("t1", [P, 2, D], F32, s)
        t2 = k.sbuf("t2", [P, 2, D], F32, s)
        par = k.sbuf("par", [P, 4], F32, s)
        inv = k.sbuf("inv", [P, 2], F32, s)
        off = k.sbuf("off", [P, 2], F32, s)
        s12 = k.sbuf("s12", [P, 1], F32, s)
        kd1 = k.sbuf("kd1", [P, 1], F32, s)
        d2s = k.sbuf("d2s", [P, 1], F32, s)
        rows = k.sbuf("rows", [P, TILES], F32, s)
        corr = k.sbuf("corr", [P, TILES], F32, s)
        cols = k.sbuf("cols", [1, B, D], F32, s)
        par_loaded, ctx_loaded = k.sem("par_loaded"), k.sem("ctx_loaded")
        q2_ready, q1_ready, q1T_psum, q1T_ready = (k.sem(f"l0a_{x}") for x in
                                                   ("q2_ready", "q1_ready", "q1T_psum", "q1T_ready"))
        cols_psum, cols_ready, product_psum = (k.sem(f"l0a_{x}") for x in
                                               ("cols_psum", "cols_ready", "product_psum"))
        with nc.Block(no_gpsimd_drain=True) as block:

            @block.sync
            def _(sp):
                for i, name in enumerate(("L0_xattn_x1_scale", "L0_xattn_x1_zp", "L0_xattn_x2_scale", "L0_xattn_x2_zp")):
                    sp.dma_start(par[:, i:i + 1], dram[name].unsqueeze(0).broadcast_to([P, 1])).then_inc(par_loaded, 16)
                for b in range(B):
                    sp.dma_start(ctx[:, b * CPB:(b + 1) * CPB, :],
                                 dram["ctx"][b].rearrange("(t p) d -> p t d", p=P)).then_inc(ctx_loaded, 16)

            @block.gpsimd
            def _(g):
                norm_gpsimd(k, n)

            @block.vector
            def _(v):
                norm_vector(k, n)
                v.wait_ge(par_loaded, 64)
                for i in range(2):
                    k.vown(v.reciprocal(inv[:, i:i + 1], par[:, 2 * i:2 * i + 1]))
                    k.vown(v.tensor_scalar(off[:, i:i + 1], par[:, 2 * i + 1:2 * i + 2], -1.0, MIDDLE, ALU.mult, ALU.add))
                k.vown(v.tensor_tensor(s12[:, :], par[:, 0:1], par[:, 2:3], ALU.mult))
                k.vown.wait()
                k.vown(v.tensor_scalar(kd1[:, :], off[:, 0:1], float(CTX), None, ALU.mult))
                k.vown(v.tensor_tensor(d2s[:, :], off[:, 1:2], s12[:, :], ALU.mult))

                def quantise(source, target, i, ready):
                    for j in range(2):
                        k.vown(v.tensor_scalar(t1[:, j, :], source(j), inv[:, i:i + 1], par[:, 2 * i + 1:2 * i + 2],
                                               ALU.mult, ALU.add))
                    k.vown.wait()
                    for j in range(2):
                        k.vown(v.tensor_scalar(t2[:, j, :], t1[:, j, :], 0.0, 255.0, ALU.max, ALU.min))
                    k.vown.wait()
                    for j in range(2):
                        v.tensor_scalar(target(j), t2[:, j, :], ROUND, ROUND + MIDDLE, ALU.add,
                                        ALU.subtract).then_inc(ready, 1)

                v.wait_ge(k.xn_ready, TILES * n + TILES)
                for t in range(0, TILES, 2):
                    quantise(lambda j: k.xn[:, t + j, :], lambda j: q1[:, t + j, :], 0, q1_ready)
                v.wait_ge(q1_ready, TILES)
                for t in range(TILES):
                    k.vown(v.tensor_reduce(rows[:, t:t + 1], q1[:, t, :], AX.X, ALU.add))
                v.wait_ge(ctx_loaded, 16 * B)
                for t in range(0, CTILES, 2):
                    quantise(lambda j: ctx[:, t + j, :], lambda j: q2[:, t + j, :], 1, q2_ready)
                k.vown.wait()
                k.vown(v.tensor_scalar(corr[:, :], rows[:, :], kd1[:, 0:1], d2s[:, 0:1], ALU.add, ALU.mult))
                k.vown.wait()
                for t in range(TILES):
                    k.vown(v.tensor_scalar(k.x[:, t, :], k.x[:, t, :], corr[:, t:t + 1], None, ALU.add))
                for b in range(B):
                    v.wait_ge(cols_psum, b + 1)
                    v.tensor_scalar(cols[:, b, :], k.bank[2 + b][0:1, :], off[0:1, 0:1], None,
                                    ALU.mult).then_inc(cols_ready, 1)
                k.vown.wait()
                for t in range(TILES):
                    v.wait_ge(product_psum, t + 1)
                    k.vown(v.scalar_tensor_tensor(k.x[:, t, :], k.bank[4 + t][:, :], s12[:, 0:1], k.x[:, t, :],
                                                  ALU.mult, ALU.add))
                k.vown.wait()

            @block.tensor
            def _(pe):
                for t in range(TILES):
                    pe.wait_ge(q1_ready, t + 1)
                    if t >= 2:
                        pe.wait_ge(q1T_ready, t - 1)
                    for f in range(KT):
                        last = pe.transpose(k.bank[t % 2][:, 0:256].bitcast(BF16)[:, f * P:(f + 1) * P],
                                            q1[:, t, f * P:(f + 1) * P], k.ident16[:, :])
                    last.then_inc(q1T_psum, 1)
                for b in range(B):
                    pe.wait_ge(q2_ready, CPB * (b + 1))
                    for f in range(CPB):
                        last = pe.matmul(k.bank[2 + b][0:1, :], k.ones16[:, :], q2[:, b * CPB + f, :],
                                         start=f == 0, stop=f == CPB - 1)
                    last.then_inc(cols_psum, 1)
                pe.wait_ge(q1T_ready, TILES)
                for t in range(TILES):
                    b = t // TPB
                    for f in range(CPB):
                        pe.matmul(k.bank[4 + t][:, :], q1T[:, f, t * P:(t + 1) * P], q2[:, b * CPB + f, :],
                                  start=f == 0, stop=False)
                    pe.wait_ge(cols_ready, b + 1)
                    pe.matmul(k.bank[4 + t][:, :], k.ones[0:1, :], cols[:, b, :],
                              start=False, stop=True).then_inc(product_psum, 1)

            @block.scalar
            def _(a):
                for t in range(TILES):
                    a.wait_ge(q1T_psum, t + 1)
                    a.copy(q1T[:, :, t * P:(t + 1) * P],
                           k.bank[t % 2][:, 0:256].bitcast(BF16).rearrange("p (f c) -> p f c", f=KT))\
                     .then_inc(q1T_ready, 1)



def layer0_ffn(k, dram):
    nc, n, m = k.nc, k.norms, k.turned
    k.norms += 1
    k.turned += 1
    PLANES, BITS = 4, 32
    WORDS = D // BITS
    CODES = 2 ** PLANES
    OT = D // P
    with ExitStack() as s:
        planes = k.sbuf("planes", [P, OT, PLANES * WORDS], I32, s)
        shifts = k.sbuf("shifts", [P, BITS], I32, s)
        moved = k.sbuf("moved", [P, PLANES * WORDS, BITS], I32, s)
        bits = k.sbuf("bits", [P, 2, PLANES, D], I32, s)
        lut = k.sbuf("lut", [P, OT, CODES], F32, s)
        diff = k.sbuf("diff", [P, OT, CODES // 2], F32, s)
        tree = k.sbuf("tree", [P, 2, CODES // 2, D], F32, s)
        weightT = k.sbuf("weightT", [P, KT, D], F32, s)
        bias = k.sbuf("bias", [P, D], F32, s)
        loaded, bias_loaded, shifts_ready, diff_ready, bits_ready, leaves_ready, weight_ready, weightT_psum, \
            weightT_ready, product_psum = (k.sem(f"l0f_{x}") for x in (
                "loaded", "bias_loaded", "shifts_ready", "diff_ready", "bits_ready", "leaves_ready", "weight_ready",
                "weightT_psum", "weightT_ready", "product_psum"))
        with nc.Block(no_gpsimd_drain=True) as block:

            @block.sync
            def _(sp):
                for p in range(PLANES):
                    sp.dma_start(planes[:, :, p * WORDS:(p + 1) * WORDS],
                                 dram["L0_ffn_qweight"][p].rearrange("(t p) w -> p t w", p=P)).then_inc(loaded, 16)
                sp.dma_start(lut[:, :, :], dram["L0_ffn_lut4"].rearrange("(t p) c -> p t c", p=P)).then_inc(loaded, 16)
                sp.dma_start(bias[:, :], dram["L0_ffn_bias"].unsqueeze(0).broadcast_to([P, D])).then_inc(bias_loaded, 16)

            @block.gpsimd
            def _(g):
                g.iota(shifts[:, :], [[1, BITS]], base=0, channel_multiplier=0).then_inc(shifts_ready, 1)
                norm_gpsimd(k, n)

            @block.vector
            def _(v):
                norm_vector(k, n)
                v.wait_ge(loaded, 16 * (PLANES + 1))
                v.wait_ge(shifts_ready, 1)
                v.tensor_tensor(diff[:, :, :], lut[:, :, 1::2], lut[:, :, 0::2], ALU.subtract).then_inc(diff_ready, 1)
                v.wait_ge(bias_loaded, 16)
                v.wait_ge(k.xn_ready, TILES * (n + 1))
                for t in range(TILES):
                    k.vown(v.tensor_tensor(k.x[:, t, :], k.x[:, t, :], bias[:, :], ALU.add))

                def unpack(o):
                    if o >= 1:
                        v.wait_ge(bits_ready, o)
                    if o >= 2:
                        v.wait_ge(weight_ready, o - 1)
                        v.wait_ge(leaves_ready, o - 1)
                    k.vown(v.tensor_tensor(moved[:, :, :], planes[:, o, :].unsqueeze(2).broadcast_to([P, PLANES * WORDS, BITS]),
                                           shifts[:, :].unsqueeze(1).broadcast_to([P, PLANES * WORDS, BITS]),
                                           ALU.logical_shift_right))
                    k.vown.wait()
                    v.tensor_scalar(bits[:, o % 2, :, :].rearrange("p a (w b) -> p (a w) b", b=BITS), moved[:, :, :],
                                    1, None, ALU.bitwise_and).then_inc(bits_ready, 1)

                def choose(o):
                    v.wait_ge(leaves_ready, o + 1)
                    left = tree[:, o % 2, :, :]
                    for level in range(1, PLANES):
                        step = 2 ** (level - 1)
                        count = CODES // 2 // (2 * step)
                        mask = bits[:, o % 2, level, :].unsqueeze(1).broadcast_to([P, count, D])
                        ins = v.copy_predicated(left[:, 0::2 * step, :], mask, left[:, step::2 * step, :])
                        if level == PLANES - 1:
                            ins.then_inc(weight_ready, 1)
                        else:
                            k.vown(ins)
                            k.vown.wait()

                unpack(0)
                for o in range(OT):
                    if o + 1 < OT:
                        unpack(o + 1)
                    choose(o)
                k.vown.wait()
                for t in range(TILES):
                    v.wait_ge(product_psum, t + 1)
                    k.vown(v.tensor_tensor(k.x[:, t, :], k.bank[4 + t][:, :], k.x[:, t, :], ALU.add))
                k.vown.wait()

            @block.scalar
            def _(a):
                def weightT_copy(o):
                    a.wait_ge(weightT_psum, o + 1)
                    a.copy(weightT[:, :, o * P:(o + 1) * P],
                                   k.bank[2 + o % 2][:, :].rearrange("p (f c) -> p f c", f=KT)).then_inc(weightT_ready, 1)

                norm_scalar(k, m, k.bank[0:2])
                a.wait_ge(diff_ready, 1)
                for o in range(OT):
                    a.wait_ge(bits_ready, o + 1)
                    if o >= 2:
                        a.wait_ge(weightT_psum, o - 1)
                    for j in range(CODES // 2):
                        ins = a.activation(tree[:, o % 2, j, :], bits[:, o % 2, 0, :], ACT.Identity,
                                           bias=lut[:, o, 2 * j:2 * j + 1], scale=diff[:, o, j:j + 1])
                    ins.then_inc(leaves_ready, 1)
                    if o >= 1:
                        weightT_copy(o - 1)
                weightT_copy(OT - 1)

            @block.tensor
            def _(pe):
                norm_tensor(k, n, m, k.bank[0:2])
                for o in range(OT):
                    pe.wait_ge(weight_ready, o + 1)
                    if o >= 2:
                        pe.wait_ge(weightT_ready, o - 1)
                    for f in range(KT):
                        last = pe.transpose(k.bank[2 + o % 2][:, f * P:(f + 1) * P],
                                            tree[:, o % 2, 0, f * P:(f + 1) * P], k.ident[:, :])
                    last.then_inc(weightT_psum, 1)
                pe.wait_ge(k.xnT_ready, TILES * (m + 1))
                pe.wait_ge(weightT_ready, OT)
                for t in range(TILES):
                    for f in range(KT):
                        last = pe.matmul(k.bank[4 + t][:, :], k.xnT[:, f, t * P:(t + 1) * P], weightT[:, f, :],
                                         start=f == 0, stop=f == KT - 1)
                    last.then_inc(product_psum, 1)



def layer1_attention(k, dram):
    nc, n, m = k.nc, k.norms, k.turned
    k.norms += 1
    k.turned += 1
    HEADS, LQ, LKV, HD = 16, D // 8, D // 16, D // 16
    GROUP = P // LKV
    GROUPS = HEADS // GROUP
    SCALE = LKV ** -0.5
    with ExitStack() as s:
        wq = k.sbuf("wq", [P, KT, LQ], F32, s)
        wkv = k.sbuf("wkv", [P, KT, P], F32, s)
        wqk = k.sbuf("wqk", [LQ, HEADS * LKV], F32, s)
        wv = k.sbuf("wv", [LKV, D], F32, s)
        keysT = k.sbuf("keysT", [P, B, CTX], F32, s)
        keysT_now = k.sbuf("keysT_now", [P, CTX], F32, s)
        values = k.sbuf("values", [P, CTILES, D], F32, s)
        latentT = k.sbuf("latentT", [LQ, TILES * P], F32, s)
        queriesT = k.sbuf("queriesT", [P, GROUPS, P], F32, s)
        probs = k.sbuf("probs", [P, 3, CTX], F32, s)
        probsT = k.sbuf("probsT", [P, 2, CPB, P], F32, s)
        negmax = k.sbuf("negmax", [P, HEADS], F32, s)
        sums = k.sbuf("sums", [P, HEADS], F32, s)
        inverse = k.sbuf("inverse", [P, HEADS], F32, s)
        mixed = k.sbuf("mixed", [P, D], F32, s)
        loaded, keys_psum, keys_ready, values_psum, values_ready, latent_psum, latent_ready, queries_psum, \
            queries_ready, keys_now, scores_psum, negmax_ready, probs_ready, probsT_psum, probsT_even, probsT_odd, \
            heads_done, inverse_ready, mixed_ready, x_updated = (k.sem(f"l1a_{x}") for x in (
                "loaded", "keys_psum", "keys_ready", "values_psum", "values_ready", "latent_psum", "latent_ready",
                "queries_psum", "queries_ready", "keys_now", "scores_psum", "negmax_ready", "probs_ready",
                "probsT_psum", "probsT_even", "probsT_odd", "heads_done", "inverse_ready", "mixed_ready", "x_updated"))
        S, T, O, Q = k.bank[0:2], k.bank[2:4], k.bank[4], k.bank[5]
        with nc.Block(no_gpsimd_drain=True) as block:

            @block.sync
            def _(sp):
                for target, source in ((wq[:, :, :], dram["L1_xattn_Wq_d"].rearrange("(f p) c -> p f c", p=P)),
                                       (wkv[:, :, :], dram["wkv4"].rearrange("(f p) c -> p f c", p=P)),
                                       (wqk[:, :], dram["L1_xattn_W_qk"]), (wv[:, :], dram["L1_xattn_Wv_u"])):
                    sp.dma_start(target, source).then_inc(loaded, 16)

            @block.gpsimd
            def _(g):
                norm_gpsimd(k, n)
                g.wait_ge(keys_ready, B)
                with g.Fori(0, TILES) as t:
                    g.wait_ge(heads_done, HEADS * t + 1)
                    g.tensor_copy(keysT_now[:, :], keysT[:, t // TPB, :]).then_inc(keys_now, 1)

            @block.tensor
            def _(pe):
                pe.wait_ge(loaded, 64)
                pe.wait_ge(k.ctxT_loaded, 16)
                for b in range(B):
                    for f in range(KT):
                        last = pe.matmul(k.bank[6 + b][:, :], wkv[:, f, :], k.ctxT[:, f, b * CTX:(b + 1) * CTX],
                                         start=f == 0, stop=f == KT - 1)
                    last.then_inc(keys_psum, 1)
                for r in range(CTILES):
                    pe.wait_ge(keys_ready, r // CPB + 1)
                    if r >= 2:
                        pe.wait_ge(values_ready, r - 1)
                    pe.matmul(S[r % 2][:, :], keysT[0:LKV, r // CPB, (r % CPB) * P:(r % CPB + 1) * P], wv[:, :],
                              start=True, stop=True).then_inc(values_psum, 1)
                norm_tensor(k, n, m, T)
                pe.wait_ge(k.xnT_ready, TILES * (m + 1))
                for f in range(KT):
                    last = pe.matmul(Q[0:LQ, :], wq[:, f, :], k.xnT[:, f, :], start=f == 0, stop=f == KT - 1)
                last.then_inc(latent_psum, 1)
                pe.wait_ge(latent_ready, 1)
                pe.wait_ge(values_ready, CTILES)
                pe.sem_inc(heads_done, 1)

                with pe.Fori(0, TILES) as t:
                    pe.wait_ge(heads_done, HEADS * t + 1)
                    for g in range(GROUPS):
                        last = pe.matmul(Q[:, g * P:(g + 1) * P], wqk[:, g * P:(g + 1) * P],
                                         latentT[:, bass.ts(t, P)], start=True, stop=True)
                    last.then_inc(queries_psum, 1)
                    pe.wait_ge(queries_ready, t + 1)
                    pe.wait_ge(keys_now, t + 1)

                    def scores(h):
                        if h >= 2:
                            pe.wait_ge(probs_ready, HEADS * t + (h - 1))
                        g, j = h // GROUP, h % GROUP
                        pe.matmul(S[h % 2][:, :], queriesT[j * LKV:(j + 1) * LKV, g, :],
                                  keysT_now[j * LKV:(j + 1) * LKV, :], start=True, stop=True).then_inc(scores_psum, 1)

                    def turn(h):
                        pe.wait_ge(probs_ready, HEADS * t + (h + 1))
                        if h >= 2:
                            pe.wait_ge((probsT_even, probsT_odd)[h % 2], HEADS // 2 * t + (h // 2))
                        for c in range(CPB):
                            last = pe.transpose(T[h % 2][:, c * P:(c + 1) * P], probs[:, h % 3, c * P:(c + 1) * P],
                                                k.ident[:, :])
                        last.then_inc(probsT_psum, 1)

                    def mix(h):
                        pe.wait_ge((probsT_even, probsT_odd)[h % 2], HEADS // 2 * t + (h // 2 + 1))
                        for c in range(CPB):
                            last = pe.matmul(O[:, h * HD:(h + 1) * HD], probsT[:, h % 2, c, :],
                                             values[:, t // TPB * CPB + c, h * HD:(h + 1) * HD],
                                             start=c == 0, stop=c == CPB - 1)
                        last.then_inc(heads_done, 1)

                    scores(0)
                    scores(1)
                    for h in range(HEADS):
                        turn(h)
                        if h + 2 < HEADS:
                            scores(h + 2)
                        if h >= 1:
                            mix(h - 1)
                    mix(HEADS - 1)
                    pe.wait_ge(mixed_ready, t + 1)

            @block.vector
            def _(v):
                norm_vector(k, n)
                for b in range(B):
                    v.wait_ge(keys_psum, b + 1)
                    v.tensor_copy(keysT[:, b, :], k.bank[6 + b][:, :]).then_inc(keys_ready, 1)
                for r in range(CTILES):
                    v.wait_ge(values_psum, r + 1)
                    v.tensor_copy(values[:, r, :], S[r % 2][:, :]).then_inc(values_ready, 1)
                with v.Fori(0, TILES) as t:

                    def copy_turned(h):
                        v.wait_ge(probsT_psum, HEADS * t + (h + 1))
                        if h >= 2:
                            v.wait_ge(heads_done, HEADS * t + h)
                        v.tensor_copy(probsT[:, h % 2, :, :], T[h % 2][:, :].rearrange("p (c q) -> p c q", c=CPB))\
                         .then_inc(probsT_even, 1)

                    for h in range(HEADS):
                        v.wait_ge(scores_psum, HEADS * t + (h + 1))
                        v.tensor_reduce(negmax[:, h:h + 1], S[h % 2][:, :], AX.X, ALU.max, negate=True)\
                         .then_inc(negmax_ready, 1)
                        if h >= 2 and h % 2 == 0:
                            copy_turned(h - 2)
                    copy_turned(HEADS - 2)
                    v.wait_ge(probs_ready, HEADS * t + HEADS)
                    v.reciprocal(inverse[:, :], sums[:, :]).then_inc(inverse_ready, 1)
                    v.wait_ge(inverse_ready, t + 1)
                    v.wait_ge(heads_done, HEADS * t + (HEADS + 1))
                    v.tensor_tensor(mixed[:, :].rearrange("p (h d) -> p h d", h=HEADS),
                                    O[:, :].rearrange("p (h d) -> p h d", h=HEADS),
                                    inverse[:, :].unsqueeze(2).broadcast_to([P, HEADS, HD]), ALU.mult)\
                     .then_inc(mixed_ready, 1)
                    v.wait_ge(mixed_ready, t + 1)
                    v.tensor_tensor(k.x[:, t, :], k.x[:, t, :], mixed[:, :], ALU.add).then_inc(x_updated, 1)
                v.wait_ge(x_updated, TILES)

            @block.scalar
            def _(a):
                norm_scalar(k, m, T)
                a.wait_ge(latent_psum, 1)
                a.activation(latentT[:, :], Q[0:LQ, :], ACT.Copy, scale=SCALE).then_inc(latent_ready, 1)
                with a.Fori(0, TILES) as t:
                    a.wait_ge(queries_psum, t + 1)
                    a.copy(queriesT[:, :, :], Q[:, :].rearrange("p (g c) -> p g c", g=GROUPS)).then_inc(queries_ready, 1)

                    def copy_turned(h):
                        a.wait_ge(probsT_psum, HEADS * t + (h + 1))
                        if h >= 2:
                            a.wait_ge(heads_done, HEADS * t + h)
                        a.copy(probsT[:, h % 2, :, :], T[h % 2][:, :].rearrange("p (c q) -> p c q", c=CPB))\
                         .then_inc(probsT_odd, 1)

                    for h in range(HEADS):
                        a.wait_ge(negmax_ready, HEADS * t + (h + 1))
                        if h >= 3:
                            a.wait_ge(probsT_psum, HEADS * t + (h - 2))
                        a.activation(probs[:, h % 3, :], S[h % 2][:, :], ACT.Exp, bias=negmax[:, h:h + 1],
                                     accum_out=sums[:, h:h + 1]).then_inc(probs_ready, 1)
                        if h >= 2 and h % 2 == 1:
                            copy_turned(h - 2)
                    copy_turned(HEADS - 1)



def layer1_ffn(k, dram):
    nc, n = k.nc, k.norms
    k.norms += 1
    I = 1376
    IT = -(-I // P)
    TAIL = I - (IT - 1) * P
    CHUNKS = [(c, min(c + 512, I)) for c in range(0, I, 512)]
    NC = len(CHUNKS)
    SQRT7 = float(np.float32(np.sqrt(7.0)))
    GATE, UP, DOWN = range(3)
    with ExitStack() as s:
        raw = k.sbuf("raw", [P, KT, I], F32, s)
        rawd = k.sbuf("rawd", [P, IT, D], F32, s)
        work = k.sbuf("work", [P, max(KT * I, IT * D)], F32, s)
        wgu = k.sbuf("wgu", [P, 2, KT, I], BF16, s)
        wd = k.sbuf("wd", [P, IT, D], BF16, s)
        total = k.sbuf("total", [P, 4], F32, s)
        wmean = k.sbuf("wmean", [P, 3], F32, s)
        winv = k.sbuf("winv", [P, 3], F32, s)
        scales = k.sbuf("scales", [P, 3], F32, s)
        wscale = k.sbuf("wscale", [P, 3], F32, s)
        round_col = k.sbuf("round_col", [P, 1], F32, s)
        t1 = k.sbuf("t1", [P, TILES, D], F32, s)
        x4 = k.sbuf("x4", [P, TILES, D], BF16, s)
        x4T = k.sbuf("x4T", [P, KT, TILES * P], BF16, s)
        beta = k.sbuf("beta", [P, TILES], F32, s)
        betae = k.sbuf("betae", [P, TILES], F32, s)
        binv = k.sbuf("binv", [P, TILES], F32, s)
        gate_scale = k.sbuf("gate_scale", [P, TILES], F32, s)
        up_scale = k.sbuf("up_scale", [P, TILES], F32, s)
        relu = k.sbuf("relu", [P, 2, 512], F32, s)
        gate = k.sbuf("gate", [P, 2, 512], F32, s)
        inner = k.sbuf("inner", [P, 2, I], F32, s)
        gamma = k.sbuf("gamma", [P, TILES], F32, s)
        gammae = k.sbuf("gammae", [P, TILES], F32, s)
        ginv = k.sbuf("ginv", [P, TILES], F32, s)
        x8 = k.sbuf("x8", [P, 2, I], BF16, s)
        x8T = k.sbuf("x8T", [P, IT, TILES * P], BF16, s)
        down_scale = k.sbuf("down_scale", [P, TILES], F32, s)
        loaded = [k.sem(f"l1f_loaded_{x}") for x in ("gate", "up", "down")]
        scales_loaded, raw_free, total_ready, total_psum, winv_ready, rounded, clipped, weights_ready, x4_ready, \
            x4T_psum, x4T_ready, gate_psum, up_psum, relu_ready, gate_ready, inner_ready, x8_ready, x8T_psum, \
            x8T_ready, down_psum, constants = (k.sem(f"l1f_{x}") for x in (
                "scales_loaded", "raw_free", "total_ready", "total_psum", "winv_ready", "rounded", "clipped",
                "weights_ready", "x4_ready", "x4T_psum", "x4T_ready", "gate_psum", "up_psum", "relu_ready",
                "gate_ready", "inner_ready", "x8_ready", "x8T_psum", "x8T_ready", "down_psum", "constants"))
        G, U, T, O = k.bank[0:2], k.bank[2:4], k.bank[4:6], k.bank[6:8]
        raws = [raw[:, :, :].rearrange("p f c -> p (f c)")] * 2 + [rawd[:, :, :].rearrange("p f c -> p (f c)")]
        targets = [wgu[:, 0, :, :].rearrange("p f c -> p (f c)"), wgu[:, 1, :, :].rearrange("p f c -> p (f c)"),
                   wd[:, :, :].rearrange("p f c -> p (f c)")]
        names = ("w_gateT", "w_upT", "w_downT")
        with nc.Block(no_gpsimd_drain=True) as block:

            def load(w):
                if w == DOWN:
                    nc.sync.wait_ge(constants, 1)
                    nc.sync.dma_start(rawd[:, 0:IT - 1, :], dram["w_downT"][0:(IT - 1) * P, :]
                                      .rearrange("(f p) c -> p f c", p=P)).then_inc(loaded[w], 16)
                    nc.sync.dma_start(rawd[0:TAIL, IT - 1, :], dram["w_downT"][(IT - 1) * P:I, :])\
                      .then_inc(loaded[w], 16)
                else:
                    nc.sync.dma_start(raw[:, :, :], dram[names[w]].rearrange("(f p) c -> p f c", p=P))\
                      .then_inc(loaded[w], 16)

            @block.sync
            def _(sp):
                for i, name in enumerate(("s_gate", "s_up", "s_down")):
                    sp.dma_start(scales[:, i:i + 1], dram["L1_ffn_" + name].unsqueeze(0).broadcast_to([P, 1]))\
                      .then_inc(scales_loaded, 16)
                load(GATE)
                load(DOWN)
                sp.wait_ge(rounded, 1)
                load(UP)

            @block.gpsimd
            def _(g):
                g.memset(rawd[:, IT - 1, :], 0.0).then_inc(constants, 1)
                g.memset(round_col[:, :], ROUND).then_inc(constants, 1)
                norm_gpsimd(k, n)

            @block.scalar
            def _(a):
                a.wait_ge(constants, 2)
                for i, w in enumerate((GATE, DOWN, UP)):
                    size = IT * D if w == DOWN else KT * I
                    a.wait_ge(loaded[w], 32 if w == DOWN else 16)
                    if i >= 1:
                        a.wait_ge(weights_ready, i)
                    a.activation(work[:, 0:size], raws[w], ACT.Abs, accum_out=total[:, w:w + 1])\
                     .then_inc(total_ready, 1)
                    a.wait_ge(total_ready, i + 1)
                    a.wait_ge(winv_ready, i + 1)
                    a.activation(work[:, 0:size], raws[w], ACT.Identity, bias=round_col[:, 0:1],
                                 scale=winv[:, w:w + 1]).then_inc(rounded, 1)
                for t in range(TILES):
                    a.wait_ge(x4T_psum, t + 1)
                    a.copy(x4T[:, :, t * P:(t + 1) * P],
                           T[t % 2][:, 0:256].bitcast(BF16).rearrange("p (f c) -> p f c", f=KT)).then_inc(x4T_ready, 1)

                def x8T_copy(t):
                    for half, (first, last) in enumerate(((0, 8), (8, IT))):
                        a.wait_ge(x8T_psum, 2 * t + half + 1)
                        rows = P if half == 0 else TAIL
                        source = T[half][:, :].bitcast(BF16).rearrange("p (f c) -> p f c", f=8)
                        if half == 0:
                            a.copy(x8T[:, 0:8, t * P:(t + 1) * P], source).then_inc(x8T_ready, 1)
                        else:
                            k.aown(a.copy(x8T[:, 8:IT - 1, t * P:(t + 1) * P], source[:, 0:IT - 9, :]))
                            a.copy(x8T[0:TAIL, IT - 1, t * P:(t + 1) * P], source[0:TAIL, IT - 9, :])\
                             .then_inc(x8T_ready, 1)

                for t in range(TILES):
                    for c, (c0, c1) in enumerate(CHUNKS):
                        i = NC * t + c
                        a.wait_ge(gate_psum, i + 1)
                        a.activation(relu[:, i % 2, 0:c1 - c0], G[i % 2][:, 0:c1 - c0], ACT.Relu,
                                     scale=gate_scale[:, t:t + 1]).then_inc(relu_ready, 1)
                        a.wait_ge(relu_ready, i + 1)
                        if i >= 2:
                            a.wait_ge(inner_ready, i - 1)
                        a.activation(gate[:, i % 2, 0:c1 - c0], relu[:, i % 2, 0:c1 - c0], ACT.Square)\
                         .then_inc(gate_ready, 1)
                    if t >= 1:
                        x8T_copy(t - 1)
                x8T_copy(TILES - 1)

            @block.vector
            def _(v):
                norm_vector(k, n)
                v.wait_ge(scales_loaded, 48)

                def weight_scale(i, w):
                    k.vown(v.tensor_scalar(wmean[:, w:w + 1], k.bank[6 + i % 2][:, 0:1], 1.0 / (I * D), None, ALU.mult))
                    k.vown.wait()
                    k.vown(v.tensor_scalar(winv[:, w:w + 1], wmean[:, w:w + 1], EPS, None, ALU.add))
                    k.vown(v.tensor_tensor(wscale[:, w:w + 1], wmean[:, w:w + 1], scales[:, w:w + 1], ALU.mult))
                    k.vown.wait()
                    v.reciprocal(winv[:, w:w + 1], winv[:, w:w + 1]).then_inc(winv_ready, 1)

                def weight_round(i, w):
                    size = IT * D if w == DOWN else KT * I
                    v.wait_ge(rounded, i + 1)
                    v.tensor_scalar(work[:, 0:size], work[:, 0:size], ROUND, -1.0, ALU.subtract, ALU.max)\
                     .then_inc(clipped, 1)
                    v.wait_ge(clipped, i + 1)
                    v.tensor_scalar(targets[w], work[:, 0:size], 1.0, None, ALU.min).then_inc(weights_ready, 1)

                def weight(i, w):
                    v.wait_ge(total_psum, i + 1)
                    weight_scale(i, w)
                    weight_round(i, w)

                weight(0, GATE)
                v.wait_ge(k.xn_ready, TILES * (n + 1))
                for t in range(TILES):
                    k.vown(v.tensor_reduce(beta[:, t:t + 1], k.xn[:, t, :], AX.X, ALU.add, apply_absolute_value=True))
                k.vown.wait()
                k.vown(v.tensor_scalar(beta[:, :], beta[:, :], 1.0 / D, None, ALU.mult))
                k.vown.wait()
                k.vown(v.tensor_scalar(betae[:, :], beta[:, :], EPS, None, ALU.add))
                k.vown.wait()
                k.vown(v.reciprocal(binv[:, :], betae[:, :]))
                k.vown.wait()
                for t in range(TILES):
                    k.vown(v.tensor_scalar(t1[:, t, :], k.xn[:, t, :], SQRT7, binv[:, t:t + 1], ALU.mult, ALU.mult))
                k.vown.wait()
                for t in range(TILES):
                    k.vown(v.tensor_scalar(t1[:, t, :], t1[:, t, :], ROUND, ROUND, ALU.add, ALU.subtract))
                k.vown.wait()
                for t in range(TILES):
                    v.tensor_scalar(x4[:, t, :], t1[:, t, :], -8.0, 7.0, ALU.max, ALU.min).then_inc(x4_ready, 1)
                weight(1, DOWN)
                weight(2, UP)
                k.vown(v.tensor_scalar(betae[:, :], beta[:, :], SQRT7, 1.0 / SQRT7, ALU.mult, ALU.mult))
                k.vown.wait()
                k.vown(v.tensor_scalar(up_scale[:, :], betae[:, :], wscale[:, UP:UP + 1], None, ALU.mult))
                k.vown(v.tensor_scalar(gate_scale[:, :], betae[:, :], wscale[:, GATE:GATE + 1], None, ALU.mult))
                k.vown.wait()
                v.engine_nop().then_inc(constants, 1)

                def quantise8(t):
                    k.vown(v.tensor_reduce(gamma[:, t:t + 1], inner[:, t % 2, :], AX.X, ALU.max, apply_absolute_value=True))
                    k.vown.wait()
                    k.vown(v.tensor_scalar(gammae[:, t:t + 1], gamma[:, t:t + 1], EPS, None, ALU.add))
                    k.vown.wait()
                    k.vown(v.reciprocal(ginv[:, t:t + 1], gammae[:, t:t + 1]))
                    k.vown.wait()
                    k.vown(v.tensor_scalar(inner[:, t % 2, :], inner[:, t % 2, :], 127.0, ginv[:, t:t + 1],
                                           ALU.mult, ALU.mult))
                    k.vown.wait()
                    k.vown(v.tensor_scalar(inner[:, t % 2, :], inner[:, t % 2, :], ROUND, ROUND, ALU.add, ALU.subtract))
                    k.vown.wait()
                    if t >= 2:
                        v.wait_ge(x8T_psum, 2 * (t - 1))
                    v.tensor_scalar(x8[:, t % 2, :], inner[:, t % 2, :], -128.0, 127.0, ALU.max, ALU.min)\
                     .then_inc(x8_ready, 1)

                for t in range(TILES):
                    for c, (c0, c1) in enumerate(CHUNKS):
                        i = NC * t + c
                        v.wait_ge(up_psum, i + 1)
                        v.wait_ge(gate_ready, i + 1)
                        if t >= 2:
                            v.wait_ge(x8_ready, t - 1)
                        v.scalar_tensor_tensor(inner[:, t % 2, c0:c1], U[i % 2][:, 0:c1 - c0], up_scale[:, t:t + 1],
                                               gate[:, i % 2, 0:c1 - c0], ALU.mult, ALU.mult).then_inc(inner_ready, 1)
                    v.wait_ge(inner_ready, NC * (t + 1))
                    quantise8(t)
                k.vown(v.tensor_scalar(gammae[:, :], gamma[:, :], 1.0 / 127.0, wscale[:, DOWN:DOWN + 1], ALU.mult, ALU.mult))
                k.vown.wait()
                for t in range(TILES):
                    v.wait_ge(down_psum, t + 1)
                    k.vown(v.scalar_tensor_tensor(k.x[:, t, :], O[t % 2][:, :], gammae[:, t:t + 1], k.x[:, t, :],
                                                  ALU.mult, ALU.add))
                    k.vown.wait()
                    v.engine_nop().then_inc(clipped, 1)

            @block.tensor
            def _(pe):
                for i, w in enumerate((GATE, DOWN, UP)):
                    pe.wait_ge(total_ready, i + 1)
                    if i >= 2:
                        pe.wait_ge(winv_ready, i - 1)
                    pe.matmul(k.bank[6 + i % 2][:, 0:1], k.ones[:, :], total[:, w:w + 1], start=True, stop=True)\
                      .then_inc(total_psum, 1)
                for t in range(TILES):
                    pe.wait_ge(x4_ready, t + 1)
                    if t >= 2:
                        pe.wait_ge(x4T_ready, t - 1)
                    for f in range(KT):
                        last = pe.transpose(T[t % 2][:, 0:256].bitcast(BF16)[:, f * P:(f + 1) * P],
                                            x4[:, t, f * P:(f + 1) * P], k.ident16[:, :])
                    last.then_inc(x4T_psum, 1)
                pe.wait_ge(x4T_ready, TILES)
                pe.wait_ge(weights_ready, 3)
                pe.wait_ge(constants, 3)

                def turn8(t):
                    pe.wait_ge(x8_ready, t + 1)
                    for f in range(IT):
                        rows = P if f < IT - 1 else TAIL
                        half = f // 8
                        if f % 8 == 0 and t >= 1:
                            pe.wait_ge(x8T_ready, 2 * (t - 1) + half + 1)
                        last = pe.transpose(T[half][:, :].bitcast(BF16)[0:rows, f % 8 * P:(f % 8 + 1) * P],
                                            x8[:, t % 2, f * P:f * P + rows], k.ident16[:, :])
                        if f in (7, IT - 1):
                            last.then_inc(x8T_psum, 1)

                for t in range(TILES):
                    for c, (c0, c1) in enumerate(CHUNKS):
                        i = NC * t + c
                        if i >= 2:
                            pe.wait_ge(relu_ready, i - 1)
                            pe.wait_ge(inner_ready, i - 1)
                        for w, bank, ready in ((GATE, G, gate_psum), (UP, U, up_psum)):
                            for f in range(KT):
                                last = pe.matmul(bank[i % 2][:, 0:c1 - c0], x4T[:, f, t * P:(t + 1) * P],
                                                 wgu[:, w, f, c0:c1], start=f == 0, stop=f == KT - 1)
                            last.then_inc(ready, 1)
                    if t >= 1:
                        turn8(t - 1)
                turn8(TILES - 1)
                for t in range(TILES):
                    pe.wait_ge(x8T_ready, 2 * (t + 1))
                    if t >= 2:
                        pe.wait_ge(clipped, 3 + t - 1)
                    for f in range(IT):
                        rows = P if f < IT - 1 else TAIL
                        last = pe.matmul(O[t % 2][:, :], x8T[0:rows, f, t * P:(t + 1) * P], wd[0:rows, f, :],
                                         start=f == 0, stop=f == IT - 1)
                    last.then_inc(down_psum, 1)



PARTS = ((0, 0), (0, 1), (1, 0))


class LoopOwn:

    def __init__(self, engine, semaphore, i, per):
        self.engine, self.semaphore, self.i, self.per, self.count = engine, semaphore, i, per, 0

    def __call__(self, instruction):
        instruction.then_inc(self.semaphore, 1)
        self.count += 1

    def wait(self):
        self.engine.wait_ge(self.semaphore, self.i * self.per + self.count)


def layer2_attention(k, dram):
    nc, n = k.nc, k.norms
    k.norms += 1
    HEADS, GROUPS, HD = 32, 8, 128
    REP = HEADS // GROUPS
    GW = REP * HD
    UNITS = B * REP * TPB
    PAIRS = UNITS // 2
    CHUNKS = 6
    SCALE = HD ** -0.5
    ROUNDS = 4
    with ExitStack() as s:
        xnT2 = k.sbuf("xnT2", [P, 2, KT, TILES * P], F32R, s)
        ctxT2 = k.sbuf("ctxT2", [P, 2, KT, B * CTX], F32R, s)
        raw = k.sbuf("raw_weights", [P, KT * GW], F32, s)
        wq = k.sbuf("wq2", [P, 2, KT, GW], F32R, s)
        wkv = k.sbuf("wkv2", [P, 2, KT, 2 * HD], F32R, s)
        wo = k.sbuf("wo2", [P, 2, REP, D], F32R, s)
        rows = k.xn
        squares = k.sbuf("squares", [P, 2, GW], F32, s)
        ssq = k.sbuf("ssq", [P, CHUNKS, REP], F32, s)
        rms = k.sbuf("rms", [P, CHUNKS, REP], F32, s)
        headsT = k.sbuf("headsT", [P, 2, REP, TILES * P], F32R, s)
        keysT = k.sbuf("keysT2", [P, 2, B * CTX], F32R, s)
        values = k.sbuf("values2", [P, 2, CTILES, HD], F32R, s)
        mask = k.sbuf("mask", [P, TPB, CTX], F32, s)
        weights = k.sbuf("norm_weights", [P, 2], F32, s)
        keyscale = k.sbuf("keyscale", [P, 1], F32, s)
        masked = k.xnT[:, 0:2, :]
        probs = k.sbuf("probs2", [P, 3, CTX], F32, s)
        probsT = k.sbuf("probsT2", [P, 2, 2, CPB, SEQ], F32R, s)
        negmax = k.sbuf("negmax2", [P, UNITS], F32, s)
        sums = k.sbuf("sums2", [P, UNITS], F32, s)
        inverse = k.sbuf("inverse2", [P, UNITS], F32, s)
        names = ("mask_loaded", "raw_loaded", "raw_split", "ctx_high", "ctx_low", "xnT_high", "xnT_low", "keyscale_ready",
                 "stepped", "pool_stepped", "xnT_psum", "kv_psum", "q_psum", "rows_copied", "squared", "ssq_ready", "gpsimd_loop", "rows_normed", "rowsT_psum",
                 "rowsT_high", "rowsT_low", "values_high", "values_low", "scores_psum", "max_ready", "exp_ready",
                 "inverse_ready", "probs_ready", "probsT_psum", "probsT_high", "probsT_low", "mix_psum", "mixT_high",
                 "mixT_low", "out_psum", "out_added", "bisect")
        S_ = {x: k.sem(f"l2a_{x}") for x in names}
        S, T, V, J = k.bank[0:2], k.bank[2:4], k.bank[4:6], k.bank[6:8]
        unit = lambda u: (u // (REP * TPB), u // TPB % REP, u % TPB)
        wq_dram = dram["wqT"].rearrange("(f p) (g c) -> g p f c", p=P, c=GW)
        wkv_dram = dram["wkvT"].rearrange("(f p) (g c) -> g p f c", p=P, c=2 * HD)
        wo_dram = dram["woT"].rearrange("(g h p) c -> g p h c", p=P, h=REP)

        with nc.Block(no_gpsimd_drain=True) as block:

            @block.sync
            def _(sp):
                sp.dma_start(mask[:, :, :], dram["mask_1x1xSxS2_ff0"][0, 0].rearrange("(t p) c -> p t c", p=P))\
                  .then_inc(S_["mask_loaded"], 16)
                for i, name in enumerate(("q_norm_w", "k_norm_w")):
                    sp.dma_start(weights[:, i:i + 1], dram["L2_xattn_" + name].unsqueeze(1)).then_inc(S_["mask_loaded"], 16)

                def load(columns, source):
                    sp.dma_start(raw[:, 0:columns].rearrange("p (f c) -> p f c", f=KT), source)\
                      .then_inc(S_["raw_loaded"], 16)

                load(KT * 2 * HD, wkv_dram[0])
                sp.wait_ge(S_["raw_split"], 1)
                load(KT * GW, wq_dram[0])
                with sp.Fori(0, GROUPS) as g:
                    sp.wait_ge(S_["raw_split"], 3 * g + 2)
                    load(KT * GW, wo_dram[g])
                    sp.wait_ge(S_["raw_split"], 3 * g + 3)
                    load(KT * 2 * HD, wkv_dram[g + 1])
                    sp.wait_ge(S_["raw_split"], 3 * g + 4)
                    load(KT * GW, wq_dram[g + 1])

            PER_POOL = 2 * CHUNKS + 3 * (2 * KT - 1)
            chunk_rows = lambda c: 2 + c if c < 2 else c % 2

            def turned(c):
                if c < 2:
                    return [keysT[:, part, c * CTX:(c + 1) * CTX] for part in range(2)], T[c % 2][:, :]
                t = c - 2
                return ([headsT[:, part, :, t * P:(t + 1) * P] for part in range(2)],
                        T[c % 2][:, :].rearrange("p (h q) -> p h q", h=REP))

            @block.gpsimd
            def _(g):
                norm_gpsimd(k, n)
                for f in range(KT):
                    g.wait_ge(S_["ctx_high"], f + 1)
                    g.tensor_tensor(ctxT2[:, 1, f, :], k.ctxT[:, f, :], ctxT2[:, 0, f, :], ALU.subtract)\
                     .then_inc(S_["ctx_low"], 1)

                def split_weights(own, target, f):
                    columns = target.shape[3]
                    source = raw[:, f * columns:(f + 1) * columns]
                    own(g.tensor_copy(target[:, 0, f, :], source))
                    own.wait()
                    ins = g.tensor_tensor(target[:, 1, f, :], source, target[:, 0, f, :], ALU.subtract)
                    if f == KT - 1:
                        ins.then_inc(S_["raw_split"], 1)
                    else:
                        own(ins)

                for j, target in enumerate((wkv, wq)):
                    g.wait_ge(S_["raw_loaded"], 16 * (j + 1))
                    for f in range(KT):
                        split_weights(k.pown, target, f)

                with g.Fori(0, GROUPS) as i:
                    own = LoopOwn(g, S_["gpsimd_loop"], i, PER_POOL)

                    def square(c):
                        g.wait_ge(S_["rows_copied"], 8 * i + (2 * c + 2 if c < 2 else c + 3))
                        if c >= 2:
                            g.wait_ge(S_["ssq_ready"], CHUNKS * i + (c - 1))
                        r = rows[:, chunk_rows(c), :]
                        g.tensor_tensor(squares[:, c % 2, :], r, r, ALU.mult).then_inc(S_["squared"], 1)

                    def norm(c):
                        g.wait_ge(S_["ssq_ready"], CHUNKS * i + (c + 1))
                        g.sem_inc(S_["pool_stepped"], 1)
                        own(g.tensor_scalar(ssq[:, c, :], ssq[:, c, :], 1.0 / HD, EPS, ALU.mult, ALU.add))
                        own.wait()
                        own(g.tensor_tensor(rms[:, c, :], ssq[:, c, :], k.minus_half[:, 0:REP], ALU.pow))
                        own.wait()
                        r = rows[:, chunk_rows(c), :].rearrange("p (h d) -> p h d", d=HD)
                        g.tensor_tensor(r, r, rms[:, c, :].unsqueeze(2).broadcast_to([P, REP, HD]), ALU.mult)\
                         .then_inc(S_["rows_normed"], 1)

                    square(0)
                    for c in range(CHUNKS):
                        if c + 1 < CHUNKS and c + 1 < 4:
                            square(c + 1)
                        norm(c)
                        if c >= 3 and c + 1 < CHUNKS:
                            square(c + 1)
                    for j, (target, free, count) in enumerate(((wo, None, 0), (wkv, "kv_psum", 4), (wq, "q_psum", 4))):
                        g.wait_ge(S_["raw_loaded"], 48 * i + 16 * (j + 3))
                        if free:
                            g.wait_ge(S_[free], count * i + count)
                        g.sem_inc(S_["pool_stepped"], 1)
                        for f in range(KT):
                            split_weights(own, target, f)
                    assert own.count == PER_POOL, own.count

            @block.tensor
            def _(pe):
                norm_tensor_two(k, n, T, S_["xnT_psum"], S_["xnT_low"])
                pe.wait_ge(S_["xnT_low"], TILES)
                pe.wait_ge(S_["ctx_low"], KT)
                with pe.Fori(0, GROUPS) as i:
                    def product(out, stationary, moving):
                        count = len(stationary)
                        for f in range(count):
                            for x, (a, b) in enumerate(PARTS):
                                last = pe.matmul(out, stationary[f][a], moving[f][b], start=f == 0 and x == 0,
                                                 stop=f == count - 1 and x == 2)
                        return last

                    def project_kv(j):
                        if j >= 2:
                            pe.wait_ge(S_["values_low"], 4 * i + (j - 1))
                        for h in range(2):
                            r = 2 * j + h
                            last = product(J[j % 2][:, h * 2 * HD:(h + 1) * 2 * HD],
                                           [[ctxT2[:, a, f, r * P:(r + 1) * P] for a in range(2)] for f in range(KT)],
                                           [[wkv[:, b, f, :] for b in range(2)] for f in range(KT)])
                        last.then_inc(S_["kv_psum"], 1)

                    def project_q(t):
                        if t < 2:
                            pe.wait_ge(S_["values_low"], 4 * i + (t + 3))
                        else:
                            pe.wait_ge(S_["rows_copied"], 8 * i + (4 + t - 1))
                        product(J[t % 2][:, :],
                                [[xnT2[:, a, f, t * P:(t + 1) * P] for a in range(2)] for f in range(KT)],
                                [[wq[:, b, f, :] for b in range(2)] for f in range(KT)]).then_inc(S_["q_psum"], 1)

                    def turn_rows(c):
                        pe.wait_ge(S_["rows_normed"], CHUNKS * i + (c + 1))
                        if c >= 2:
                            pe.wait_ge(S_["rowsT_low"], CHUNKS * i + (c - 1))
                        for h in range(REP):
                            last = pe.transpose(T[c % 2][:, h * P:(h + 1) * P],
                                                rows[:, chunk_rows(c), h * P:(h + 1) * P], k.ident[:, :])
                        last.then_inc(S_["rowsT_psum"], 1)

                    def scores(u):
                        b, h, q = unit(u)
                        if u >= 2:
                            pe.wait_ge(S_["max_ready"], UNITS * i + (u - 1))
                        if u == 0:
                            pe.wait_ge(S_["rowsT_low"], CHUNKS * i + 4)
                        if u == REP * TPB:
                            pe.wait_ge(S_["rowsT_low"], CHUNKS * i + 6)
                        token = (b * TPB + q) * P
                        product(S[u % 2][:, :], [[headsT[:, a, h, token:token + P] for a in range(2)]],
                                [[keysT[:, x, b * CTX:(b + 1) * CTX] for x in range(2)]]).then_inc(S_["scores_psum"], 1)

                    def turn_probs(u):
                        pe.wait_ge(S_["probs_ready"], UNITS * i + (u + 1))
                        if u < 2:
                            pe.wait_ge(S_["rowsT_low"], CHUNKS * i + (u + 5))
                        else:
                            pe.wait_ge(S_["probsT_low"], UNITS * i + (u - 1))
                        for c in range(CPB):
                            last = pe.transpose(T[u % 2][:, c * P:(c + 1) * P], probs[:, u % 3, c * P:(c + 1) * P],
                                                k.ident[:, :])
                        last.then_inc(S_["probsT_psum"], 1)

                    def mix(p):
                        b = unit(2 * p)[0]
                        pe.wait_ge(S_["probsT_low"], UNITS * i + (2 * p + 2))
                        if p >= 2:
                            pe.wait_ge(S_["mixT_low"], PAIRS * i + (p - 1))
                        if p == 0:
                            pe.wait_ge(S_["values_low"], 4 * i + 4)
                        product(V[p % 2][:, 0:SEQ],
                                [[values[:, a, b * CPB + c, :] for a in range(2)] for c in range(CPB)],
                                [[probsT[:, x, p % 2, c, :] for x in range(2)] for c in range(CPB)])\
                            .then_inc(S_["mix_psum"], 1)

                    pe.wait_ge(S_["out_added"], TILES * i + 1)
                    pe.wait_ge(S_["raw_split"], 3 * i + 1)
                    for j in range(4):
                        project_kv(j)
                    pe.wait_ge(S_["raw_split"], 3 * i + 2)
                    project_q(0)
                    project_q(1)
                    turn_rows(0)
                    project_q(2)
                    turn_rows(1)
                    project_q(3)
                    turn_rows(2)
                    turn_rows(3)
                    scores(0)
                    scores(1)
                    turn_rows(4)
                    turn_rows(5)
                    for u in range(UNITS):
                        if u + 2 < UNITS:
                            scores(u + 2)
                        turn_probs(u)
                        if u >= 2 and u % 2 == 0:
                            mix(u // 2 - 1)
                    mix(PAIRS - 1)
                    pe.wait_ge(S_["mixT_low"], PAIRS * i + PAIRS)
                    pe.wait_ge(S_["raw_split"], 3 * i + 3)
                    for t in range(TILES):
                        if t >= 2:
                            pe.wait_ge(S_["out_added"], TILES * i + t)
                        product(J[t % 2][:, :],
                                [[headsT[:, a, h, t * P:(t + 1) * P] for a in range(2)] for h in range(REP)],
                                [[wo[:, x, h, :] for x in range(2)] for h in range(REP)]).then_inc(S_["out_psum"], 1)

            @block.scalar
            def _(a):
                a.wait_ge(k.ctxT_loaded, 16)
                for f in range(KT):
                    a.copy(ctxT2[:, 0, f, :], k.ctxT[:, f, :]).then_inc(S_["ctx_high"], 1)
                for t in range(TILES):
                    a.wait_ge(S_["xnT_psum"], t + 1)
                    a.copy(xnT2[:, 0, :, t * P:(t + 1) * P], T[t % 2][:, :].rearrange("p (f c) -> p f c", f=KT))\
                     .then_inc(S_["xnT_high"], 1)
                a.wait_ge(S_["keyscale_ready"], 1)
                with a.Fori(0, GROUPS) as i:
                    def copy_kv(j):
                        a.wait_ge(S_["kv_psum"], 4 * i + (j + 1))
                        both = J[j % 2][:, :].rearrange("p (r c) -> p r c", r=2)
                        a.copy(rows[:, chunk_rows(j // 2), j % 2 * 2 * HD:(j % 2 + 1) * 2 * HD]
                               .rearrange("p (r c) -> p r c", r=2), both[:, :, 0:HD]).then_inc(S_["rows_copied"], 1)
                        a.copy(values[:, 0, 2 * j:2 * j + 2, :], both[:, :, HD:2 * HD]).then_inc(S_["values_high"], 1)

                    def copy_q(t):
                        a.wait_ge(S_["q_psum"], TILES * i + (t + 1))
                        if t >= 2:
                            a.wait_ge(S_["rowsT_psum"], CHUNKS * i + (t + 1))
                        a.copy(rows[:, t % 2, :], J[t % 2][:, :]).then_inc(S_["rows_copied"], 1)

                    def rowsT(c):
                        a.wait_ge(S_["rowsT_psum"], CHUNKS * i + (c + 1))
                        (high, _), source = turned(c)
                        if c < 2:
                            a.activation(high, source, ACT.Copy, scale=keyscale[:, 0:1]).then_inc(S_["rowsT_high"], 1)
                        else:
                            a.copy(high, source).then_inc(S_["rowsT_high"], 1)

                    def exponentials(u):
                        a.wait_ge(S_["max_ready"], UNITS * i + (u + 1))
                        if u >= 3:
                            a.wait_ge(S_["probsT_psum"], UNITS * i + (u - 2))
                        a.activation(probs[:, u % 3, :], masked[:, u % 2, :], ACT.Exp, bias=negmax[:, u:u + 1],
                                     scale=-1.0, accum_out=sums[:, u:u + 1]).then_inc(S_["exp_ready"], 1)

                    def divide(u):
                        a.wait_ge(S_["inverse_ready"], UNITS * i + (u + 1))
                        a.activation(probs[:, u % 3, :], probs[:, u % 3, :], ACT.Copy, scale=inverse[:, u:u + 1])\
                         .then_inc(S_["probs_ready"], 1)

                    def probsT_high(u):
                        p = u // 2
                        a.wait_ge(S_["probsT_psum"], UNITS * i + (u + 1))
                        if p >= 2:
                            a.wait_ge(S_["mix_psum"], PAIRS * i + (p - 1))
                        a.copy(probsT[:, 0, p % 2, :, u % 2 * P:(u % 2 + 1) * P],
                               T[u % 2][:, :].rearrange("p (c q) -> p c q", c=CPB)).then_inc(S_["probsT_high"], 1)

                    def mixT_high(p):
                        b, h, _ = unit(2 * p)
                        a.wait_ge(S_["mix_psum"], PAIRS * i + (p + 1))
                        a.copy(headsT[:, 0, h, b * SEQ:(b + 1) * SEQ], V[p % 2][:, 0:SEQ]).then_inc(S_["mixT_high"], 1)

                    for j in range(4):
                        copy_kv(j)
                    copy_q(0)
                    copy_q(1)
                    rowsT(0)
                    rowsT(1)
                    rowsT(2)
                    copy_q(2)
                    rowsT(3)
                    copy_q(3)
                    exponentials(0)
                    divide(0)
                    rowsT(4)
                    rowsT(5)
                    for u in range(1, UNITS):
                        if u >= 4 and u % 2 == 0:
                            mixT_high(u // 2 - 2)
                        exponentials(u)
                        probsT_high(u - 1)
                        divide(u)
                    probsT_high(UNITS - 1)
                    mixT_high(PAIRS - 2)
                    mixT_high(PAIRS - 1)

            @block.vector
            def _(v):
                norm_vector(k, n)
                for t in range(TILES):
                    v.wait_ge(S_["xnT_high"], t + 1)
                    v.tensor_tensor(xnT2[:, 1, :, t * P:(t + 1) * P], T[t % 2][:, :].rearrange("p (f c) -> p f c", f=KT),
                                    xnT2[:, 0, :, t * P:(t + 1) * P], ALU.subtract).then_inc(S_["xnT_low"], 1)
                v.wait_ge(S_["mask_loaded"], 48)
                v.scalar_tensor_tensor(keyscale[:, :], weights[:, 0:1], SCALE, weights[:, 1:2], ALU.mult, ALU.mult)\
                 .then_inc(S_["keyscale_ready"], 1)
                v.wait_ge(S_["ctx_low"], KT)
                bisection_start(k)
                v.engine_nop().then_inc(S_["out_added"], 1)
                with v.Fori(0, GROUPS) as i:
                    own = LoopOwn(v, S_["bisect"], i, BISECT_PER_ROUND * ROUNDS)

                    def values_low(j):
                        v.wait_ge(S_["values_high"], 4 * i + (j + 1))
                        v.tensor_tensor(values[:, 1, 2 * j:2 * j + 2, :],
                                        J[j % 2][:, :].rearrange("p (r c) -> p r c", r=2)[:, :, HD:2 * HD],
                                        values[:, 0, 2 * j:2 * j + 2, :], ALU.subtract).then_inc(S_["values_low"], 1)

                    def sum_squares(c):
                        v.wait_ge(S_["squared"], CHUNKS * i + (c + 1))
                        v.tensor_reduce(ssq[:, c, :], squares[:, c % 2, :].rearrange("p (h d) -> p h d", d=HD),
                                        AX.X, ALU.add).then_inc(S_["ssq_ready"], 1)

                    def rowsT(c):
                        v.wait_ge(S_["rowsT_high"], CHUNKS * i + (c + 1))
                        (high, low), source = turned(c)
                        if c < 2:
                            v.scalar_tensor_tensor(low, source, keyscale[:, 0:1], high, ALU.mult, ALU.subtract)\
                             .then_inc(S_["rowsT_low"], 1)
                        else:
                            v.tensor_tensor(low, source, high, ALU.subtract).then_inc(S_["rowsT_low"], 1)

                    def maximum(u):
                        v.wait_ge(S_["scores_psum"], UNITS * i + (u + 1))
                        v.sem_inc(S_["stepped"], 1)
                        v.tensor_tensor_reduce(masked[:, u % 2, :], S[u % 2][:, :], mask[:, unit(u)[2], :], -1.0, 3.4e38,
                                               ALU.add, ALU.min, negmax[:, u:u + 1]).then_inc(S_["max_ready"], 1)

                    def invert(u):
                        v.wait_ge(S_["exp_ready"], UNITS * i + (u + 1))
                        v.reciprocal(inverse[:, u:u + 1], sums[:, u:u + 1]).then_inc(S_["inverse_ready"], 1)

                    def probsT_low(u):
                        p = u // 2
                        v.wait_ge(S_["probsT_high"], UNITS * i + (u + 1))
                        columns = slice(u % 2 * P, (u % 2 + 1) * P)
                        v.tensor_tensor(probsT[:, 1, p % 2, :, columns], T[u % 2][:, :].rearrange("p (c q) -> p c q", c=CPB),
                                        probsT[:, 0, p % 2, :, columns], ALU.subtract).then_inc(S_["probsT_low"], 1)

                    def mixT_low(p):
                        b, h, _ = unit(2 * p)
                        v.wait_ge(S_["mixT_high"], PAIRS * i + (p + 1))
                        v.tensor_tensor(headsT[:, 1, h, b * SEQ:(b + 1) * SEQ], V[p % 2][:, 0:SEQ],
                                        headsT[:, 0, h, b * SEQ:(b + 1) * SEQ], ALU.subtract).then_inc(S_["mixT_low"], 1)

                    for j in range(4):
                        values_low(j)
                        if j % 2 == 1:
                            sum_squares(j // 2)
                    sum_squares(2)
                    rowsT(0)
                    sum_squares(3)
                    rowsT(1)
                    rowsT(2)
                    sum_squares(4)
                    rowsT(3)
                    sum_squares(5)
                    maximum(0)
                    invert(0)
                    rowsT(4)
                    rowsT(5)
                    for u in range(UNITS):
                        if u >= 4 and u % 2 == 0:
                            mixT_low(u // 2 - 2)
                        if u >= 1:
                            maximum(u)
                        bisection_count(k, own, u % REP)
                        if u >= 1:
                            invert(u)
                            probsT_low(u - 1)
                        if u % REP == REP - 1:
                            bisection_update(k, own)
                    probsT_low(UNITS - 1)
                    mixT_low(PAIRS - 2)
                    mixT_low(PAIRS - 1)
                    for t in range(TILES):
                        v.wait_ge(S_["out_psum"], TILES * i + (t + 1))
                        v.tensor_tensor(k.x[:, t, :], J[t % 2][:, :], k.x[:, t, :], ALU.add).then_inc(S_["out_added"], 1)
                    assert own.count == BISECT_PER_ROUND * ROUNDS, own.count
                v.wait_ge(S_["out_added"], TILES * GROUPS + 1)
                v.wait_ge(S_["bisect"], GROUPS * ROUNDS * BISECT_PER_ROUND)


def norm_tensor_two(k, n, banks, in_psum, low_ready):
    pe = k.nc.tensor
    for t in range(TILES):
        pe.wait_ge(k.xn_ready, TILES * n + t + 1)
        if t >= 2:
            pe.wait_ge(low_ready, t - 1)
        for f in range(KT):
            last = pe.transpose(banks[t % 2][:, f * P:(f + 1) * P], k.xn[:, t, f * P:(f + 1) * P], k.ident[:, :])
        last.then_inc(in_psum, 1)



TOPK = 154
BISECT_PER_ROUND = 8 + 5


def bisection_buffers(k):
    k.sign = k.sbuf("sign", [P, CTILES], F32)
    k.rank = k.sbuf("rank", [P, CTILES], F32)
    k.counts = k.sbuf("counts", [P, CTILES], F32)
    k.found = k.sbuf("found", [P, CTILES], I32)
    k.candidate = k.sbuf("candidate", [P, CTILES], I32)
    k.bit = k.sbuf("bit", [P, CTILES], I32)
    k.enough = k.sbuf("enough", [P, CTILES], F32)
    k.set_bit = k.sbuf("set_bit", [P, CTILES], I32)
    k.flags = k.sbuf("flags", [P, 2, CTX], BF16)


def row_tile(k, r):
    return k.ctxT[:, r // B, r % B * CTX:(r % B + 1) * CTX]


def bisection_start(k):
    v, own = k.nc.vector, k.vown
    for r in range(CTILES):
        if r >= 2:
            own.wait()
        own(v.tensor_scalar(k.flags[:, r % 2, :], row_tile(k, r), 0.0, 0.0, ALU.is_ge, ALU.add,
                            accum_out=k.counts[:, r:r + 1]))
    own(v.memset(k.found[:, :], 0))
    own(v.memset(k.bit[:, :], 2 ** 30))
    own(v.memset(k.candidate[:, :], 2 ** 30))
    own.wait()
    own(v.tensor_scalar(k.enough[:, :], k.counts[:, :], float(TOPK), None, ALU.is_lt))
    own.wait()
    own(v.tensor_scalar(k.sign[:, :], k.enough[:, :], -2.0, 1.0, ALU.mult, ALU.add))
    own(v.tensor_scalar(k.rank[:, :], k.enough[:, :], float(CTX + 1 - 2 * TOPK), float(TOPK), ALU.mult, ALU.add))
    own.wait()
    for r in range(CTILES):
        own(v.tensor_scalar(row_tile(k, r), row_tile(k, r), k.sign[:, r:r + 1], None, ALU.mult))
    own.wait()


def bisection_count(k, own, j):
    own.wait()
    for r in (2 * j, 2 * j + 1):
        own(k.nc.vector.tensor_scalar(k.flags[:, r % 2, :], row_tile(k, r), k.candidate[:, r:r + 1].bitcast(F32), 0.0,
                                      ALU.is_ge, ALU.add, accum_out=k.counts[:, r:r + 1]))


def bisection_update(k, own):
    v = k.nc.vector
    own.wait()
    own(v.tensor_tensor(k.enough[:, :], k.counts[:, :], k.rank[:, :], ALU.is_ge))
    own.wait()
    own(v.tensor_tensor(k.set_bit[:, :], k.enough[:, :], k.bit[:, :], ALU.mult))
    own.wait()
    own(v.tensor_tensor(k.found[:, :], k.found[:, :], k.set_bit[:, :], ALU.bitwise_or))
    own(v.tensor_scalar(k.bit[:, :], k.bit[:, :], 1, None, ALU.logical_shift_right))
    own.wait()
    own(v.tensor_tensor(k.candidate[:, :], k.found[:, :], k.bit[:, :], ALU.bitwise_or))



def layer3_attention(k, dram):
    nc, n, m = k.nc, k.norms, k.turned
    k.norms += 1
    k.turned += 1
    TAPS, BRANCHES = 7, 2
    HALF = TAPS // 2
    with ExitStack() as s:
        conv = k.sbuf("conv", [P, 2 * TAPS], F32, s)
        gamma = k.sbuf("bn_gamma", [P, 1], F32, s)
        beta = k.sbuf("bn_beta", [P, 1], F32, s)
        distance = k.sbuf("distance", [P, 3, P], F32, s)
        band = k.sbuf("band", [P, 2, 3, P], F32, s)
        term = k.sbuf("term", [P, 2, 3, P], F32, s)
        plain = k.sbuf("plain", [P, 2, CTX], F32, s)
        greater = k.sbuf("greater", [P, 2, CTX], F32, s)
        equal = k.sbuf("equal", [P, 2, SEQ], F32, s)
        prefix = k.sbuf("prefix", [P, 2, SEQ], F32, s)
        zeros = k.sbuf("zeros", [P, SEQ], F32, s)
        limit = k.sbuf("limit", [P, CTILES], F32, s)
        above = k.sbuf("above", [P, CTILES], F32, s)
        left = k.sbuf("left", [P, CTILES], F32, s)
        chosen = k.sbuf("chosen", [P, KT, B, SEQ], F32, s)
        parts = k.sbuf("parts", [P, BRANCHES, KT, B, SEQ], F32, s)
        gated = k.sbuf("gated", [P, BRANCHES, KT, B, SEQ], F32, s)
        features = k.sbuf("features", [P, 2, KT, BRANCHES, B], F32, s)
        z = k.sbuf("z", [P, KT, BRANCHES, B], F32, s)
        sq = k.sbuf("sq", [P, KT, BRANCHES, B], F32, s)
        moment = k.sbuf("moment", [P, BRANCHES], F32, s)
        rstd = k.sbuf("rstd3", [P, BRANCHES], F32, s)
        names = ("loaded", "distance_ready", "band_ready", "features_ready", "z_psum", "z_ready", "sum_psum", "sq_ready",
                 "sumsq_psum", "var_ready", "rstd_ready", "relu_ready", "exp_ready", "gated_ready", "back_psum")
        S_ = {x: k.sem(f"l3a_{x}") for x in names}
        with nc.Block(no_gpsimd_drain=True) as block:

            @block.sync
            def _(sp):
                sp.dma_start(conv[:, :], dram["L3_xattn_conv_w"].rearrange("a c t -> a (c t)").broadcast_to([P, 2 * TAPS]))\
                  .then_inc(S_["loaded"], 16)
                for target, name in ((gamma, "gamma"), (beta, "beta")):
                    sp.dma_start(target[:, :], dram["L3_xattn_bn_" + name].unsqueeze(0).broadcast_to([P, 1]))\
                      .then_inc(S_["loaded"], 16)

            @block.gpsimd
            def _(g):
                norm_gpsimd(k, n)
                g.iota(distance[:, :, :], [[P, 3], [-1, P]], base=-P, channel_multiplier=1,
                       allow_small_or_imprecise_dtypes=True).then_inc(S_["distance_ready"], 1)
                g.wait_ge(S_["distance_ready"], 1)
                g.wait_ge(S_["loaded"], 48)
                for c in range(2):
                    for tap in range(TAPS):
                        w = conv[:, c * TAPS + tap:c * TAPS + tap + 1]
                        target = band[:, c] if tap == 0 else term[:, tap % 2]
                        k.pown(g.tensor_scalar(target, distance[:, :, :], float(tap - HALF), w, ALU.is_equal, ALU.mult))
                        k.pown.wait()
                        if tap:
                            k.pown(g.tensor_tensor(band[:, c], band[:, c], target, ALU.add))
                            k.pown.wait()
                g.engine_nop().then_inc(S_["band_ready"], 1)
                g.wait_ge(S_["var_ready"], 1)
                g.tensor_tensor(rstd[:, :], moment[:, :], k.minus_half[:, 0:BRANCHES], ALU.pow).then_inc(S_["rstd_ready"], 1)

            @block.vector
            def _(v):
                norm_vector(k, n)
                own = k.vown
                own(v.memset(zeros[:, :], 0.0))
                own(v.tensor_tensor(limit[:, :], k.found[:, :].bitcast(F32), k.sign[:, :], ALU.mult))
                own.wait()
                for r in range(0, CTILES, 2):
                    two = (0, 1)
                    for j in two:
                        own(v.tensor_scalar(plain[:, j, :], row_tile(k, r + j), k.sign[:, r + j:r + j + 1], None, ALU.mult))
                    own.wait()
                    for j in two:
                        own(v.tensor_scalar(greater[:, j, :], plain[:, j, :], limit[:, r + j:r + j + 1], 0.0,
                                            ALU.is_gt, ALU.add, accum_out=above[:, r + j:r + j + 1]))
                        own(v.tensor_scalar(equal[:, j, :], plain[:, j, 0:SEQ], limit[:, r + j:r + j + 1], None, ALU.is_equal))
                    own.wait()
                    for j in two:
                        own(v.tensor_tensor_scan(prefix[:, j, :], equal[:, j, :], zeros[:, :], 0.0, ALU.add, ALU.add))
                    own(v.tensor_scalar(left[:, r:r + 2], above[:, r:r + 2], -1.0, float(TOPK), ALU.mult, ALU.add))
                    own.wait()
                    for j in two:
                        own(v.scalar_tensor_tensor(equal[:, j, :], prefix[:, j, :], left[:, r + j:r + j + 1], equal[:, j, :],
                                                   ALU.is_le, ALU.mult))
                    own.wait()
                    for j in two:
                        own(v.tensor_tensor(chosen[:, (r + j) // B, (r + j) % B, :], greater[:, j, 0:SEQ], equal[:, j, :], ALU.add))
                own.wait()
                v.wait_ge(k.xnT_ready, TILES * (m + 1))
                flat = lambda a: a.rearrange("p f b c -> p (f b c)")
                xnT = k.xnT[:, :, :].rearrange("p f c -> p (f c)")
                own(v.tensor_tensor(flat(parts[:, 0]), flat(chosen[:, :, :, :]), xnT, ALU.mult))
                own.wait()
                own(v.tensor_tensor(flat(parts[:, 1]), xnT, flat(parts[:, 0]), ALU.subtract))
                own.wait()
                for branch, count in ((0, TOPK), (1, SEQ - TOPK)):
                    own(v.tensor_reduce(features[:, 0, :, branch, :], parts[:, branch], AX.X, ALU.max))
                    own(v.tensor_reduce(features[:, 1, :, branch, :], parts[:, branch], AX.X, ALU.add))
                    own.wait()
                    own(v.tensor_scalar(features[:, 1, :, branch, :], features[:, 1, :, branch, :], 1.0 / SEQ, SEQ / count,
                                        ALU.mult, ALU.mult))
                own.wait()
                v.engine_nop().then_inc(S_["features_ready"], 1)
                v.wait_ge(S_["z_psum"], 1)
                spread = lambda a: a.unsqueeze(1).unsqueeze(3).broadcast_to([P, KT, BRANCHES, B])
                v.tensor_copy(z[:, :, :, :].rearrange("p f r b -> p (f r b)"), k.bank[2][:, 0:16]).then_inc(S_["z_ready"], 1)
                v.wait_ge(S_["z_ready"], 1)
                v.wait_ge(S_["sum_psum"], 1)
                own(v.tensor_reduce(moment[:, :], k.bank[3][:, 0:16].rearrange("p (f r b) -> p r f b", f=KT, r=BRANCHES),
                                    AX.XY, ALU.add))
                own.wait()
                own(v.tensor_scalar(moment[:, :], moment[:, :], 1.0 / (B * D), None, ALU.mult))
                own.wait()
                own(v.tensor_tensor(z[:, :, :, :], z[:, :, :, :], spread(moment[:, :]), ALU.subtract))
                own.wait()
                v.tensor_tensor(sq[:, :, :, :], z[:, :, :, :], z[:, :, :, :], ALU.mult).then_inc(S_["sq_ready"], 1)
                v.wait_ge(S_["sumsq_psum"], 1)
                own(v.tensor_reduce(moment[:, :], k.bank[4][:, 0:16].rearrange("p (f r b) -> p r f b", f=KT, r=BRANCHES),
                                    AX.XY, ALU.add))
                own.wait()
                v.tensor_scalar(moment[:, :], moment[:, :], 1.0 / (B * D), EPS, ALU.mult, ALU.add).then_inc(S_["var_ready"], 1)
                v.wait_ge(S_["rstd_ready"], 1)
                own(v.tensor_tensor(z[:, :, :, :], z[:, :, :, :], spread(rstd[:, :]), ALU.mult))
                own.wait()
                v.wait_ge(S_["loaded"], 48)
                own(v.tensor_scalar(z[:, :, :, :], z[:, :, :, :], gamma[:, 0:1], beta[:, 0:1], ALU.mult, ALU.add))
                own.wait()
                v.tensor_scalar(z[:, :, :, :], z[:, :, :, :], 0.0, None, ALU.max).then_inc(S_["relu_ready"], 1)
                v.wait_ge(S_["exp_ready"], 1)
                own(v.tensor_scalar(sq[:, :, :, :], sq[:, :, :, :], 1.0, None, ALU.add))
                own.wait()
                own(v.reciprocal(z[:, :, :, :], sq[:, :, :, :]))
                own.wait()
                for branch in range(BRANCHES):
                    own(v.tensor_tensor(gated[:, branch], parts[:, branch],
                                        z[:, :, branch, :].unsqueeze(3).broadcast_to([P, KT, B, SEQ]), ALU.mult))
                own.wait()
                v.tensor_tensor(flat(gated[:, 0]), flat(gated[:, 0]), flat(gated[:, 1]), ALU.add).then_inc(S_["gated_ready"], 1)
                for t in range(TILES):
                    v.wait_ge(S_["back_psum"], t + 1)
                    own(v.tensor_tensor(k.x[:, t, :], k.bank[4 + t][:, :], k.x[:, t, :], ALU.add))
                own.wait()

            @block.scalar
            def _(a):
                norm_scalar(k, m, k.bank[0:2])
                a.wait_ge(S_["relu_ready"], 1)
                a.activation(sq[:, :, :, :], z[:, :, :, :], ACT.Exp, scale=-1.0).then_inc(S_["exp_ready"], 1)

            @block.tensor
            def _(pe):
                norm_tensor(k, n, m, k.bank[0:2])
                pe.wait_ge(S_["band_ready"], 1)
                pe.wait_ge(S_["features_ready"], 1)
                for f in range(KT):
                    terms = [(c, blk) for c in range(2) for blk in range(3) if 0 <= f + blk - 1 < KT]
                    for j, (c, blk) in enumerate(terms):
                        last = pe.matmul(k.bank[2][:, f * 4:f * 4 + 4], band[:, c, blk, :],
                                         features[:, c, f + blk - 1].rearrange("p r b -> p (r b)"),
                                         start=j == 0, stop=j == len(terms) - 1)
                last.then_inc(S_["z_psum"], 1)
                for source, ready, bank, done in ((z, "z_ready", 3, "sum_psum"), (sq, "sq_ready", 4, "sumsq_psum")):
                    pe.wait_ge(S_[ready], 1)
                    pe.matmul(k.bank[bank][:, 0:16], k.ones[:, :], source[:, :, :, :].rearrange("p f r b -> p (f r b)"),
                              start=True, stop=True).then_inc(S_[done], 1)
                pe.wait_ge(S_["gated_ready"], 1)
                for t in range(TILES):
                    for f in range(KT):
                        last = pe.transpose(k.bank[4 + t][:, f * P:(f + 1) * P],
                                            gated[:, 0, f, t // TPB, t % TPB * P:(t % TPB + 1) * P], k.ident[:, :])
                    last.then_inc(S_["back_psum"], 1)



def layer2_ffn(k, dram):
    nc, n, m = k.nc, k.norms, k.turned
    k.norms += 1
    k.turned += 1
    E, TOP = 64, 8
    with ExitStack() as s:
        router = k.sbuf("router", [P, KT, E], F32, s)
        rbias = k.sbuf("rbias", [P, E], F32, s)
        ebias = k.sbuf("ebias", [E, D], F32, s)
        logits = k.sbuf("logits", [P, TILES, E], F32, s)
        shifted = k.sbuf("shifted", [P, TILES, E], F32, s)
        expd = k.sbuf("expd", [P, TILES, E], F32, s)
        top = k.sbuf("top", [P, TILES], F32, s)
        total = k.sbuf("total", [P, TILES], F32, s)
        scores = k.sbuf("scores", [P, TILES, E], F32, s)
        rest = k.sbuf("rest", [P, TILES, E], F32, s)
        best = k.sbuf("best", [P, TILES, TOP], F32, s)
        wsum = k.sbuf("wsum", [P, TILES], F32, s)
        dense = k.sbuf("dense", [P, TILES, E], F32, s)
        denseT = k.sbuf("denseT", [E, TILES * P], F32, s)
        loaded, logits_psum, shifted_ready, expd_ready, dense_ready, denseT_psum, denseT_ready, mix_psum = (
            k.sem(f"l2f_{x}") for x in ("loaded", "logits_psum", "shifted_ready", "expd_ready", "dense_ready",
                                        "denseT_psum", "denseT_ready", "mix_psum"))
        with nc.Block(no_gpsimd_drain=True) as block:

            @block.sync
            def _(sp):
                sp.dma_start(router[:, :, :], dram["routerT"].rearrange("(f p) e -> p f e", p=P)).then_inc(loaded, 16)
                sp.dma_start(rbias[:, :], dram["L2_ffn_router_bias"].unsqueeze(0).broadcast_to([P, E])).then_inc(loaded, 16)
                sp.dma_start(ebias[:, :], dram["L2_ffn_expert_bias"]).then_inc(loaded, 16)

            @block.gpsimd
            def _(g):
                norm_gpsimd(k, n)

            @block.tensor
            def _(pe):
                norm_tensor(k, n, m, k.bank[0:2])
                pe.wait_ge(loaded, 48)
                for t in range(TILES):
                    pe.wait_ge(k.xnT_ready, TILES * m + t + 1)
                    for f in range(KT):
                        last = pe.matmul(k.bank[2][:, t * E:(t + 1) * E], k.xnT[:, f, t * P:(t + 1) * P],
                                         router[:, f, :], start=f == 0, stop=f == KT - 1)
                last.then_inc(logits_psum, 1)
                pe.wait_ge(dense_ready, 1)
                for t in range(TILES):
                    last = pe.transpose(k.bank[3][0:E, t * P:(t + 1) * P], dense[:, t, :], k.ident[:, :])
                last.then_inc(denseT_psum, 1)
                pe.wait_ge(denseT_ready, 1)
                for t in range(TILES):
                    pe.matmul(k.bank[4 + t][:, :], denseT[:, t * P:(t + 1) * P], ebias[:, :],
                              start=True, stop=True).then_inc(mix_psum, 1)

            @block.vector
            def _(v):
                norm_vector(k, n)
                spread = lambda a: a[:, :].unsqueeze(2).broadcast_to([P, TILES, E])
                v.wait_ge(loaded, 48)
                v.wait_ge(logits_psum, 1)
                k.vown(v.tensor_tensor(logits[:, :, :], k.bank[2][:, 0:TILES * E].rearrange("p (t e) -> p t e", e=E),
                                       rbias[:, :].unsqueeze(1).broadcast_to([P, TILES, E]), ALU.add))
                k.vown.wait()
                k.vown(v.tensor_reduce(top[:, :], logits[:, :, :], AX.X, ALU.max))
                k.vown.wait()
                v.tensor_tensor(shifted[:, :, :], logits[:, :, :], spread(top), ALU.subtract).then_inc(shifted_ready, 1)
                v.wait_ge(expd_ready, 1)
                k.vown(v.tensor_reduce(total[:, :], expd[:, :, :], AX.X, ALU.add))
                k.vown.wait()
                k.vown(v.reciprocal(total[:, :], total[:, :]))
                k.vown.wait()
                k.vown(v.tensor_tensor(scores[:, :, :], expd[:, :, :], spread(total), ALU.mult))
                k.vown.wait()
                for t in range(TILES):
                    k.vown(v.max(best[:, t, :], scores[:, t, :]))
                k.vown.wait()
                for t in range(TILES):
                    k.vown(v.match_replace(rest[:, t, :], best[:, t, :], scores[:, t, :], 0.0))
                k.vown(v.tensor_reduce(wsum[:, :], best[:, :, :], AX.X, ALU.add))
                k.vown.wait()
                v.tensor_tensor(dense[:, :, :], scores[:, :, :], rest[:, :, :], ALU.subtract).then_inc(dense_ready, 1)
                for t in range(TILES):
                    k.vown(v.scalar_tensor_tensor(k.x[:, t, :], k.xn[:, t, :], wsum[:, t:t + 1], k.x[:, t, :],
                                                  ALU.mult, ALU.add))
                k.vown.wait()
                for t in range(TILES):
                    v.wait_ge(mix_psum, t + 1)
                    k.vown(v.tensor_tensor(k.x[:, t, :], k.bank[4 + t][:, :], k.x[:, t, :], ALU.add))
                k.vown.wait()

            @block.scalar
            def _(a):
                norm_scalar(k, m, k.bank[0:2])
                a.wait_ge(shifted_ready, 1)
                a.activation(expd[:, :, :], shifted[:, :, :], ACT.Exp).then_inc(expd_ready, 1)
                a.wait_ge(denseT_psum, 1)
                a.copy(denseT[:, :], k.bank[3][0:E, :]).then_inc(denseT_ready, 1)



def layer3_ffn(k, dram):
    nc, n, m = k.nc, k.norms, k.turned
    k.norms += 1
    k.turned += 1
    E, R, TOP = 8, 16, 2
    SCALING = 2.0
    with ExitStack() as s:
        wb = k.sbuf("wb", [P, KT, D], F32, s)
        wra = k.sbuf("wra", [P, KT, E + E * R], F32, s)
        bm = k.sbuf("bm", [E * R, D], F32, s)
        bias = k.sbuf("bias3", [P, D], F32, s)
        lower = k.sbuf("lower", [P, E, E], F32, s)
        logits = k.sbuf("logits3", [P, TILES, E], F32, s)
        expd = k.sbuf("expd3", [P, TILES, E], F32, s)
        top = k.sbuf("top3", [P, TILES], F32, s)
        total = k.sbuf("total3", [P, TILES], F32, s)
        probs = k.sbuf("probs3", [P, TILES, E], F32, s)
        more = k.sbuf("more", [P, TILES, E, E], F32, s)
        same = k.sbuf("same", [P, TILES, E, E], F32, s)
        rank = k.sbuf("rank", [P, TILES, E], F32, s)
        weight = k.sbuf("weight3", [P, TILES, E], F32, s)
        low = k.sbuf("low", [P, TILES, E * R], F32, s)
        lowT = k.sbuf("lowT", [E * R, TILES * P], F32, s)
        loaded, lower_zeroed, lower_ready, low_psum, shifted_ready, expd_ready, low_ready, lowT_psum, lowT_ready, \
            out_psum = (k.sem(f"l3f_{x}") for x in (
                "loaded", "lower_zeroed", "lower_ready", "low_psum", "shifted_ready", "expd_ready", "low_ready",
                "lowT_psum", "lowT_ready", "out_psum"))
        with nc.Block(no_gpsimd_drain=True) as block:

            @block.sync
            def _(sp):
                sp.dma_start(bias[:, :], dram["L3_ffn_bias"].unsqueeze(0).broadcast_to([P, D])).then_inc(loaded, 16)
                sp.dma_start(wra[:, :, :], dram["wraT"].rearrange("(f p) c -> p f c", p=P)).then_inc(loaded, 16)
                sp.dma_start(wb[:, :, :], dram["wbT"].rearrange("(f p) c -> p f c", p=P)).then_inc(loaded, 16)
                sp.dma_start(bm[:, :], dram["bmT"]).then_inc(loaded, 16)

            @block.gpsimd
            def _(g):
                norm_gpsimd(k, n)
                g.memset(lower[:, :, :], 1.0).then_inc(lower_zeroed, 1)
                g.wait_ge(lower_zeroed, 1)
                g.affine_select(out=lower[:, :, :], in_=lower[:, :, :], compare_op=ALU.is_gt, fill=0.0, base=0,
                                pattern=[[1, E], [-1, E]], channel_multiplier=0).then_inc(lower_ready, 1)

            @block.tensor
            def _(pe):
                norm_tensor(k, n, m, k.bank[0:2])
                pe.wait_ge(loaded, 64)
                for t in range(TILES):
                    pe.wait_ge(k.xnT_ready, TILES * m + t + 1)
                    for f in range(KT):
                        last = pe.matmul(k.bank[2 + t // 2][:, t % 2 * 256:t % 2 * 256 + E + E * R],
                                         k.xnT[:, f, t * P:(t + 1) * P], wra[:, f, :], start=f == 0, stop=f == KT - 1)
                last.then_inc(low_psum, 1)
                for t in range(TILES):
                    for f in range(KT):
                        pe.matmul(k.bank[4 + t][:, :], k.xnT[:, f, t * P:(t + 1) * P], wb[:, f, :],
                                  start=f == 0, stop=False)
                for t in range(TILES):
                    pe.wait_ge(low_ready, t + 1)
                    last = pe.transpose(k.bank[0][:, t * P:(t + 1) * P], low[:, t, :], k.ident[:, :])
                last.then_inc(lowT_psum, 1)
                pe.wait_ge(lowT_ready, 1)
                for t in range(TILES):
                    pe.matmul(k.bank[4 + t][:, :], lowT[:, t * P:(t + 1) * P], bm[:, :],
                              start=False, stop=True).then_inc(out_psum, 1)

            @block.vector
            def _(v):
                norm_vector(k, n)
                v.wait_ge(loaded, 64)
                v.wait_ge(k.xn_ready, TILES * (n + 1))
                for t in range(TILES):
                    k.vown(v.tensor_tensor(k.x[:, t, :], k.x[:, t, :], bias[:, :], ALU.add))
                v.wait_ge(low_psum, 1)
                for h in range(2):
                    k.vown(v.tensor_copy(logits[:, 2 * h:2 * h + 2, :],
                                         k.bank[2 + h][:, :].rearrange("p (t c) -> p t c", t=2)[:, :, 0:E]))
                k.vown.wait()
                spread = lambda a: a[:, :].unsqueeze(2).broadcast_to([P, TILES, E])
                k.vown(v.tensor_reduce(top[:, :], logits[:, :, :], AX.X, ALU.max))
                k.vown.wait()
                v.tensor_tensor(logits[:, :, :], logits[:, :, :], spread(top), ALU.subtract).then_inc(shifted_ready, 1)
                v.wait_ge(expd_ready, 1)
                k.vown(v.tensor_reduce(total[:, :], expd[:, :, :], AX.X, ALU.add))
                k.vown.wait()
                k.vown(v.reciprocal(total[:, :], total[:, :]))
                k.vown.wait()
                k.vown(v.tensor_tensor(probs[:, :, :], expd[:, :, :], spread(total), ALU.mult))
                k.vown.wait()
                of_f = probs[:, :, :].unsqueeze(2).broadcast_to([P, TILES, E, E])
                of_e = probs[:, :, :].unsqueeze(3).broadcast_to([P, TILES, E, E])
                k.vown(v.tensor_tensor(more[:, :, :, :], of_f, of_e, ALU.is_gt))
                k.vown(v.tensor_tensor(same[:, :, :, :], of_f, of_e, ALU.is_equal))
                k.vown.wait()
                v.wait_ge(lower_ready, 1)
                k.vown(v.tensor_tensor(same[:, :, :, :], same[:, :, :, :],
                                       lower[:, :, :].unsqueeze(1).broadcast_to([P, TILES, E, E]), ALU.mult))
                k.vown.wait()
                k.vown(v.tensor_tensor(more[:, :, :, :], more[:, :, :, :], same[:, :, :, :], ALU.add))
                k.vown.wait()
                k.vown(v.tensor_reduce(rank[:, :, :], more[:, :, :, :], AX.X, ALU.add))
                k.vown.wait()
                k.vown(v.scalar_tensor_tensor(weight[:, :, :], rank[:, :, :], float(TOP), probs[:, :, :],
                                              ALU.is_lt, ALU.mult))
                k.vown.wait()
                k.vown(v.tensor_reduce(total[:, :], weight[:, :, :], AX.X, ALU.add))
                k.vown.wait()
                k.vown(v.reciprocal(total[:, :], total[:, :]))
                k.vown.wait()
                k.vown(v.scalar_tensor_tensor(weight[:, :, :], weight[:, :, :], SCALING, spread(total), ALU.mult, ALU.mult))
                k.vown.wait()
                for t in range(TILES):
                    h = k.bank[2 + t // 2][:, t % 2 * 256 + E:t % 2 * 256 + E + E * R]
                    v.tensor_tensor(low[:, t, :].rearrange("p (e r) -> p e r", r=R), h.rearrange("p (e r) -> p e r", r=R),
                                    weight[:, t, :].unsqueeze(2).broadcast_to([P, E, R]), ALU.mult)\
                     .then_inc(low_ready, 1)
                for t in range(TILES):
                    v.wait_ge(out_psum, t + 1)
                    k.vown(v.tensor_tensor(k.x[:, t, :], k.bank[4 + t][:, :], k.x[:, t, :], ALU.add))
                k.vown.wait()

            @block.scalar
            def _(a):
                norm_scalar(k, m, k.bank[0:2])
                a.wait_ge(shifted_ready, 1)
                a.activation(expd[:, :, :], logits[:, :, :], ACT.Exp).then_inc(expd_ready, 1)
                a.wait_ge(lowT_psum, 1)
                a.copy(lowT[:, :], k.bank[0][:, :]).then_inc(lowT_ready, 1)


def epilogue(k, out):
    nc = k.nc
    stored = k.sem("stored")
    with nc.Block(no_gpsimd_drain=True) as block:

        @block.sync
        def _(sp):
            sp.dma_start(out.rearrange("b (t p) d -> p (b t) d", p=P), k.x[:, :, :]).then_inc(stored, 16)
            sp.wait_ge(stored, 16)


LAYERS = [layer0_attention, layer0_ffn, layer1_attention, layer1_ffn, layer2_attention, layer2_ffn, layer3_attention, layer3_ffn]


def build(nc, dram, out, first=0, layers=len(LAYERS)):
    with ExitStack() as stack:
        k = Core(nc, stack)
        prologue(k, dram)
        for layer in LAYERS[first:layers]:
            k.label = layer.__name__ + "_"
            layer(k, dram)
        epilogue(k, out)


def layout(inputs):
    a = {n: np.ascontiguousarray(v) for n, v in inputs.items()}
    ctx = a.pop("ctx_4096")
    a["ctx"] = ctx
    a["ctxT"] = np.ascontiguousarray(ctx.reshape(B * CTX, D).T)
    a["wkv4"] = np.ascontiguousarray(np.tile(a.pop("L1_xattn_Wkv_d"), (1, 4)))
    for name, source in (("w_gateT", "L1_ffn_w_gate"), ("w_upT", "L1_ffn_w_up"), ("w_downT", "L1_ffn_w_down"),
                         ("routerT", "L2_ffn_router_weight"), ("wbT", "L3_ffn_Wb")):
        a[name] = np.ascontiguousarray(a.pop(source).T)
    G, H = 8, 128
    wkv = np.stack([a.pop("L2_xattn_k_proj_w").reshape(G, H, D), a.pop("L2_xattn_v_proj_w").reshape(G, H, D)], axis=1)
    wkv = wkv.reshape(G, 2 * H, D)
    a["wkvT"] = np.ascontiguousarray(np.concatenate([wkv, wkv[:1]]).reshape(-1, D).T)
    wq = a.pop("L2_xattn_q_proj_w").reshape(G, -1, D)
    a["wqT"] = np.ascontiguousarray(np.concatenate([wq, wq[:1]]).reshape(-1, D).T)
    a["woT"] = np.ascontiguousarray(a.pop("L2_xattn_o_proj_w").T)
    low = a.pop("L3_ffn_A")
    a["wraT"] = np.ascontiguousarray(np.concatenate([a.pop("L3_ffn_Wr").T, low.reshape(-1, D).T], axis=1))
    a["bmT"] = np.ascontiguousarray(a.pop("L3_ffn_Bm").transpose(0, 2, 1).reshape(-1, D))
    return a


def kernel(**inputs):
    import numpy as _np
    import concourse.bacc as _bacc
    from concourse import mybir as _mybir
    from concourse.bass_utils import run_bass_kernel_spmd as _run

    nc = _bacc.Bacc("TRN2", target_bir_lowering=False, num_devices=1)
    arrays, dram = {}, {}
    for name, a in layout({n: _np.asarray(v) for n, v in inputs.items()}).items():
        arrays[f"in_{name}"] = a
        dram[name] = nc.dram_tensor(f"in_{name}", a.shape, _mybir.dt.from_np(a.dtype), kind="ExternalInput").ap()
    out = nc.dram_tensor("out_0_dram", (B, SEQ, D), _mybir.dt.float32, kind="ExternalOutput").ap()
    build(nc, dram, out)
    return _run(nc, [arrays], core_ids=[0]).results[0]["out_0_dram"]
```

```python
from contextlib import ExitStack

import numpy as np

import concourse.bass as bass
from concourse import mybir

F32, BF16, I32, F32R = mybir.dt.float32, mybir.dt.bfloat16, mybir.dt.int32, mybir.dt.float32r
ALU = mybir.AluOpType
ACT = mybir.ActivationFunctionType
AX = mybir.AxisListType

P = 128
B, SEQ, D = 2, 256, 512
CTX = 512
TILES = B * SEQ // P
TPB = SEQ // P
KT = D // P
CTILES = B * CTX // P
CPB = CTX // P
EPS = 1e-5
ROUND = 1.5 * 2.0 ** 23
BANKS = 8


class Own:

    def __init__(self, engine, semaphore):
        self.engine, self.semaphore, self.count = engine, semaphore, 0

    def __call__(self, instruction):
        instruction.then_inc(self.semaphore, 1)
        self.count += 1

    def wait(self):
        self.engine.wait_ge(self.semaphore, self.count)


class Core:

    def __init__(self, nc, stack):
        self.nc, self.stack, self.norms, self.turned, self.label = nc, stack, 0, 0, ""
        sb = self.sbuf
        self.x = sb("x", [P, TILES, D], F32)
        self.xn = sb("xn", [P, TILES, D], F32)
        self.xnT = sb("xnT", [P, KT, TILES * P], F32)
        self.ctxT = sb("ctxT", [P, KT, B * CTX], F32)
        self.ident = sb("ident", [P, P], F32)
        self.ident16 = sb("ident16", [P, P], BF16)
        self.ones = sb("ones", [P, P], F32)
        self.ones16 = sb("ones16", [P, 1], BF16)
        self.minus_half = sb("minus_half", [P, 8], F32)
        self.stats = sb("stats", [P, TILES, 6], F32)
        self.meanvar = sb("meanvar", [P, TILES, 2], F32)
        self.varep = sb("varep", [P, TILES], F32)
        self.rstd = sb("rstd", [P, TILES], F32)
        bisection_buffers(self)
        self.bank = [stack.enter_context(nc.psum_tensor(f"bank{i}", [P, 512], F32)) for i in range(BANKS)]
        self.vown = Own(nc.vector, self.sem("vector_own"))
        self.pown = Own(nc.gpsimd, self.sem("gpsimd_own"))
        self.aown = Own(nc.scalar, self.sem("scalar_own"))
        self.variance_ready = self.sem("variance_ready")
        self.rstd_ready = self.sem("rstd_ready")
        self.xn_ready = self.sem("xn_ready")
        self.xnT_in_psum = self.sem("xnT_in_psum")
        self.xnT_ready = self.sem("xnT_ready")
        self.x_loaded = self.sem("x_loaded")
        self.ctxT_loaded = self.sem("ctxT_loaded")

    def sbuf(self, name, shape, dtype, stack=None):
        return (stack or self.stack).enter_context(self.nc.sbuf_tensor(self.label + name, shape, dtype))

    def sem(self, name):
        return self.stack.enter_context(self.nc.semaphore(name))


def at(step, per, c):
    i, offset = step
    return per * offset + c if i is None else i * (2 * per) + (per * offset + c)


def after(step, steps=1):
    return step[0], step[1] + steps


def is_start(step):
    return step[0] is None and step[1] == 0


class StepOwn:

    def __init__(self, engine, semaphore, step, per):
        self.engine, self.semaphore, self.step, self.per, self.count = engine, semaphore, step, per, 0

    def __call__(self, instruction):
        instruction.then_inc(self.semaphore, 1)
        self.count += 1

    def wait(self):
        self.engine.wait_ge(self.semaphore, at(self.step, self.per, self.count))



def norm_vector(k, n):
    v = k.nc.vector
    for t in range(TILES):
        k.vown(v.bn_stats(k.stats[:, t, :], k.x[:, t, :]))
    k.vown.wait()
    for t in range(TILES):
        k.vown(v.bn_aggr(k.meanvar[:, t, :], k.stats[:, t, :]))
    k.vown.wait()
    v.tensor_scalar(k.varep[:, :], k.meanvar[:, :, 1], EPS, None, ALU.add).then_inc(k.variance_ready, 1)
    v.wait_ge(k.rstd_ready, n + 1)
    for t in range(TILES):
        v.tensor_scalar(k.xn[:, t, :], k.x[:, t, :], k.meanvar[:, t, 0:1], k.rstd[:, t:t + 1],
                        ALU.subtract, ALU.mult).then_inc(k.xn_ready, 1)


def norm_gpsimd(k, n):
    g = k.nc.gpsimd
    g.wait_ge(k.variance_ready, n + 1)
    g.tensor_tensor(k.rstd[:, :], k.varep[:, :], k.minus_half[:, 0:TILES], ALU.pow).then_inc(k.rstd_ready, 1)


def norm_tensor(k, n, m, banks):
    pe = k.nc.tensor
    for t in range(TILES):
        pe.wait_ge(k.xn_ready, TILES * n + t + 1)
        if t >= 2:
            pe.wait_ge(k.xnT_ready, TILES * m + t - 1)
        for f in range(KT):
            last = pe.transpose(banks[t % 2][:, f * P:(f + 1) * P], k.xn[:, t, f * P:(f + 1) * P], k.ident[:, :])
        last.then_inc(k.xnT_in_psum, 1)


def norm_scalar(k, m, banks):
    a = k.nc.scalar
    for t in range(TILES):
        a.wait_ge(k.xnT_in_psum, TILES * m + t + 1)
        a.copy(k.xnT[:, :, t * P:(t + 1) * P],
               banks[t % 2][:, :].rearrange("p (f c) -> p f c", f=KT)).then_inc(k.xnT_ready, 1)



def prologue(k, dram):
    nc = k.nc
    identity_zeroed = k.sem("identity_zeroed")
    with nc.Block(no_gpsimd_drain=True) as block:

        @block.sync
        def _(sp):
            sp.dma_start(k.x[:, :, :], dram["x"].rearrange("b (t p) d -> p (b t) d", p=P)).then_inc(k.x_loaded, 16)
            sp.dma_start(k.ctxT[:, :, :], dram["ctxT"].rearrange("(f p) r -> p f r", p=P)).then_inc(k.ctxT_loaded, 16)
            sp.wait_ge(k.x_loaded, 16)

        @block.gpsimd
        def _(g):
            g.memset(k.ident[:, :], 0.0).then_inc(identity_zeroed, 1)
            g.memset(k.ident16[:, :], 0.0).then_inc(identity_zeroed, 1)
            k.pown(g.memset(k.ones[:, :], 1.0))
            k.pown(g.memset(k.ones16[:, :], 1.0))
            k.pown(g.memset(k.minus_half[:, :], -0.5))
            g.wait_ge(identity_zeroed, 2)
            for m in (k.ident, k.ident16):
                k.pown(g.affine_select(out=m[:, :], in_=m[:, :], compare_op=ALU.not_equal, fill=1.0,
                                       base=0, pattern=[[-1, P]], channel_multiplier=1))
            k.pown.wait()



def layer0_attention(k, dram):
    nc, n = k.nc, k.norms
    k.norms += 1
    MIDDLE = 128.0
    with ExitStack() as s:
        ctx = k.sbuf("ctx", [P, CTILES, D], F32, s)
        q2 = k.sbuf("q2", [P, CTILES, D], BF16, s)
        q1 = k.sbuf("q1", [P, TILES, D], BF16, s)
        q1T = k.sbuf("q1T", [P, KT, TILES * P], BF16, s)
        t1 = k.sbuf("t1", [P, 2, D], F32, s)
        t2 = k.sbuf("t2", [P, 2, D], F32, s)
        par = k.sbuf("par", [P, 4], F32, s)
        inv = k.sbuf("inv", [P, 2], F32, s)
        off = k.sbuf("off", [P, 2], F32, s)
        s12 = k.sbuf("s12", [P, 1], F32, s)
        kd1 = k.sbuf("kd1", [P, 1], F32, s)
        d2s = k.sbuf("d2s", [P, 1], F32, s)
        rows = k.sbuf("rows", [P, TILES], F32, s)
        corr = k.sbuf("corr", [P, TILES], F32, s)
        cols = k.sbuf("cols", [1, B, D], F32, s)
        par_loaded, ctx_loaded = k.sem("par_loaded"), k.sem("ctx_loaded")
        q2_ready, q1_ready, q1T_psum, q1T_ready = (k.sem(f"l0a_{x}") for x in
                                                   ("q2_ready", "q1_ready", "q1T_psum", "q1T_ready"))
        cols_psum, cols_ready, product_psum = (k.sem(f"l0a_{x}") for x in
                                               ("cols_psum", "cols_ready", "product_psum"))
        with nc.Block(no_gpsimd_drain=True) as block:

            @block.sync
            def _(sp):
                for i, name in enumerate(("L0_xattn_x1_scale", "L0_xattn_x1_zp", "L0_xattn_x2_scale", "L0_xattn_x2_zp")):
                    sp.dma_start(par[:, i:i + 1], dram[name].unsqueeze(0).broadcast_to([P, 1])).then_inc(par_loaded, 16)
                for b in range(B):
                    sp.dma_start(ctx[:, b * CPB:(b + 1) * CPB, :],
                                 dram["ctx"][b].rearrange("(t p) d -> p t d", p=P)).then_inc(ctx_loaded, 16)

            @block.gpsimd
            def _(g):
                norm_gpsimd(k, n)

            @block.vector
            def _(v):
                norm_vector(k, n)
                v.wait_ge(par_loaded, 64)
                for i in range(2):
                    k.vown(v.reciprocal(inv[:, i:i + 1], par[:, 2 * i:2 * i + 1]))
                    k.vown(v.tensor_scalar(off[:, i:i + 1], par[:, 2 * i + 1:2 * i + 2], -1.0, MIDDLE, ALU.mult, ALU.add))
                k.vown(v.tensor_tensor(s12[:, :], par[:, 0:1], par[:, 2:3], ALU.mult))
                k.vown.wait()
                k.vown(v.tensor_scalar(kd1[:, :], off[:, 0:1], float(CTX), None, ALU.mult))
                k.vown(v.tensor_tensor(d2s[:, :], off[:, 1:2], s12[:, :], ALU.mult))

                def quantise(source, target, i, ready):
                    for j in range(2):
                        k.vown(v.tensor_scalar(t1[:, j, :], source(j), inv[:, i:i + 1], par[:, 2 * i + 1:2 * i + 2],
                                               ALU.mult, ALU.add))
                    k.vown.wait()
                    for j in range(2):
                        k.vown(v.tensor_scalar(t2[:, j, :], t1[:, j, :], 0.0, 255.0, ALU.max, ALU.min))
                    k.vown.wait()
                    for j in range(2):
                        v.tensor_scalar(target(j), t2[:, j, :], ROUND, ROUND + MIDDLE, ALU.add,
                                        ALU.subtract).then_inc(ready, 1)

                v.wait_ge(k.xn_ready, TILES * n + TILES)
                for t in range(0, TILES, 2):
                    quantise(lambda j: k.xn[:, t + j, :], lambda j: q1[:, t + j, :], 0, q1_ready)
                v.wait_ge(q1_ready, TILES)
                for t in range(TILES):
                    k.vown(v.tensor_reduce(rows[:, t:t + 1], q1[:, t, :], AX.X, ALU.add))
                v.wait_ge(ctx_loaded, 16 * B)
                for t in range(0, CTILES, 2):
                    quantise(lambda j: ctx[:, t + j, :], lambda j: q2[:, t + j, :], 1, q2_ready)
                k.vown.wait()
                k.vown(v.tensor_scalar(corr[:, :], rows[:, :], kd1[:, 0:1], d2s[:, 0:1], ALU.add, ALU.mult))
                k.vown.wait()
                for t in range(TILES):
                    k.vown(v.tensor_scalar(k.x[:, t, :], k.x[:, t, :], corr[:, t:t + 1], None, ALU.add))
                for b in range(B):
                    v.wait_ge(cols_psum, b + 1)
                    v.tensor_scalar(cols[:, b, :], k.bank[2 + b][0:1, :], off[0:1, 0:1], None,
                                    ALU.mult).then_inc(cols_ready, 1)
                k.vown.wait()
                for t in range(TILES):
                    v.wait_ge(product_psum, t + 1)
                    k.vown(v.scalar_tensor_tensor(k.x[:, t, :], k.bank[4 + t][:, :], s12[:, 0:1], k.x[:, t, :],
                                                  ALU.mult, ALU.add))
                k.vown.wait()

            @block.tensor
            def _(pe):
                for t in range(TILES):
                    pe.wait_ge(q1_ready, t + 1)
                    if t >= 2:
                        pe.wait_ge(q1T_ready, t - 1)
                    for f in range(KT):
                        last = pe.transpose(k.bank[t % 2][:, 0:256].bitcast(BF16)[:, f * P:(f + 1) * P],
                                            q1[:, t, f * P:(f + 1) * P], k.ident16[:, :])
                    last.then_inc(q1T_psum, 1)
                for b in range(B):
                    pe.wait_ge(q2_ready, CPB * (b + 1))
                    for f in range(CPB):
                        last = pe.matmul(k.bank[2 + b][0:1, :], k.ones16[:, :], q2[:, b * CPB + f, :],
                                         start=f == 0, stop=f == CPB - 1)
                    last.then_inc(cols_psum, 1)
                pe.wait_ge(q1T_ready, TILES)
                for t in range(TILES):
                    b = t // TPB
                    for f in range(CPB):
                        pe.matmul(k.bank[4 + t][:, :], q1T[:, f, t * P:(t + 1) * P], q2[:, b * CPB + f, :],
                                  start=f == 0, stop=False)
                    pe.wait_ge(cols_ready, b + 1)
                    pe.matmul(k.bank[4 + t][:, :], k.ones[0:1, :], cols[:, b, :],
                              start=False, stop=True).then_inc(product_psum, 1)

            @block.scalar
            def _(a):
                for t in range(TILES):
                    a.wait_ge(q1T_psum, t + 1)
                    a.copy(q1T[:, :, t * P:(t + 1) * P],
                           k.bank[t % 2][:, 0:256].bitcast(BF16).rearrange("p (f c) -> p f c", f=KT))\
                     .then_inc(q1T_ready, 1)



def layer0_ffn(k, dram):
    nc, n, m = k.nc, k.norms, k.turned
    k.norms += 1
    k.turned += 1
    PLANES, BITS = 4, 32
    WORDS = D // BITS
    CODES = 2 ** PLANES
    OT = D // P
    with ExitStack() as s:
        planes = k.sbuf("planes", [P, OT, PLANES * WORDS], I32, s)
        shifts = k.sbuf("shifts", [P, BITS], I32, s)
        moved = k.sbuf("moved", [P, PLANES * WORDS, BITS], I32, s)
        bits = k.sbuf("bits", [P, 2, PLANES, D], I32, s)
        lut = k.sbuf("lut", [P, OT, CODES], F32, s)
        diff = k.sbuf("diff", [P, OT, CODES // 2], F32, s)
        tree = k.sbuf("tree", [P, 2, CODES // 2, D], F32, s)
        weightT = k.sbuf("weightT", [P, KT, D], F32, s)
        bias = k.sbuf("bias", [P, D], F32, s)
        loaded, bias_loaded, shifts_ready, diff_ready, bits_ready, leaves_ready, weight_ready, weightT_psum, \
            weightT_ready, product_psum = (k.sem(f"l0f_{x}") for x in (
                "loaded", "bias_loaded", "shifts_ready", "diff_ready", "bits_ready", "leaves_ready", "weight_ready",
                "weightT_psum", "weightT_ready", "product_psum"))
        with nc.Block(no_gpsimd_drain=True) as block:

            @block.sync
            def _(sp):
                for p in range(PLANES):
                    sp.dma_start(planes[:, :, p * WORDS:(p + 1) * WORDS],
                                 dram["L0_ffn_qweight"][p].rearrange("(t p) w -> p t w", p=P)).then_inc(loaded, 16)
                sp.dma_start(lut[:, :, :], dram["L0_ffn_lut4"].rearrange("(t p) c -> p t c", p=P)).then_inc(loaded, 16)
                sp.dma_start(bias[:, :], dram["L0_ffn_bias"].unsqueeze(0).broadcast_to([P, D])).then_inc(bias_loaded, 16)

            @block.gpsimd
            def _(g):
                g.iota(shifts[:, :], [[1, BITS]], base=0, channel_multiplier=0).then_inc(shifts_ready, 1)
                norm_gpsimd(k, n)

            @block.vector
            def _(v):
                norm_vector(k, n)
                v.wait_ge(loaded, 16 * (PLANES + 1))
                v.wait_ge(shifts_ready, 1)
                v.tensor_tensor(diff[:, :, :], lut[:, :, 1::2], lut[:, :, 0::2], ALU.subtract).then_inc(diff_ready, 1)
                v.wait_ge(bias_loaded, 16)
                v.wait_ge(k.xn_ready, TILES * (n + 1))
                for t in range(TILES):
                    k.vown(v.tensor_tensor(k.x[:, t, :], k.x[:, t, :], bias[:, :], ALU.add))

                def unpack(o):
                    if o >= 1:
                        v.wait_ge(bits_ready, o)
                    if o >= 2:
                        v.wait_ge(weight_ready, o - 1)
                        v.wait_ge(leaves_ready, o - 1)
                    k.vown(v.tensor_tensor(moved[:, :, :], planes[:, o, :].unsqueeze(2).broadcast_to([P, PLANES * WORDS, BITS]),
                                           shifts[:, :].unsqueeze(1).broadcast_to([P, PLANES * WORDS, BITS]),
                                           ALU.logical_shift_right))
                    k.vown.wait()
                    v.tensor_scalar(bits[:, o % 2, :, :].rearrange("p a (w b) -> p (a w) b", b=BITS), moved[:, :, :],
                                    1, None, ALU.bitwise_and).then_inc(bits_ready, 1)

                def choose(o):
                    v.wait_ge(leaves_ready, o + 1)
                    left = tree[:, o % 2, :, :]
                    for level in range(1, PLANES):
                        step = 2 ** (level - 1)
                        count = CODES // 2 // (2 * step)
                        mask = bits[:, o % 2, level, :].unsqueeze(1).broadcast_to([P, count, D])
                        ins = v.copy_predicated(left[:, 0::2 * step, :], mask, left[:, step::2 * step, :])
                        if level == PLANES - 1:
                            ins.then_inc(weight_ready, 1)
                        else:
                            k.vown(ins)
                            k.vown.wait()

                unpack(0)
                for o in range(OT):
                    if o + 1 < OT:
                        unpack(o + 1)
                    choose(o)
                k.vown.wait()
                for t in range(TILES):
                    v.wait_ge(product_psum, t + 1)
                    k.vown(v.tensor_tensor(k.x[:, t, :], k.bank[4 + t][:, :], k.x[:, t, :], ALU.add))
                k.vown.wait()

            @block.scalar
            def _(a):
                def weightT_copy(o):
                    a.wait_ge(weightT_psum, o + 1)
                    a.copy(weightT[:, :, o * P:(o + 1) * P],
                                   k.bank[2 + o % 2][:, :].rearrange("p (f c) -> p f c", f=KT)).then_inc(weightT_ready, 1)

                norm_scalar(k, m, k.bank[0:2])
                a.wait_ge(diff_ready, 1)
                for o in range(OT):
                    a.wait_ge(bits_ready, o + 1)
                    if o >= 2:
                        a.wait_ge(weightT_psum, o - 1)
                    for j in range(CODES // 2):
                        ins = a.activation(tree[:, o % 2, j, :], bits[:, o % 2, 0, :], ACT.Identity,
                                           bias=lut[:, o, 2 * j:2 * j + 1], scale=diff[:, o, j:j + 1])
                    ins.then_inc(leaves_ready, 1)
                    if o >= 1:
                        weightT_copy(o - 1)
                weightT_copy(OT - 1)

            @block.tensor
            def _(pe):
                norm_tensor(k, n, m, k.bank[0:2])
                for o in range(OT):
                    pe.wait_ge(weight_ready, o + 1)
                    if o >= 2:
                        pe.wait_ge(weightT_ready, o - 1)
                    for f in range(KT):
                        last = pe.transpose(k.bank[2 + o % 2][:, f * P:(f + 1) * P],
                                            tree[:, o % 2, 0, f * P:(f + 1) * P], k.ident[:, :])
                    last.then_inc(weightT_psum, 1)
                pe.wait_ge(k.xnT_ready, TILES * (m + 1))
                pe.wait_ge(weightT_ready, OT)
                for t in range(TILES):
                    for f in range(KT):
                        last = pe.matmul(k.bank[4 + t][:, :], k.xnT[:, f, t * P:(t + 1) * P], weightT[:, f, :],
                                         start=f == 0, stop=f == KT - 1)
                    last.then_inc(product_psum, 1)



def layer1_attention(k, dram):
    nc, n, m = k.nc, k.norms, k.turned
    k.norms += 1
    k.turned += 1
    HEADS, LQ, LKV, HD = 16, D // 8, D // 16, D // 16
    COPIES = P // LKV
    QUERIES_AT = (0, 5, 9, 13)
    AHEAD = 4
    SCALE = LKV ** -0.5
    with ExitStack() as s:
        ctxT = k.sbuf("ctxT_plain", [P, KT, B * CTX], F32, s)
        wq = k.sbuf("wq", [P, KT, 2 * LQ], F32, s)
        wkv = k.sbuf("wkv", [P, KT, P], F32, s)
        raw_qk = k.sbuf("raw_qk", [P, HEADS * P], F32, s)
        wqk = k.sbuf("wqk", [P, 2, HEADS * P], F32R, s)
        raw_v = k.sbuf("raw_v", [P, D], F32, s)
        wv = k.sbuf("wv", [P, D], F32R, s)
        keysT = k.sbuf("keysT", [P, B, CTX], F32R, s)
        values = k.sbuf("values", [P, CTILES, D], F32, s)
        latentT = k.sbuf("latentT", [P, TILES * P], F32R, s)
        queriesT = k.sbuf("queriesT", [P, B, HEADS, P], F32R, s)
        probs = k.sbuf("probs", [P, 4, CTX], F32, s)
        probsT = k.sbuf("probsT", [P, 4, CPB, P], F32, s)
        negmax = k.sbuf("negmax", [P, B, HEADS], F32, s)
        sums = k.sbuf("sums", [P, B, HEADS], F32, s)
        inverse = k.sbuf("inverse", [P, HEADS], F32, s)
        mixedT = k.sbuf("mixedT", [P, D], F32, s)
        mixed = k.sbuf("mixed", [P, D], F32, s)
        k.flags = k.sbuf("flags", [P, 2, CTX], BF16, s)
        names = ("operands_psum", "operands_high", "operands_low",
                 "loaded", "ctx_loaded", "wqk_low", "values_psum", "values_ready",
                 "queries_psum", "queries_high", "queries_low", "scores_psum", "negmax_ready", "probs_ready",
                 "probsT_psum", "probsT_ready", "heads_done", "mixedT_ready", "mixed_psum", "inverse_ready", "mixed_ready", "x_updated")
        S_ = {x: k.sem(f"l1a_{x}") for x in names}
        S, T, O, Q = k.bank[0:4], k.bank[4:6], k.bank[6], k.bank[7]
        batch = lambda step: step[1] % B
        ahead = lambda step, h: (step, h + AHEAD - 1) if h + AHEAD - 1 < HEADS else (after(step), h + AHEAD - 1 - HEADS)

        def tile(step):
            i, offset = step
            return batch(step) * TPB + (offset // B if i is None else i + offset // B)

        with nc.Block(no_gpsimd_drain=True) as block:

            @block.sync
            def _(sp):
                for target, source in ((wkv[:, :, :], dram["wkv4"].rearrange("(f p) c -> p f c", p=P)),
                                       (raw_v[:, :], dram["wv4"])):
                    sp.dma_start(target, source).then_inc(S_["ctx_loaded"], 16)
                sp.dma_start(ctxT[:, :, :], dram["ctxT"].rearrange("(f p) r -> p f r", p=P)).then_inc(S_["ctx_loaded"], 16)
                for target, source in ((wq[:, :, :], dram["wq2"].rearrange("(f p) c -> p f c", p=P)),
                                       (raw_qk[:, :], dram["wqk8"])):
                    sp.dma_start(target, source).then_inc(S_["loaded"], 16)

            @block.gpsimd
            def _(g):
                norm_gpsimd(k, n)
                g.wait_ge(S_["loaded"], 32)
                k.pown(g.tensor_copy(wqk[:, 0, :], raw_qk[:, :]))
                k.pown.wait()
                g.tensor_tensor(wqk[:, 1, :], raw_qk[:, :], wqk[:, 0, :], ALU.subtract).then_inc(S_["wqk_low"], 1)

            @block.tensor
            def _(pe):
                norm_tensor(k, n, m, T)
                pe.wait_ge(S_["loaded"], 32)
                pe.wait_ge(k.xnT_ready, TILES * (m + 1))
                for f in range(KT):
                    last = pe.matmul(Q[:, :], wq[:, f, :], k.xnT[:, f, :], start=f == 0, stop=f == KT - 1)
                last.then_inc(S_["operands_psum"], 1)
                pe.wait_ge(S_["ctx_loaded"], 48)
                for b in range(B):
                    for f in range(KT):
                        last = pe.matmul(S[b][:, :], wkv[:, f, :], ctxT[:, f, b * CTX:(b + 1) * CTX],
                                         start=f == 0, stop=f == KT - 1)
                    last.then_inc(S_["operands_psum"], 1)

                def queries(step, j):
                    if not (step[0] is None and j == 0):
                        pe.wait_ge(S_["queries_low"], at(step, 4, j))
                    t = tile(step)
                    tokens = slice(t * P, (t + 1) * P) if step[0] is None else bass.ts(t, P)
                    for h in range(4 * j, 4 * j + 4):
                        for part in range(2):
                            last = pe.matmul(Q[:, h % 4 * P:(h % 4 + 1) * P], wqk[:, part, h * P:(h + 1) * P],
                                             latentT[:, tokens], start=part == 0, stop=part == 1)
                    last.then_inc(S_["queries_psum"], 1)

                def scores(step, h):
                    if step[0] is not None:
                        pe.wait_ge(S_["probs_ready"], at(step, HEADS, h - 3))
                    if h % 4 == 0:
                        pe.wait_ge(S_["queries_low"], at(step, 4, h // 4 + 1))
                    pe.matmul(S[h % 4][:, :], queriesT[:, batch(step), h, :], keysT[:, batch(step), :],
                              start=True, stop=True).then_inc(S_["scores_psum"], 1)

                def turn(step, h):
                    if h >= 2:
                        pe.wait_ge(S_["probsT_ready"], at(step, HEADS, h - 1))
                    pe.wait_ge(S_["probs_ready"], at(step, HEADS, h + 1))
                    for c in range(CPB):
                        last = pe.transpose(T[h % 2][:, c * P:(c + 1) * P], probs[:, h % 4, c * P:(c + 1) * P],
                                            k.ident[:, :])
                    last.then_inc(S_["probsT_psum"], 1)

                def mix(step, h):
                    if h == 0:
                        pe.wait_ge(S_["mixedT_ready"], at(step, 1, 1))
                    pe.wait_ge(S_["probsT_ready"], at(step, HEADS, h + 1))
                    for c in range(CPB):
                        last = pe.matmul(O[h % 4 * HD:(h % 4 + 1) * HD, h // 4 * P:(h // 4 + 1) * P],
                                         values[:, batch(step) * CPB + c, h * HD:(h + 1) * HD], probsT[:, h % 4, c, :],
                                         start=c == 0, stop=c == CPB - 1)
                    last.then_inc(S_["heads_done"], 1)

                def turn_mixed(step, c):
                    pe.wait_ge(S_["queries_low"], at(after(step, 2), 4, c))
                    pe.wait_ge(S_["mixedT_ready"], at(step, 1, 2))
                    for g in range(HEADS // 4):
                        last = pe.transpose(Q[:, g * P:(g + 1) * P], mixedT[:, g * P:(g + 1) * P], k.ident[:, :])
                    last.then_inc(S_["mixed_psum"], 1)

                pe.wait_ge(S_["operands_low"], 1)
                pe.wait_ge(S_["wqk_low"], 1)
                start = (None, 0)
                queries(start, 0)
                pe.wait_ge(S_["operands_low"], 2)
                for r in range(CTILES):
                    pe.wait_ge(S_["operands_low"], r // CPB + 3)
                    if r >= 2:
                        pe.wait_ge(S_["values_ready"], r - 1)
                    pe.matmul(S[2 + r % 2][:, :], keysT[:, r // CPB, (r % CPB) * P:(r % CPB + 1) * P], wv[:, :],
                              start=True, stop=True).then_inc(S_["values_psum"], 1)
                    if r % 2 == 1 and r < 6:
                        queries(start, r // 2 + 1)
                pe.wait_ge(S_["values_ready"], CTILES)
                for h in range(AHEAD):
                    scores(start, h)
                with pe.Fori(0, TPB) as i:
                    for b in range(B):
                        step = (i, b)
                        for h in range(HEADS):
                            if h == 3 and b == 1:
                                turn_mixed((i, 0), 1)
                            if h in QUERIES_AT:
                                if (b, h) in ((0, QUERIES_AT[0]), (1, QUERIES_AT[1])):
                                    pe.wait_ge(S_["mixed_ready"], at((i, 0), 1, b + 1))
                                queries(after(step), QUERIES_AT.index(h))
                            turn(step, h)
                            if h + AHEAD < HEADS:
                                scores(step, h + AHEAD)
                            else:
                                scores(after(step), h + AHEAD - HEADS)
                            if h >= 2:
                                mix(step, h - 2)
                        mix(step, HEADS - 2)
                        mix(step, HEADS - 1)
                    turn_mixed((i, 1), 0)

            @block.vector
            def _(v):
                own = k.vown
                norm_vector(k, n)
                v.wait_ge(k.ctxT_loaded, 16)
                bisection_start(k)
                v.wait_ge(S_["operands_high"], 1)
                v.scalar_tensor_tensor(latentT[LQ:P, :], Q[LQ:P, :], SCALE, latentT[LQ:P, :],
                                       ALU.mult, ALU.subtract).then_inc(S_["operands_low"], 1)
                v.wait_ge(S_["operands_high"], 2)
                v.tensor_tensor(wv[P // 2:P, :], raw_v[P // 2:P, :], wv[P // 2:P, :], ALU.subtract).then_inc(S_["operands_low"], 1)
                for b in range(B):
                    v.wait_ge(S_["operands_high"], b + 3)
                    for j in (1, 3):
                        rows = slice(j * LKV, (j + 1) * LKV)
                        last = v.tensor_tensor(keysT[rows, b, :], S[b][rows, :], keysT[rows, b, :], ALU.subtract)
                    last.then_inc(S_["operands_low"], 1)

                def queries_low(step, j):
                    v.wait_ge(S_["queries_high"], at(step, 4, j + 1))
                    now = queriesT[P // 2:P, batch(step), 4 * j:4 * j + 4, :]
                    v.tensor_tensor(now, Q[P // 2:P, :].rearrange("p (h q) -> p h q", h=4), now, ALU.subtract)\
                     .then_inc(S_["queries_low"], 1)

                start = (None, 0)
                queries_low(start, 0)
                for r in range(CTILES):
                    v.wait_ge(S_["values_psum"], r + 1)
                    v.tensor_copy(values[:, r, :], S[2 + r % 2][:, :]).then_inc(S_["values_ready"], 1)
                    if r % 2 == 1 and r < 6:
                        queries_low(start, r // 2 + 1)
                v.sem_inc(S_["mixed_ready"], 1)

                def maximum(step, h):
                    v.wait_ge(S_["scores_psum"], at(step, HEADS, h + 1))
                    v.tensor_reduce(negmax[:, batch(step), h:h + 1], S[h % 4][:, :], AX.X, ALU.max, negate=True)\
                     .then_inc(S_["negmax_ready"], 1)

                def add_mixed(step):
                    v.wait_ge(S_["probs_ready"], at(step, HEADS, HEADS))
                    v.reciprocal(inverse[:, :], sums[:, batch(step), :]).then_inc(S_["inverse_ready"], 1)
                    v.wait_ge(S_["inverse_ready"], at(step, 1, 1))
                    v.wait_ge(S_["mixed_psum"], at(step, 1, 1))
                    v.tensor_tensor(mixed[:, :].rearrange("p (h d) -> p h d", h=HEADS),
                                    Q[:, :].rearrange("p (h d) -> p h d", h=HEADS),
                                    inverse[:, :].unsqueeze(2).broadcast_to([P, HEADS, HD]), ALU.mult)\
                     .then_inc(S_["mixed_ready"], 1)
                    v.wait_ge(S_["mixed_ready"], at(step, 1, 2))
                    v.tensor_tensor(k.x[:, tile(step), :], k.x[:, tile(step), :], mixed[:, :], ALU.add)\
                     .then_inc(S_["x_updated"], 1)

                for h in range(AHEAD - 1):
                    maximum(start, h)
                with v.Fori(0, TPB) as i:
                    for b in range(B):
                        step = (i, b)
                        for h in range(HEADS):
                            maximum(*ahead(step, h))
                            if h - 2 in QUERIES_AT:
                                queries_low(after(step), QUERIES_AT.index(h - 2))
                            if h == 3 and b == 1:
                                add_mixed((i, 0))
                    add_mixed((i, 1))
                v.wait_ge(S_["x_updated"], TILES)

            @block.scalar
            def _(a):
                norm_scalar(k, m, T)
                a.wait_ge(S_["operands_psum"], 1)
                a.activation(latentT[:, :], Q[:, :], ACT.Copy, scale=SCALE).then_inc(S_["operands_high"], 1)
                a.wait_ge(S_["ctx_loaded"], 48)
                a.copy(wv[:, :], raw_v[:, :]).then_inc(S_["operands_high"], 1)
                for b in range(B):
                    a.wait_ge(S_["operands_psum"], b + 2)
                    a.copy(keysT[:, b, :], S[b][:, :]).then_inc(S_["operands_high"], 1)

                def queries_high(step, j):
                    a.wait_ge(S_["queries_psum"], at(step, 4, j + 1))
                    a.copy(queriesT[:, batch(step), 4 * j:4 * j + 4, :], Q[:, :].rearrange("p (h q) -> p h q", h=4))\
                     .then_inc(S_["queries_high"], 1)

                start = (None, 0)
                queries_high(start, 0)
                for j in range(1, 4):
                    queries_high(start, j)

                def exponentials(step, h):
                    a.wait_ge(S_["negmax_ready"], at(step, HEADS, h + 1))
                    if not (is_start(step) and h < 4):
                        a.wait_ge(S_["probsT_psum"], at(step, HEADS, h - 3))
                    if h == 0 and not is_start(step):
                        a.wait_ge(S_["mixed_ready"], at(step, 1, 0))
                    a.activation(probs[:, h % 4, :], S[h % 4][:, :], ACT.Exp, bias=negmax[:, batch(step), h:h + 1],
                                 accum_out=sums[:, batch(step), h:h + 1]).then_inc(S_["probs_ready"], 1)

                def copy_turned(step, h):
                    a.wait_ge(S_["probsT_psum"], at(step, HEADS, h + 1))
                    if h >= 4:
                        a.wait_ge(S_["heads_done"], at(step, HEADS, h - 3))
                    a.copy(probsT[:, h % 4, :, :], T[h % 2][:, :].rearrange("p (c q) -> p c q", c=CPB))\
                     .then_inc(S_["probsT_ready"], 1)

                def copy_mixed(step):
                    a.wait_ge(S_["heads_done"], at(step, HEADS, HEADS))
                    a.wait_ge(S_["mixed_ready"], at(step, 1, 1))
                    a.copy(mixedT[:, :], O[:, :]).then_inc(S_["mixedT_ready"], 1)

                a.sem_inc(S_["mixedT_ready"], 1)
                for h in range(AHEAD - 1):
                    exponentials(start, h)
                with a.Fori(0, TPB) as i:
                    for b in range(B):
                        step = (i, b)
                        for h in range(HEADS):
                            copy_turned(step, h)
                            exponentials(*ahead(step, h))
                            if h - 2 in QUERIES_AT:
                                queries_high(after(step), QUERIES_AT.index(h - 2))
                            if h == 0 and b == 1:
                                copy_mixed((i, 0))
                    copy_mixed((i, 1))



def layer1_ffn(k, dram):
    nc, n = k.nc, k.norms
    k.norms += 1
    I = 1376
    IT = -(-I // P)
    TAIL = I - (IT - 1) * P
    CHUNKS = [(c, min(c + 512, I)) for c in range(0, I, 512)]
    NC = len(CHUNKS)
    SQRT7 = float(np.float32(np.sqrt(7.0)))
    GATE, UP, DOWN = range(3)
    with ExitStack() as s:
        raw = k.sbuf("raw", [P, KT, I], F32, s)
        rawd = k.sbuf("rawd", [P, IT, D], F32, s)
        work = k.sbuf("work", [P, max(KT * I, IT * D)], F32, s)
        wgu = k.sbuf("wgu", [P, 2, KT, I], BF16, s)
        wd = k.sbuf("wd", [P, IT, D], BF16, s)
        total = k.sbuf("total", [P, 4], F32, s)
        wmean = k.sbuf("wmean", [P, 3], F32, s)
        winv = k.sbuf("winv", [P, 3], F32, s)
        scales = k.sbuf("scales", [P, 3], F32, s)
        wscale = k.sbuf("wscale", [P, 3], F32, s)
        round_col = k.sbuf("round_col", [P, 1], F32, s)
        t1 = k.sbuf("t1", [P, TILES, D], F32, s)
        x4 = k.sbuf("x4", [P, TILES, D], BF16, s)
        x4T = k.sbuf("x4T", [P, KT, TILES * P], BF16, s)
        beta = k.sbuf("beta", [P, TILES], F32, s)
        betae = k.sbuf("betae", [P, TILES], F32, s)
        binv = k.sbuf("binv", [P, TILES], F32, s)
        gate_scale = k.sbuf("gate_scale", [P, TILES], F32, s)
        up_scale = k.sbuf("up_scale", [P, TILES], F32, s)
        relu = k.sbuf("relu", [P, 2, 512], F32, s)
        gate = k.sbuf("gate", [P, 2, 512], F32, s)
        inner = k.sbuf("inner", [P, 2, I], F32, s)
        gamma = k.sbuf("gamma", [P, TILES], F32, s)
        gammae = k.sbuf("gammae", [P, TILES], F32, s)
        ginv = k.sbuf("ginv", [P, TILES], F32, s)
        x8 = k.sbuf("x8", [P, 2, I], BF16, s)
        x8T = k.sbuf("x8T", [P, IT, TILES * P], BF16, s)
        down_scale = k.sbuf("down_scale", [P, TILES], F32, s)
        loaded = [k.sem(f"l1f_loaded_{x}") for x in ("gate", "up", "down")]
        scales_loaded, raw_free, total_ready, total_psum, winv_ready, rounded, clipped, weights_ready, x4_ready, \
            x4T_psum, x4T_ready, gate_psum, up_psum, relu_ready, gate_ready, inner_ready, x8_ready, x8T_psum, \
            x8T_ready, down_psum, constants = (k.sem(f"l1f_{x}") for x in (
                "scales_loaded", "raw_free", "total_ready", "total_psum", "winv_ready", "rounded", "clipped",
                "weights_ready", "x4_ready", "x4T_psum", "x4T_ready", "gate_psum", "up_psum", "relu_ready",
                "gate_ready", "inner_ready", "x8_ready", "x8T_psum", "x8T_ready", "down_psum", "constants"))
        G, U, T, O = k.bank[0:2], k.bank[2:4], k.bank[4:6], k.bank[6:8]
        raws = [raw[:, :, :].rearrange("p f c -> p (f c)")] * 2 + [rawd[:, :, :].rearrange("p f c -> p (f c)")]
        targets = [wgu[:, 0, :, :].rearrange("p f c -> p (f c)"), wgu[:, 1, :, :].rearrange("p f c -> p (f c)"),
                   wd[:, :, :].rearrange("p f c -> p (f c)")]
        names = ("w_gateT", "w_upT", "w_downT")
        with nc.Block(no_gpsimd_drain=True) as block:

            def load(w):
                if w == DOWN:
                    nc.sync.wait_ge(constants, 1)
                    nc.sync.dma_start(rawd[:, 0:IT - 1, :], dram["w_downT"][0:(IT - 1) * P, :]
                                      .rearrange("(f p) c -> p f c", p=P)).then_inc(loaded[w], 16)
                    nc.sync.dma_start(rawd[0:TAIL, IT - 1, :], dram["w_downT"][(IT - 1) * P:I, :])\
                      .then_inc(loaded[w], 16)
                else:
                    nc.sync.dma_start(raw[:, :, :], dram[names[w]].rearrange("(f p) c -> p f c", p=P))\
                      .then_inc(loaded[w], 16)

            @block.sync
            def _(sp):
                for i, name in enumerate(("s_gate", "s_up", "s_down")):
                    sp.dma_start(scales[:, i:i + 1], dram["L1_ffn_" + name].unsqueeze(0).broadcast_to([P, 1]))\
                      .then_inc(scales_loaded, 16)
                load(GATE)
                load(DOWN)
                sp.wait_ge(rounded, 1)
                load(UP)

            @block.gpsimd
            def _(g):
                g.memset(rawd[:, IT - 1, :], 0.0).then_inc(constants, 1)
                g.memset(round_col[:, :], ROUND).then_inc(constants, 1)
                norm_gpsimd(k, n)

            @block.scalar
            def _(a):
                a.wait_ge(constants, 2)
                for i, w in enumerate((GATE, DOWN, UP)):
                    size = IT * D if w == DOWN else KT * I
                    a.wait_ge(loaded[w], 32 if w == DOWN else 16)
                    if i >= 1:
                        a.wait_ge(weights_ready, i)
                    a.activation(work[:, 0:size], raws[w], ACT.Abs, accum_out=total[:, w:w + 1])\
                     .then_inc(total_ready, 1)
                    a.wait_ge(total_ready, i + 1)
                    a.wait_ge(winv_ready, i + 1)
                    a.activation(work[:, 0:size], raws[w], ACT.Identity, bias=round_col[:, 0:1],
                                 scale=winv[:, w:w + 1]).then_inc(rounded, 1)
                for t in range(TILES):
                    a.wait_ge(x4T_psum, t + 1)
                    a.copy(x4T[:, :, t * P:(t + 1) * P],
                           T[t % 2][:, 0:256].bitcast(BF16).rearrange("p (f c) -> p f c", f=KT)).then_inc(x4T_ready, 1)

                def x8T_copy(t):
                    for half, (first, last) in enumerate(((0, 8), (8, IT))):
                        a.wait_ge(x8T_psum, 2 * t + half + 1)
                        rows = P if half == 0 else TAIL
                        source = T[half][:, :].bitcast(BF16).rearrange("p (f c) -> p f c", f=8)
                        if half == 0:
                            a.copy(x8T[:, 0:8, t * P:(t + 1) * P], source).then_inc(x8T_ready, 1)
                        else:
                            k.aown(a.copy(x8T[:, 8:IT - 1, t * P:(t + 1) * P], source[:, 0:IT - 9, :]))
                            a.copy(x8T[0:TAIL, IT - 1, t * P:(t + 1) * P], source[0:TAIL, IT - 9, :])\
                             .then_inc(x8T_ready, 1)

                for t in range(TILES):
                    for c, (c0, c1) in enumerate(CHUNKS):
                        i = NC * t + c
                        a.wait_ge(gate_psum, i + 1)
                        a.activation(relu[:, i % 2, 0:c1 - c0], G[i % 2][:, 0:c1 - c0], ACT.Relu,
                                     scale=gate_scale[:, t:t + 1]).then_inc(relu_ready, 1)
                        a.wait_ge(relu_ready, i + 1)
                        if i >= 2:
                            a.wait_ge(inner_ready, i - 1)
                        a.activation(gate[:, i % 2, 0:c1 - c0], relu[:, i % 2, 0:c1 - c0], ACT.Square)\
                         .then_inc(gate_ready, 1)
                    if t >= 1:
                        x8T_copy(t - 1)
                x8T_copy(TILES - 1)

            @block.vector
            def _(v):
                norm_vector(k, n)
                v.wait_ge(scales_loaded, 48)

                def weight_scale(i, w):
                    k.vown(v.tensor_scalar(wmean[:, w:w + 1], k.bank[6 + i % 2][:, 0:1], 1.0 / (I * D), None, ALU.mult))
                    k.vown.wait()
                    k.vown(v.tensor_scalar(winv[:, w:w + 1], wmean[:, w:w + 1], EPS, None, ALU.add))
                    k.vown(v.tensor_tensor(wscale[:, w:w + 1], wmean[:, w:w + 1], scales[:, w:w + 1], ALU.mult))
                    k.vown.wait()
                    v.reciprocal(winv[:, w:w + 1], winv[:, w:w + 1]).then_inc(winv_ready, 1)

                def weight_round(i, w):
                    size = IT * D if w == DOWN else KT * I
                    v.wait_ge(rounded, i + 1)
                    v.tensor_scalar(work[:, 0:size], work[:, 0:size], ROUND, -1.0, ALU.subtract, ALU.max)\
                     .then_inc(clipped, 1)
                    v.wait_ge(clipped, i + 1)
                    v.tensor_scalar(targets[w], work[:, 0:size], 1.0, None, ALU.min).then_inc(weights_ready, 1)

                def weight(i, w):
                    v.wait_ge(total_psum, i + 1)
                    weight_scale(i, w)
                    weight_round(i, w)

                weight(0, GATE)
                v.wait_ge(k.xn_ready, TILES * (n + 1))
                for t in range(TILES):
                    k.vown(v.tensor_reduce(beta[:, t:t + 1], k.xn[:, t, :], AX.X, ALU.add, apply_absolute_value=True))
                k.vown.wait()
                k.vown(v.tensor_scalar(beta[:, :], beta[:, :], 1.0 / D, None, ALU.mult))
                k.vown.wait()
                k.vown(v.tensor_scalar(betae[:, :], beta[:, :], EPS, None, ALU.add))
                k.vown.wait()
                k.vown(v.reciprocal(binv[:, :], betae[:, :]))
                k.vown.wait()
                for t in range(TILES):
                    k.vown(v.tensor_scalar(t1[:, t, :], k.xn[:, t, :], SQRT7, binv[:, t:t + 1], ALU.mult, ALU.mult))
                k.vown.wait()
                for t in range(TILES):
                    k.vown(v.tensor_scalar(t1[:, t, :], t1[:, t, :], ROUND, ROUND, ALU.add, ALU.subtract))
                k.vown.wait()
                for t in range(TILES):
                    v.tensor_scalar(x4[:, t, :], t1[:, t, :], -8.0, 7.0, ALU.max, ALU.min).then_inc(x4_ready, 1)
                weight(1, DOWN)
                weight(2, UP)
                k.vown(v.tensor_scalar(betae[:, :], beta[:, :], SQRT7, 1.0 / SQRT7, ALU.mult, ALU.mult))
                k.vown.wait()
                k.vown(v.tensor_scalar(up_scale[:, :], betae[:, :], wscale[:, UP:UP + 1], None, ALU.mult))
                k.vown(v.tensor_scalar(gate_scale[:, :], betae[:, :], wscale[:, GATE:GATE + 1], None, ALU.mult))
                k.vown.wait()
                v.engine_nop().then_inc(constants, 1)

                def quantise8(t):
                    k.vown(v.tensor_reduce(gamma[:, t:t + 1], inner[:, t % 2, :], AX.X, ALU.max, apply_absolute_value=True))
                    k.vown.wait()
                    k.vown(v.tensor_scalar(gammae[:, t:t + 1], gamma[:, t:t + 1], EPS, None, ALU.add))
                    k.vown.wait()
                    k.vown(v.reciprocal(ginv[:, t:t + 1], gammae[:, t:t + 1]))
                    k.vown.wait()
                    k.vown(v.tensor_scalar(inner[:, t % 2, :], inner[:, t % 2, :], 127.0, ginv[:, t:t + 1],
                                           ALU.mult, ALU.mult))
                    k.vown.wait()
                    k.vown(v.tensor_scalar(inner[:, t % 2, :], inner[:, t % 2, :], ROUND, ROUND, ALU.add, ALU.subtract))
                    k.vown.wait()
                    if t >= 2:
                        v.wait_ge(x8T_psum, 2 * (t - 1))
                    v.tensor_scalar(x8[:, t % 2, :], inner[:, t % 2, :], -128.0, 127.0, ALU.max, ALU.min)\
                     .then_inc(x8_ready, 1)

                for t in range(TILES):
                    for c, (c0, c1) in enumerate(CHUNKS):
                        i = NC * t + c
                        v.wait_ge(up_psum, i + 1)
                        v.wait_ge(gate_ready, i + 1)
                        if t >= 2:
                            v.wait_ge(x8_ready, t - 1)
                        v.scalar_tensor_tensor(inner[:, t % 2, c0:c1], U[i % 2][:, 0:c1 - c0], up_scale[:, t:t + 1],
                                               gate[:, i % 2, 0:c1 - c0], ALU.mult, ALU.mult).then_inc(inner_ready, 1)
                    v.wait_ge(inner_ready, NC * (t + 1))
                    quantise8(t)
                k.vown(v.tensor_scalar(gammae[:, :], gamma[:, :], 1.0 / 127.0, wscale[:, DOWN:DOWN + 1], ALU.mult, ALU.mult))
                k.vown.wait()
                for t in range(TILES):
                    v.wait_ge(down_psum, t + 1)
                    k.vown(v.scalar_tensor_tensor(k.x[:, t, :], O[t % 2][:, :], gammae[:, t:t + 1], k.x[:, t, :],
                                                  ALU.mult, ALU.add))
                    k.vown.wait()
                    v.engine_nop().then_inc(clipped, 1)

            @block.tensor
            def _(pe):
                for i, w in enumerate((GATE, DOWN, UP)):
                    pe.wait_ge(total_ready, i + 1)
                    if i >= 2:
                        pe.wait_ge(winv_ready, i - 1)
                    pe.matmul(k.bank[6 + i % 2][:, 0:1], k.ones[:, :], total[:, w:w + 1], start=True, stop=True)\
                      .then_inc(total_psum, 1)
                for t in range(TILES):
                    pe.wait_ge(x4_ready, t + 1)
                    if t >= 2:
                        pe.wait_ge(x4T_ready, t - 1)
                    for f in range(KT):
                        last = pe.transpose(T[t % 2][:, 0:256].bitcast(BF16)[:, f * P:(f + 1) * P],
                                            x4[:, t, f * P:(f + 1) * P], k.ident16[:, :])
                    last.then_inc(x4T_psum, 1)
                pe.wait_ge(x4T_ready, TILES)
                pe.wait_ge(weights_ready, 3)
                pe.wait_ge(constants, 3)

                def turn8(t):
                    pe.wait_ge(x8_ready, t + 1)
                    for f in range(IT):
                        rows = P if f < IT - 1 else TAIL
                        half = f // 8
                        if f % 8 == 0 and t >= 1:
                            pe.wait_ge(x8T_ready, 2 * (t - 1) + half + 1)
                        last = pe.transpose(T[half][:, :].bitcast(BF16)[0:rows, f % 8 * P:(f % 8 + 1) * P],
                                            x8[:, t % 2, f * P:f * P + rows], k.ident16[:, :])
                        if f in (7, IT - 1):
                            last.then_inc(x8T_psum, 1)

                for t in range(TILES):
                    for c, (c0, c1) in enumerate(CHUNKS):
                        i = NC * t + c
                        if i >= 2:
                            pe.wait_ge(relu_ready, i - 1)
                            pe.wait_ge(inner_ready, i - 1)
                        for w, bank, ready in ((GATE, G, gate_psum), (UP, U, up_psum)):
                            for f in range(KT):
                                last = pe.matmul(bank[i % 2][:, 0:c1 - c0], x4T[:, f, t * P:(t + 1) * P],
                                                 wgu[:, w, f, c0:c1], start=f == 0, stop=f == KT - 1)
                            last.then_inc(ready, 1)
                    if t >= 1:
                        turn8(t - 1)
                turn8(TILES - 1)
                for t in range(TILES):
                    pe.wait_ge(x8T_ready, 2 * (t + 1))
                    if t >= 2:
                        pe.wait_ge(clipped, 3 + t - 1)
                    for f in range(IT):
                        rows = P if f < IT - 1 else TAIL
                        last = pe.matmul(O[t % 2][:, :], x8T[0:rows, f, t * P:(t + 1) * P], wd[0:rows, f, :],
                                         start=f == 0, stop=f == IT - 1)
                    last.then_inc(down_psum, 1)



PARTS = ((0, 0), (0, 1), (1, 0))


def layer2_attention(k, dram):
    nc, n = k.nc, k.norms
    k.norms += 1
    HEADS, GROUPS, HD = 32, 8, 128
    REP = HEADS // GROUPS
    GW = REP * HD
    STEPS = GROUPS * B
    UNITS = REP * TPB
    PAIRS = UNITS // 2
    CHUNKS = 1 + TPB
    KV = CPB // 2
    SCALE = HD ** -0.5
    ROUNDS = 32 // STEPS
    OWN_V, OWN_P = BISECT_PER_ROUND * ROUNDS, 2 * CHUNKS
    with ExitStack() as s:
        xnT2 = k.sbuf("xnT2", [P, 2, KT, TILES * P], F32R, s)
        ctxT2 = k.sbuf("ctxT2", [P, 2, KT, B * CTX], F32R, s)
        raw_kv = k.sbuf("raw_kv", [P, KT, 2 * HD], F32, s)
        raw_q = k.sbuf("raw_q", [P, KT, GW], F32, s)
        raw_o = k.sbuf("raw_o", [P, REP, D], F32, s)
        wq = k.sbuf("wq2", [P, 2, KT, GW], F32R, s)
        wkv = k.sbuf("wkv2", [P, 2, KT, 2 * HD], F32R, s)
        wo = k.sbuf("wo2", [P, 2, REP, D], F32R, s)
        rows = k.xn
        k.flags = k.xn[:, 3, :].bitcast(BF16).rearrange("p (j c) -> p j c", j=2)
        masked = k.xnT[:, 0:2, :]
        squares = k.xnT[:, 2:4, :]
        ssq = k.sbuf("ssq", [P, CHUNKS, REP], F32, s)
        headsT = k.sbuf("headsT", [P, 2, REP, TILES * P], F32R, s)
        keysT = k.sbuf("keysT2", [P, 2, B * CTX], F32R, s)
        values = k.sbuf("values2", [P, 2, CTILES, HD], F32R, s)
        mask = k.sbuf("mask", [P, TPB, CTX], F32, s)
        weights = k.sbuf("norm_weights", [P, 2], F32, s)
        keyscale = weights
        probs = k.sbuf("probs2", [P, 3, CTX], F32, s)
        probsT = k.sbuf("probsT2", [P, 2, 2, CPB, SEQ], F32R, s)
        statistics = k.stats[:, :, :].rearrange("p t s -> p (t s)")
        negmax, sums, inverse = (statistics[:, j * UNITS:(j + 1) * UNITS] for j in range(3))
        names = ("mask_loaded", "kv_loaded", "q_loaded", "o_loaded", "kv_weights_high", "q_weights_high", "o_weights_high",
                 "kv_weights_low", "q_weights_low", "o_weights_low", "ctx_high", "ctx_low", "xnT_psum", "xnT_high", "xnT_low",
                 "keyscale_ready", "stepped", "kv_psum", "q_psum", "rows_copied", "squared",
                 "ssq_ready", "gpsimd_steps", "rows_normed", "rowsT_psum", "rowsT_high", "rowsT_low", "values_high",
                 "values_low", "scores_psum", "max_ready", "exp_ready", "inverse_ready", "probs_ready", "probsT_psum",
                 "probsT_high", "probsT_low", "mix_psum", "mixT_high", "mixT_low", "out_psum", "out_added", "bisection")
        S_ = {x: k.sem(f"l2a_{x}") for x in names}
        S, T, V, R, J = k.bank[0:2], k.bank[2:4], k.bank[4], k.bank[5], k.bank[6:8]
        wq_dram = dram["wqT"].rearrange("(f p) (g c) -> g p f c", p=P, c=GW)
        wkv_dram = dram["wkvT"].rearrange("(f p) (g c) -> g p f c", p=P, c=2 * HD)
        wo_dram = dram["woT"].rearrange("(g h p) c -> g p h c", p=P, h=REP)
        batch = lambda step: step[1] % B

        def group(step):
            i, offset = step
            return offset // 2 if i is None else i + offset // 2

        def turned(step, c):
            b, source = batch(step), R[:, :]
            if c == 0:
                return [keysT[:, part, b * CTX:(b + 1) * CTX] for part in range(2)], source
            t = b * TPB + c - 1
            return ([headsT[:, part, :, t * P:(t + 1) * P] for part in range(2)],
                    source.rearrange("p (h q) -> p h q", h=REP))

        with nc.Block(no_gpsimd_drain=True) as block:

            @block.sync
            def _(sp):
                def load_kv(group):
                    sp.dma_start(raw_kv[:, :, :], wkv_dram[group]).then_inc(S_["kv_loaded"], 16)

                def load_q(group):
                    sp.dma_start(raw_q[:, :, :], wq_dram[group]).then_inc(S_["q_loaded"], 16)

                def load_o(group):
                    sp.dma_start(raw_o[:, :, :], wo_dram[group]).then_inc(S_["o_loaded"], 16)

                load_kv(0)
                load_q(0)
                sp.dma_start(mask[:, :, :], dram["mask_1x1xSxS2_ff0"][0, 0].rearrange("(t p) c -> p t c", p=P))\
                  .then_inc(S_["mask_loaded"], 16)
                for i, name in enumerate(("q_norm_w", "k_norm_w")):
                    sp.dma_start(weights[:, i:i + 1], dram["L2_xattn_" + name].unsqueeze(1)).then_inc(S_["mask_loaded"], 16)
                load_o(0)
                with sp.Fori(0, GROUPS) as i:
                    sp.wait_ge(S_["kv_weights_low"], i + 1)
                    load_kv(i + 1)
                    sp.wait_ge(S_["q_weights_low"], i + 1)
                    load_q(i + 1)
                    sp.wait_ge(S_["o_weights_low"], 2 * i + 2)
                    load_o(i + 1)

            @block.gpsimd
            def _(g):
                norm_gpsimd(k, n)

                def weights_low(target, source, high, value, done):
                    g.wait_ge(high, value)
                    g.tensor_tensor(target[:, 1], source, target[:, 0], ALU.subtract).then_inc(done, 1)

                def kv_weights_low(step):
                    weights_low(wkv, raw_kv[:, :, :], S_["kv_weights_high"], group(step) + 2, S_["kv_weights_low"])

                def q_weights_low(step):
                    weights_low(wq, raw_q[:, :, :], S_["q_weights_high"], group(step) + 2, S_["q_weights_low"])

                def o_weights_low(step, half):
                    heads = slice(half * REP // 2, (half + 1) * REP // 2)
                    if half == 0:
                        g.wait_ge(S_["o_weights_high"], group(step) + 1)
                    g.tensor_tensor(wo[:, 1, heads], raw_o[:, heads], wo[:, 0, heads], ALU.subtract)\
                     .then_inc(S_["o_weights_low"], 1)

                def square(step, c):
                    g.wait_ge(S_["rows_copied"], at(step, KV + TPB, KV + c))
                    if c == 2:
                        g.wait_ge(S_["ssq_ready"], at(step, CHUNKS, 1))
                    elif c == 0 and not is_start(step):
                        g.wait_ge(S_["ssq_ready"], at(step, CHUNKS, 0))
                    g.tensor_tensor(squares[:, c % 2, :], rows[:, c, :], rows[:, c, :], ALU.mult)\
                     .then_inc(S_["squared"], 1)

                def norm(step, own, c):
                    g.wait_ge(S_["ssq_ready"], at(step, CHUNKS, c + 1))
                    g.sem_inc(S_["stepped"], 1)
                    own(g.tensor_scalar(ssq[:, c, :], ssq[:, c, :], 1.0 / HD, EPS, ALU.mult, ALU.add))
                    own.wait()
                    own(g.tensor_tensor(ssq[:, c, :], ssq[:, c, :], k.minus_half[:, 0:REP], ALU.pow))
                    own.wait()
                    r = rows[:, c, :].rearrange("p (h d) -> p h d", d=HD)
                    g.tensor_tensor(r, r, ssq[:, c, :].unsqueeze(2).broadcast_to([P, REP, HD]), ALU.mult)\
                     .then_inc(S_["rows_normed"], 1)

                def run(step, last=False):
                    new_o_weights = step[1] % 2 == 1 and step[1] > 0
                    if new_o_weights:
                        o_weights_low(step, 0)
                        if last:
                            o_weights_low(step, 1)
                            return
                    following = after(step)
                    own = StepOwn(g, S_["gpsimd_steps"], following, OWN_P)
                    square(following, 0)
                    norm(following, own, 0)
                    if new_o_weights:
                        o_weights_low(step, 1)
                    square(following, 1)
                    if step[1] % 2 == 0:
                        kv_weights_low(step)
                    square(following, 2)
                    norm(following, own, 1)
                    norm(following, own, 2)
                    assert own.count == OWN_P
                    if step[1] % 2 == 0:
                        q_weights_low(step)

                weights_low(wkv, raw_kv[:, :, :], S_["kv_weights_high"], 1, S_["kv_weights_low"])
                weights_low(wq, raw_q[:, :, :], S_["q_weights_high"], 1, S_["q_weights_low"])
                run((None, -1))
                run((None, 0))
                with g.Fori(0, STEPS // 2 - 1) as i:
                    run((i, 1))
                    run((i, 2))
                run((None, STEPS - 1), last=True)

            @block.tensor
            def _(pe):
                def product(out, stationary, moving, half=None):
                    count = len(stationary)
                    tiles = range(count) if half is None else range(count)[half * count // 2:(half + 1) * count // 2]
                    for f in tiles:
                        for x, (a, b) in enumerate(PARTS):
                            last = pe.matmul(out, stationary[f][a], moving[f][b], start=f == 0 and x == 0,
                                             stop=f == count - 1 and x == 2)
                    return last

                def project_kv(step, j):
                    if step[0] is None and step[1] == 1:
                        pe.wait_ge(S_["rows_copied"], KV + j + 1)
                    elif not is_start(step):
                        pe.wait_ge(S_["out_added"], at(after(step, -2), TPB, j + 1))
                    for h in range(2):
                        r = batch(step) * CPB + 2 * j + h
                        last = product(J[j][:, h * 2 * HD:(h + 1) * 2 * HD],
                                       [[ctxT2[:, a, f, r * P:(r + 1) * P] for a in range(2)] for f in range(KT)],
                                       [[wkv[:, b, f, :] for b in range(2)] for f in range(KT)])
                    last.then_inc(S_["kv_psum"], 1)

                def project_q(step, t, half):
                    if half == 0:
                        pe.wait_ge(S_["values_low"], at(step, KV, t + 1))
                    token = (batch(step) * TPB + t) * P
                    last = product(J[t][:, :],
                                   [[xnT2[:, a, f, token:token + P] for a in range(2)] for f in range(KT)],
                                   [[wq[:, b, f, :] for b in range(2)] for f in range(KT)], half)
                    if half == 1:
                        last.then_inc(S_["q_psum"], 1)

                def project_out(step, t, half):
                    token = (batch(step) * TPB + t) * P
                    last = product(J[t][:, :],
                                   [[headsT[:, a, h, token:token + P] for a in range(2)] for h in range(REP)],
                                   [[wo[:, x, h, :] for x in range(2)] for h in range(REP)], half)
                    if half == 1:
                        last.then_inc(S_["out_psum"], 1)

                def turn_rows(step, c):
                    if c or not is_start(step):
                        pe.wait_ge(S_["rowsT_low"], at(step, CHUNKS, c))
                    pe.wait_ge(S_["rows_normed"], at(step, CHUNKS, c + 1))
                    for h in range(REP):
                        last = pe.transpose(R[:, h * P:(h + 1) * P], rows[:, c, h * P:(h + 1) * P], k.ident[:, :])
                    last.then_inc(S_["rowsT_psum"], 1)

                def scores(step, u):
                    h, q = u // TPB, u % TPB
                    if not is_start(step) or u >= 2:
                        pe.wait_ge(S_["max_ready"], at(step, UNITS, u - 1))
                    if u < TPB:
                        pe.wait_ge(S_["rowsT_low"], at(step, CHUNKS, u + 2))
                    b = batch(step)
                    token = (b * TPB + q) * P
                    product(S[u % 2][:, :], [[headsT[:, a, h, token:token + P] for a in range(2)]],
                            [[keysT[:, x, b * CTX:(b + 1) * CTX] for x in range(2)]]).then_inc(S_["scores_psum"], 1)

                def turn_probs(step, u):
                    if not is_start(step) or u >= 2:
                        pe.wait_ge(S_["probsT_low"], at(step, UNITS, u - 1))
                    pe.wait_ge(S_["probs_ready"], at(step, UNITS, u + 1))
                    for c in range(CPB):
                        last = pe.transpose(T[u % 2][:, c * P:(c + 1) * P], probs[:, u % 3, c * P:(c + 1) * P],
                                            k.ident[:, :])
                    last.then_inc(S_["probsT_psum"], 1)

                def mix(step, p):
                    if not is_start(step) or p >= 1:
                        pe.wait_ge(S_["mixT_low"], at(step, PAIRS, p))
                    pe.wait_ge(S_["probsT_low"], at(step, UNITS, 2 * p + 2))
                    product(V[:, 0:SEQ],
                            [[values[:, a, batch(step) * CPB + c, :] for a in range(2)] for c in range(CPB)],
                            [[probsT[:, x, p % 2, c, :] for x in range(2)] for c in range(CPB)])\
                        .then_inc(S_["mix_psum"], 1)

                def fill(step, u, first, last):
                    following, before = after(step), after(step, -1)
                    if not last:
                        if u == 0:
                            pe.wait_ge(S_["kv_weights_low"], group(following) + 1)
                        if u == 2:
                            pe.wait_ge(S_["q_weights_low"], group(following) + 1)
                        if u < KV:
                            project_kv(following, u)
                        if u == 2:
                            project_q(following, 0, 0)
                            project_q(following, 0, 1)
                        if u in (3, 4):
                            project_q(following, 1, u - 3)
                        if u == 5:
                            turn_rows(following, 0)
                    if not first:
                        if u == 5:
                            pe.wait_ge(S_["o_weights_low"], 2 * group(before) + 2)
                            pe.wait_ge(S_["mixT_low"], at(before, PAIRS, PAIRS))
                            free(following, before, 0, last)
                            project_out(before, 0, 0)
                            project_out(before, 0, 1)
                        if u == 6:
                            free(following, before, 1, last)
                            project_out(before, 1, 0)
                        if u == 7:
                            project_out(before, 1, 1)
                    if not last and u == 6:
                        turn_rows(following, 1)
                    if not last and u == 7:
                        turn_rows(following, 2)

                def free(following, before, t, last):
                    if last:
                        pe.wait_ge(S_["out_added"], at(before, TPB, t + 1))
                    else:
                        pe.wait_ge(S_["rows_copied"], at(following, KV + TPB, KV + t + 1))

                def run(step, first=False, last=False):
                    for u in range(UNITS):
                        fill(step, u, first, last)
                        turn_probs(step, u)
                        if u + 2 < UNITS:
                            scores(step, u + 2)
                        if u >= 2 and u % 2 == 0:
                            mix(step, u // 2 - 1)
                    if not last:
                        scores(after(step), 0)
                    mix(step, PAIRS - 1)
                    if not last:
                        scores(after(step), 1)

                norm_tensor_two(k, n, T, S_["xnT_psum"], S_["xnT_low"])
                pe.wait_ge(S_["xnT_low"], TILES)
                pe.wait_ge(S_["ctx_low"], CTILES)
                pe.wait_ge(S_["kv_weights_low"], 1)
                start = (None, 0)
                for j in range(KV):
                    project_kv(start, j)
                pe.wait_ge(S_["q_weights_low"], 1)
                for t in range(TPB):
                    project_q(start, t, 0)
                    project_q(start, t, 1)
                for c in range(CHUNKS):
                    turn_rows(start, c)
                scores(start, 0)
                scores(start, 1)
                run(start, first=True)
                with pe.Fori(0, STEPS // 2 - 1) as i:
                    run((i, 1))
                    run((i, 2))
                run((None, STEPS - 1), last=True)
                for t in range(TPB):
                    if t == 0:
                        pe.wait_ge(S_["mixT_low"], PAIRS * STEPS)
                    pe.wait_ge(S_["out_added"], TPB * (STEPS - 1) + t + 1)
                    project_out((None, STEPS - 1), t, 0)
                    project_out((None, STEPS - 1), t, 1)

            @block.scalar
            def _(a):
                def copy_kv(step, j):
                    a.wait_ge(S_["kv_psum"], at(step, KV, j + 1))
                    both = J[j][:, :].rearrange("p (r c) -> p r c", r=2)
                    a.copy(rows[:, 0, j * 2 * HD:(j + 1) * 2 * HD].rearrange("p (r c) -> p r c", r=2),
                           both[:, :, 0:HD]).then_inc(S_["rows_copied"], 1)
                    r = batch(step) * CPB + 2 * j
                    a.copy(values[:, 0, r:r + 2, :], both[:, :, HD:2 * HD]).then_inc(S_["values_high"], 1)

                def copy_q(step, t):
                    a.wait_ge(S_["q_psum"], at(step, TPB, t + 1))
                    a.copy(rows[:, 1 + t, :], J[t][:, :]).then_inc(S_["rows_copied"], 1)

                def rowsT_high(step, c):
                    a.wait_ge(S_["rowsT_psum"], at(step, CHUNKS, c + 1))
                    (high, _), source = turned(step, c)
                    if c == 0:
                        a.activation(high, source, ACT.Copy, scale=keyscale[:, 0:1]).then_inc(S_["rowsT_high"], 1)
                    else:
                        a.copy(high, source).then_inc(S_["rowsT_high"], 1)

                def exponentials(step, u):
                    a.wait_ge(S_["max_ready"], at(step, UNITS, u + 1))
                    if u >= 3:
                        a.wait_ge(S_["probsT_psum"], at(step, UNITS, u - 2))
                    elif not is_start(step):
                        a.wait_ge(S_["probsT_psum"], at(step, UNITS, min(u - 1, 0)))
                    a.activation(probs[:, u % 3, :], masked[:, u % 2, :], ACT.Exp, bias=negmax[:, u:u + 1],
                                 scale=-1.0, accum_out=sums[:, u:u + 1]).then_inc(S_["exp_ready"], 1)

                def divide(step, u):
                    a.wait_ge(S_["inverse_ready"], at(step, UNITS, u + 1))
                    a.activation(probs[:, u % 3, :], probs[:, u % 3, :], ACT.Copy, scale=inverse[:, u:u + 1])\
                     .then_inc(S_["probs_ready"], 1)

                def probsT_high(step, u):
                    p = u // 2
                    a.wait_ge(S_["probsT_psum"], at(step, UNITS, u + 1))
                    if not is_start(step) or p >= 2:
                        a.wait_ge(S_["mix_psum"], at(step, PAIRS, p - 1))
                    a.copy(probsT[:, 0, p % 2, :, u % 2 * P:(u % 2 + 1) * P],
                           T[u % 2][:, :].rearrange("p (c q) -> p c q", c=CPB)).then_inc(S_["probsT_high"], 1)

                def mixT_high(step, p):
                    b = batch(step)
                    a.wait_ge(S_["mix_psum"], at(step, PAIRS, p + 1))
                    a.copy(headsT[:, 0, p, b * SEQ:(b + 1) * SEQ], V[:, 0:SEQ]).then_inc(S_["mixT_high"], 1)

                def kv_weights_high(group):
                    a.wait_ge(S_["kv_loaded"], 16 * group + 16)
                    a.copy(wkv[:, 0], raw_kv[:, :, :]).then_inc(S_["kv_weights_high"], 1)

                def q_weights_high(group):
                    a.wait_ge(S_["q_loaded"], 16 * group + 16)
                    a.copy(wq[:, 0], raw_q[:, :, :]).then_inc(S_["q_weights_high"], 1)

                def o_weights_high(step):
                    a.wait_ge(S_["o_loaded"], 16 * group(step) + 16)
                    if not is_start(after(step, -1)):
                        a.wait_ge(S_["out_psum"], at(after(step, -2), TPB, TPB))
                    a.copy(wo[:, 0], raw_o[:, :, :]).then_inc(S_["o_weights_high"], 1)

                def run(step, last=False):
                    following = after(step)
                    for u in range(UNITS):
                        if u + 1 < UNITS:
                            exponentials(step, u + 1)
                        if u:
                            probsT_high(step, u - 1)
                        divide(step, u)
                        if u % 2 == 1 and u >= 3:
                            mixT_high(step, u // 2 - 1)
                        if not last:
                            if u < KV:
                                copy_kv(following, u)
                            if u == 2:
                                copy_q(following, 0)
                            if u == 4:
                                copy_q(following, 1)
                            if u in (5, 6, 7):
                                rowsT_high(following, u - 5)
                            if step[1] % 2 == 0 and u == 3:
                                kv_weights_high(group(step) + 1)
                            if step[1] % 2 == 0 and u == 5:
                                q_weights_high(group(step) + 1)
                        if step[1] % 2 == 1 and u == 1:
                            o_weights_high(step)
                    probsT_high(step, UNITS - 1)
                    if not last:
                        exponentials(following, 0)
                    mixT_high(step, PAIRS - 1)

                kv_weights_high(0)
                for r in range(CTILES):
                    a.activation(row_tile(ctxT2[:, 0], r), row_tile(k.ctxT, r), ACT.Copy, scale=k.sign[:, r:r + 1])\
                     .then_inc(S_["ctx_high"], 1)
                q_weights_high(0)
                for t in range(TILES):
                    a.wait_ge(S_["xnT_psum"], t + 1)
                    a.copy(xnT2[:, 0, :, t * P:(t + 1) * P], T[t % 2][:, :].rearrange("p (f c) -> p f c", f=KT))\
                     .then_inc(S_["xnT_high"], 1)
                a.wait_ge(S_["keyscale_ready"], 1)
                start = (None, 0)
                for j in range(KV):
                    copy_kv(start, j)
                for t in range(TPB):
                    copy_q(start, t)
                for c in range(CHUNKS):
                    rowsT_high(start, c)
                exponentials(start, 0)
                run(start)
                with a.Fori(0, STEPS // 2 - 1) as i:
                    run((i, 1))
                    run((i, 2))
                run((None, STEPS - 1), last=True)

            @block.vector
            def _(v):
                def values_low(step, j):
                    v.wait_ge(S_["values_high"], at(step, KV, j + 1))
                    r = batch(step) * CPB + 2 * j
                    v.tensor_tensor(values[:, 1, r:r + 2, :], J[j][:, :].rearrange("p (r c) -> p r c", r=2)[:, :, HD:2 * HD],
                                    values[:, 0, r:r + 2, :], ALU.subtract).then_inc(S_["values_low"], 1)

                def sum_squares(step, c):
                    v.wait_ge(S_["squared"], at(step, CHUNKS, c + 1))
                    v.tensor_reduce(ssq[:, c, :], squares[:, c % 2, :].rearrange("p (h d) -> p h d", d=HD),
                                    AX.X, ALU.add).then_inc(S_["ssq_ready"], 1)

                def rowsT_low(step, c):
                    v.wait_ge(S_["rowsT_high"], at(step, CHUNKS, c + 1))
                    (high, low), source = turned(step, c)
                    if c == 0:
                        v.scalar_tensor_tensor(low, source, keyscale[:, 0:1], high, ALU.mult, ALU.subtract)\
                         .then_inc(S_["rowsT_low"], 1)
                    else:
                        v.tensor_tensor(low, source, high, ALU.subtract).then_inc(S_["rowsT_low"], 1)

                def maximum(step, u):
                    v.wait_ge(S_["scores_psum"], at(step, UNITS, u + 1))
                    v.sem_inc(S_["stepped"], 1)
                    v.tensor_tensor_reduce(masked[:, u % 2, :], S[u % 2][:, :], mask[:, u % TPB, :], -1.0, 3.4e38,
                                           ALU.add, ALU.min, negmax[:, u:u + 1]).then_inc(S_["max_ready"], 1)

                def invert(step, u):
                    v.wait_ge(S_["exp_ready"], at(step, UNITS, u + 1))
                    v.reciprocal(inverse[:, u:u + 1], sums[:, u:u + 1]).then_inc(S_["inverse_ready"], 1)

                def probsT_low(step, u):
                    p = u // 2
                    v.wait_ge(S_["probsT_high"], at(step, UNITS, u + 1))
                    columns = slice(u % 2 * P, (u % 2 + 1) * P)
                    v.tensor_tensor(probsT[:, 1, p % 2, :, columns], T[u % 2][:, :].rearrange("p (c q) -> p c q", c=CPB),
                                    probsT[:, 0, p % 2, :, columns], ALU.subtract).then_inc(S_["probsT_low"], 1)

                def mixT_low(step, p):
                    b = batch(step)
                    v.wait_ge(S_["mixT_high"], at(step, PAIRS, p + 1))
                    v.tensor_tensor(headsT[:, 1, p, b * SEQ:(b + 1) * SEQ], V[:, 0:SEQ],
                                    headsT[:, 0, p, b * SEQ:(b + 1) * SEQ], ALU.subtract).then_inc(S_["mixT_low"], 1)

                def add_out(step, t):
                    v.wait_ge(S_["out_psum"], at(step, TPB, t + 1))
                    tile = batch(step) * TPB + t
                    v.tensor_tensor(k.x[:, tile, :], J[t][:, :], k.x[:, tile, :], ALU.add).then_inc(S_["out_added"], 1)

                def run(step, first=False, last=False):
                    following, before = after(step), after(step, -1)
                    own = StepOwn(v, S_["bisection"], step, OWN_V)
                    for u in range(UNITS):
                        if u + 1 < UNITS:
                            maximum(step, u + 1)
                        for c in range(ROUNDS * u // 2, ROUNDS * (u + 1) // 2):
                            bisection_count(k, own, c % REP)
                        invert(step, u)
                        if u:
                            probsT_low(step, u - 1)
                        if ROUNDS * (u + 1) % UNITS == 0:
                            bisection_update(k, own)
                        if u % 2 == 1 and u >= 3:
                            mixT_low(step, u // 2 - 1)
                        if not last:
                            if u < KV:
                                values_low(following, u)
                            if u in (3, 4, 5):
                                sum_squares(following, u - 3)
                            if u in (5, 6, 7):
                                rowsT_low(following, u - 5)
                        if not first and u in (5, 7):
                            add_out(before, (u - 5) // 2)
                    probsT_low(step, UNITS - 1)
                    if not last:
                        maximum(following, 0)
                    mixT_low(step, PAIRS - 1)
                    assert own.count == OWN_V, own.count

                norm_vector(k, n)
                for r in range(CTILES):
                    v.wait_ge(S_["ctx_high"], r + 1)
                    v.scalar_tensor_tensor(row_tile(ctxT2[:, 1], r), row_tile(k.ctxT, r), k.sign[:, r:r + 1],
                                           row_tile(ctxT2[:, 0], r), ALU.mult, ALU.subtract).then_inc(S_["ctx_low"], 1)
                for t in range(TILES):
                    v.wait_ge(S_["xnT_high"], t + 1)
                    v.tensor_tensor(xnT2[:, 1, :, t * P:(t + 1) * P], T[t % 2][:, :].rearrange("p (f c) -> p f c", f=KT),
                                    xnT2[:, 0, :, t * P:(t + 1) * P], ALU.subtract).then_inc(S_["xnT_low"], 1)
                v.wait_ge(S_["mask_loaded"], 48)
                v.scalar_tensor_tensor(keyscale[:, 0:1], weights[:, 0:1], SCALE, weights[:, 1:2], ALU.mult, ALU.mult)\
                 .then_inc(S_["keyscale_ready"], 1)
                start = (None, 0)
                for j in range(KV):
                    values_low(start, j)
                for c in range(CHUNKS):
                    sum_squares(start, c)
                for c in range(CHUNKS):
                    rowsT_low(start, c)
                maximum(start, 0)
                v.sem_inc(S_["out_added"], TPB)
                run(start, first=True)
                with v.Fori(0, STEPS // 2 - 1) as i:
                    run((i, 1))
                    run((i, 2))
                run((None, STEPS - 1), last=True)
                for t in range(TPB):
                    add_out((None, STEPS - 1), t)
                v.wait_ge(S_["out_added"], TPB * (STEPS + 1))
                v.wait_ge(S_["bisection"], STEPS * OWN_V)


def norm_tensor_two(k, n, banks, in_psum, low_ready):
    pe = k.nc.tensor
    for t in range(TILES):
        pe.wait_ge(k.xn_ready, TILES * n + t + 1)
        if t >= 2:
            pe.wait_ge(low_ready, t - 1)
        for f in range(KT):
            last = pe.transpose(banks[t % 2][:, f * P:(f + 1) * P], k.xn[:, t, f * P:(f + 1) * P], k.ident[:, :])
        last.then_inc(in_psum, 1)



TOPK = 154
BISECT_PER_ROUND = 8 + 5


def bisection_buffers(k):
    k.sign = k.sbuf("sign", [P, CTILES], F32)
    k.rank = k.sbuf("rank", [P, CTILES], F32)
    k.counts = k.sbuf("counts", [P, CTILES], F32)
    k.found = k.sbuf("found", [P, CTILES], I32)
    k.candidate = k.sbuf("candidate", [P, CTILES], I32)
    k.bit = k.sbuf("bit", [P, CTILES], I32)
    k.enough = k.sbuf("enough", [P, CTILES], F32)
    k.set_bit = k.sbuf("set_bit", [P, CTILES], I32)


def row_tile(ctxT, r):
    return ctxT[:, r // B, r % B * CTX:(r % B + 1) * CTX]


def bisection_start(k):
    v, own = k.nc.vector, k.vown
    for r in range(CTILES):
        if r >= 2:
            own.wait()
        own(v.tensor_scalar(k.flags[:, r % 2], row_tile(k.ctxT, r), 0.0, 0.0, ALU.is_ge, ALU.add,
                            accum_out=k.counts[:, r:r + 1]))
    own(v.memset(k.found[:, :], 0))
    own(v.memset(k.bit[:, :], 2 ** 30))
    own(v.memset(k.candidate[:, :], 2 ** 30))
    own.wait()
    own(v.tensor_scalar(k.enough[:, :], k.counts[:, :], float(TOPK), None, ALU.is_lt))
    own.wait()
    own(v.tensor_scalar(k.sign[:, :], k.enough[:, :], -2.0, 1.0, ALU.mult, ALU.add))
    own(v.tensor_scalar(k.rank[:, :], k.enough[:, :], float(CTX + 1 - 2 * TOPK), float(TOPK), ALU.mult, ALU.add))
    own.wait()
    for r in range(CTILES):
        own(v.tensor_scalar(row_tile(k.ctxT, r), row_tile(k.ctxT, r), k.sign[:, r:r + 1], None, ALU.mult))
    own.wait()


def bisection_count(k, own, j):
    own.wait()
    for r in (2 * j, 2 * j + 1):
        own(k.nc.vector.tensor_scalar(k.flags[:, r % 2], row_tile(k.ctxT, r), k.candidate[:, r:r + 1].bitcast(F32), 0.0,
                                      ALU.is_ge, ALU.add, accum_out=k.counts[:, r:r + 1]))


def bisection_update(k, own):
    v = k.nc.vector
    own.wait()
    own(v.tensor_tensor(k.enough[:, :], k.counts[:, :], k.rank[:, :], ALU.is_ge))
    own.wait()
    own(v.tensor_tensor(k.set_bit[:, :], k.enough[:, :], k.bit[:, :], ALU.mult))
    own.wait()
    own(v.tensor_tensor(k.found[:, :], k.found[:, :], k.set_bit[:, :], ALU.bitwise_or))
    own(v.tensor_scalar(k.bit[:, :], k.bit[:, :], 1, None, ALU.logical_shift_right))
    own.wait()
    own(v.tensor_tensor(k.candidate[:, :], k.found[:, :], k.bit[:, :], ALU.bitwise_or))



def layer3_attention(k, dram):
    nc, n, m = k.nc, k.norms, k.turned
    k.norms += 1
    k.turned += 1
    TAPS, BRANCHES = 7, 2
    HALF = TAPS // 2
    with ExitStack() as s:
        conv = k.sbuf("conv", [P, 2 * TAPS], F32, s)
        gamma = k.sbuf("bn_gamma", [P, 1], F32, s)
        beta = k.sbuf("bn_beta", [P, 1], F32, s)
        distance = k.sbuf("distance", [P, 3, P], F32, s)
        band = k.sbuf("band", [P, 2, 3, P], F32, s)
        term = k.sbuf("term", [P, 2, 3, P], F32, s)
        plain = k.sbuf("plain", [P, 2, CTX], F32, s)
        greater = k.sbuf("greater", [P, 2, CTX], F32, s)
        equal = k.sbuf("equal", [P, 2, SEQ], F32, s)
        prefix = k.sbuf("prefix", [P, 2, SEQ], F32, s)
        zeros = k.sbuf("zeros", [P, SEQ], F32, s)
        limit = k.sbuf("limit", [P, CTILES], F32, s)
        above = k.sbuf("above", [P, CTILES], F32, s)
        left = k.sbuf("left", [P, CTILES], F32, s)
        chosen = k.sbuf("chosen", [P, KT, B, SEQ], F32, s)
        parts = k.sbuf("parts", [P, BRANCHES, KT, B, SEQ], F32, s)
        gated = k.sbuf("gated", [P, BRANCHES, KT, B, SEQ], F32, s)
        features = k.sbuf("features", [P, 2, KT, BRANCHES, B], F32, s)
        z = k.sbuf("z", [P, KT, BRANCHES, B], F32, s)
        sq = k.sbuf("sq", [P, KT, BRANCHES, B], F32, s)
        moment = k.sbuf("moment", [P, BRANCHES], F32, s)
        rstd = k.sbuf("rstd3", [P, BRANCHES], F32, s)
        names = ("loaded", "distance_ready", "band_ready", "features_ready", "z_psum", "z_ready", "sum_psum", "sq_ready",
                 "sumsq_psum", "var_ready", "rstd_ready", "relu_ready", "exp_ready", "gated_ready", "back_psum")
        S_ = {x: k.sem(f"l3a_{x}") for x in names}
        with nc.Block(no_gpsimd_drain=True) as block:

            @block.sync
            def _(sp):
                sp.dma_start(conv[:, :], dram["L3_xattn_conv_w"].rearrange("a c t -> a (c t)").broadcast_to([P, 2 * TAPS]))\
                  .then_inc(S_["loaded"], 16)
                for target, name in ((gamma, "gamma"), (beta, "beta")):
                    sp.dma_start(target[:, :], dram["L3_xattn_bn_" + name].unsqueeze(0).broadcast_to([P, 1]))\
                      .then_inc(S_["loaded"], 16)

            @block.gpsimd
            def _(g):
                norm_gpsimd(k, n)
                g.iota(distance[:, :, :], [[P, 3], [-1, P]], base=-P, channel_multiplier=1,
                       allow_small_or_imprecise_dtypes=True).then_inc(S_["distance_ready"], 1)
                g.wait_ge(S_["distance_ready"], 1)
                g.wait_ge(S_["loaded"], 48)
                for c in range(2):
                    for tap in range(TAPS):
                        w = conv[:, c * TAPS + tap:c * TAPS + tap + 1]
                        target = band[:, c] if tap == 0 else term[:, tap % 2]
                        k.pown(g.tensor_scalar(target, distance[:, :, :], float(tap - HALF), w, ALU.is_equal, ALU.mult))
                        k.pown.wait()
                        if tap:
                            k.pown(g.tensor_tensor(band[:, c], band[:, c], target, ALU.add))
                            k.pown.wait()
                g.engine_nop().then_inc(S_["band_ready"], 1)
                g.wait_ge(S_["var_ready"], 1)
                g.tensor_tensor(rstd[:, :], moment[:, :], k.minus_half[:, 0:BRANCHES], ALU.pow).then_inc(S_["rstd_ready"], 1)

            @block.vector
            def _(v):
                norm_vector(k, n)
                own = k.vown
                own(v.memset(zeros[:, :], 0.0))
                own(v.tensor_tensor(limit[:, :], k.found[:, :].bitcast(F32), k.sign[:, :], ALU.mult))
                own.wait()
                for r in range(0, CTILES, 2):
                    two = (0, 1)
                    for j in two:
                        own(v.tensor_scalar(plain[:, j, :], row_tile(k.ctxT, r + j), k.sign[:, r + j:r + j + 1], None, ALU.mult))
                    own.wait()
                    for j in two:
                        own(v.tensor_scalar(greater[:, j, :], plain[:, j, :], limit[:, r + j:r + j + 1], 0.0,
                                            ALU.is_gt, ALU.add, accum_out=above[:, r + j:r + j + 1]))
                        own(v.tensor_scalar(equal[:, j, :], plain[:, j, 0:SEQ], limit[:, r + j:r + j + 1], None, ALU.is_equal))
                    own.wait()
                    for j in two:
                        own(v.tensor_tensor_scan(prefix[:, j, :], equal[:, j, :], zeros[:, :], 0.0, ALU.add, ALU.add))
                    own(v.tensor_scalar(left[:, r:r + 2], above[:, r:r + 2], -1.0, float(TOPK), ALU.mult, ALU.add))
                    own.wait()
                    for j in two:
                        own(v.scalar_tensor_tensor(equal[:, j, :], prefix[:, j, :], left[:, r + j:r + j + 1], equal[:, j, :],
                                                   ALU.is_le, ALU.mult))
                    own.wait()
                    for j in two:
                        own(v.tensor_tensor(chosen[:, (r + j) // B, (r + j) % B, :], greater[:, j, 0:SEQ], equal[:, j, :], ALU.add))
                own.wait()
                v.wait_ge(k.xnT_ready, TILES * (m + 1))
                flat = lambda a: a.rearrange("p f b c -> p (f b c)")
                xnT = k.xnT[:, :, :].rearrange("p f c -> p (f c)")
                own(v.tensor_tensor(flat(parts[:, 0]), flat(chosen[:, :, :, :]), xnT, ALU.mult))
                own.wait()
                own(v.tensor_tensor(flat(parts[:, 1]), xnT, flat(parts[:, 0]), ALU.subtract))
                own.wait()
                for branch, count in ((0, TOPK), (1, SEQ - TOPK)):
                    own(v.tensor_reduce(features[:, 0, :, branch, :], parts[:, branch], AX.X, ALU.max))
                    own(v.tensor_reduce(features[:, 1, :, branch, :], parts[:, branch], AX.X, ALU.add))
                    own.wait()
                    own(v.tensor_scalar(features[:, 1, :, branch, :], features[:, 1, :, branch, :], 1.0 / SEQ, SEQ / count,
                                        ALU.mult, ALU.mult))
                own.wait()
                v.engine_nop().then_inc(S_["features_ready"], 1)
                v.wait_ge(S_["z_psum"], 1)
                spread = lambda a: a.unsqueeze(1).unsqueeze(3).broadcast_to([P, KT, BRANCHES, B])
                v.tensor_copy(z[:, :, :, :].rearrange("p f r b -> p (f r b)"), k.bank[2][:, 0:16]).then_inc(S_["z_ready"], 1)
                v.wait_ge(S_["z_ready"], 1)
                v.wait_ge(S_["sum_psum"], 1)
                own(v.tensor_reduce(moment[:, :], k.bank[3][:, 0:16].rearrange("p (f r b) -> p r f b", f=KT, r=BRANCHES),
                                    AX.XY, ALU.add))
                own.wait()
                own(v.tensor_scalar(moment[:, :], moment[:, :], 1.0 / (B * D), None, ALU.mult))
                own.wait()
                own(v.tensor_tensor(z[:, :, :, :], z[:, :, :, :], spread(moment[:, :]), ALU.subtract))
                own.wait()
                v.tensor_tensor(sq[:, :, :, :], z[:, :, :, :], z[:, :, :, :], ALU.mult).then_inc(S_["sq_ready"], 1)
                v.wait_ge(S_["sumsq_psum"], 1)
                own(v.tensor_reduce(moment[:, :], k.bank[4][:, 0:16].rearrange("p (f r b) -> p r f b", f=KT, r=BRANCHES),
                                    AX.XY, ALU.add))
                own.wait()
                v.tensor_scalar(moment[:, :], moment[:, :], 1.0 / (B * D), EPS, ALU.mult, ALU.add).then_inc(S_["var_ready"], 1)
                v.wait_ge(S_["rstd_ready"], 1)
                own(v.tensor_tensor(z[:, :, :, :], z[:, :, :, :], spread(rstd[:, :]), ALU.mult))
                own.wait()
                v.wait_ge(S_["loaded"], 48)
                own(v.tensor_scalar(z[:, :, :, :], z[:, :, :, :], gamma[:, 0:1], beta[:, 0:1], ALU.mult, ALU.add))
                own.wait()
                v.tensor_scalar(z[:, :, :, :], z[:, :, :, :], 0.0, None, ALU.max).then_inc(S_["relu_ready"], 1)
                v.wait_ge(S_["exp_ready"], 1)
                own(v.tensor_scalar(sq[:, :, :, :], sq[:, :, :, :], 1.0, None, ALU.add))
                own.wait()
                own(v.reciprocal(z[:, :, :, :], sq[:, :, :, :]))
                own.wait()
                for branch in range(BRANCHES):
                    own(v.tensor_tensor(gated[:, branch], parts[:, branch],
                                        z[:, :, branch, :].unsqueeze(3).broadcast_to([P, KT, B, SEQ]), ALU.mult))
                own.wait()
                v.tensor_tensor(flat(gated[:, 0]), flat(gated[:, 0]), flat(gated[:, 1]), ALU.add).then_inc(S_["gated_ready"], 1)
                for t in range(TILES):
                    v.wait_ge(S_["back_psum"], t + 1)
                    own(v.tensor_tensor(k.x[:, t, :], k.bank[4 + t][:, :], k.x[:, t, :], ALU.add))
                own.wait()

            @block.scalar
            def _(a):
                norm_scalar(k, m, k.bank[0:2])
                a.wait_ge(S_["relu_ready"], 1)
                a.activation(sq[:, :, :, :], z[:, :, :, :], ACT.Exp, scale=-1.0).then_inc(S_["exp_ready"], 1)

            @block.tensor
            def _(pe):
                norm_tensor(k, n, m, k.bank[0:2])
                pe.wait_ge(S_["band_ready"], 1)
                pe.wait_ge(S_["features_ready"], 1)
                for f in range(KT):
                    terms = [(c, blk) for c in range(2) for blk in range(3) if 0 <= f + blk - 1 < KT]
                    for j, (c, blk) in enumerate(terms):
                        last = pe.matmul(k.bank[2][:, f * 4:f * 4 + 4], band[:, c, blk, :],
                                         features[:, c, f + blk - 1].rearrange("p r b -> p (r b)"),
                                         start=j == 0, stop=j == len(terms) - 1)
                last.then_inc(S_["z_psum"], 1)
                for source, ready, bank, done in ((z, "z_ready", 3, "sum_psum"), (sq, "sq_ready", 4, "sumsq_psum")):
                    pe.wait_ge(S_[ready], 1)
                    pe.matmul(k.bank[bank][:, 0:16], k.ones[:, :], source[:, :, :, :].rearrange("p f r b -> p (f r b)"),
                              start=True, stop=True).then_inc(S_[done], 1)
                pe.wait_ge(S_["gated_ready"], 1)
                for t in range(TILES):
                    for f in range(KT):
                        last = pe.transpose(k.bank[4 + t][:, f * P:(f + 1) * P],
                                            gated[:, 0, f, t // TPB, t % TPB * P:(t % TPB + 1) * P], k.ident[:, :])
                    last.then_inc(S_["back_psum"], 1)



def layer2_ffn(k, dram):
    nc, n, m = k.nc, k.norms, k.turned
    k.norms += 1
    k.turned += 1
    E, TOP = 64, 8
    with ExitStack() as s:
        router = k.sbuf("router", [P, KT, E], F32, s)
        rbias = k.sbuf("rbias", [P, E], F32, s)
        ebias = k.sbuf("ebias", [E, D], F32, s)
        logits = k.sbuf("logits", [P, TILES, E], F32, s)
        shifted = k.sbuf("shifted", [P, TILES, E], F32, s)
        expd = k.sbuf("expd", [P, TILES, E], F32, s)
        top = k.sbuf("top", [P, TILES], F32, s)
        total = k.sbuf("total", [P, TILES], F32, s)
        scores = k.sbuf("scores", [P, TILES, E], F32, s)
        rest = k.sbuf("rest", [P, TILES, E], F32, s)
        best = k.sbuf("best", [P, TILES, TOP], F32, s)
        wsum = k.sbuf("wsum", [P, TILES], F32, s)
        dense = k.sbuf("dense", [P, TILES, E], F32, s)
        denseT = k.sbuf("denseT", [E, TILES * P], F32, s)
        loaded, logits_psum, shifted_ready, expd_ready, dense_ready, denseT_psum, denseT_ready, mix_psum = (
            k.sem(f"l2f_{x}") for x in ("loaded", "logits_psum", "shifted_ready", "expd_ready", "dense_ready",
                                        "denseT_psum", "denseT_ready", "mix_psum"))
        with nc.Block(no_gpsimd_drain=True) as block:

            @block.sync
            def _(sp):
                sp.dma_start(router[:, :, :], dram["routerT"].rearrange("(f p) e -> p f e", p=P)).then_inc(loaded, 16)
                sp.dma_start(rbias[:, :], dram["L2_ffn_router_bias"].unsqueeze(0).broadcast_to([P, E])).then_inc(loaded, 16)
                sp.dma_start(ebias[:, :], dram["L2_ffn_expert_bias"]).then_inc(loaded, 16)

            @block.gpsimd
            def _(g):
                norm_gpsimd(k, n)

            @block.tensor
            def _(pe):
                norm_tensor(k, n, m, k.bank[0:2])
                pe.wait_ge(loaded, 48)
                for t in range(TILES):
                    pe.wait_ge(k.xnT_ready, TILES * m + t + 1)
                    for f in range(KT):
                        last = pe.matmul(k.bank[2][:, t * E:(t + 1) * E], k.xnT[:, f, t * P:(t + 1) * P],
                                         router[:, f, :], start=f == 0, stop=f == KT - 1)
                last.then_inc(logits_psum, 1)
                pe.wait_ge(dense_ready, 1)
                for t in range(TILES):
                    last = pe.transpose(k.bank[3][0:E, t * P:(t + 1) * P], dense[:, t, :], k.ident[:, :])
                last.then_inc(denseT_psum, 1)
                pe.wait_ge(denseT_ready, 1)
                for t in range(TILES):
                    pe.matmul(k.bank[4 + t][:, :], denseT[:, t * P:(t + 1) * P], ebias[:, :],
                              start=True, stop=True).then_inc(mix_psum, 1)

            @block.vector
            def _(v):
                norm_vector(k, n)
                spread = lambda a: a[:, :].unsqueeze(2).broadcast_to([P, TILES, E])
                v.wait_ge(loaded, 48)
                v.wait_ge(logits_psum, 1)
                k.vown(v.tensor_tensor(logits[:, :, :], k.bank[2][:, 0:TILES * E].rearrange("p (t e) -> p t e", e=E),
                                       rbias[:, :].unsqueeze(1).broadcast_to([P, TILES, E]), ALU.add))
                k.vown.wait()
                k.vown(v.tensor_reduce(top[:, :], logits[:, :, :], AX.X, ALU.max))
                k.vown.wait()
                v.tensor_tensor(shifted[:, :, :], logits[:, :, :], spread(top), ALU.subtract).then_inc(shifted_ready, 1)
                v.wait_ge(expd_ready, 1)
                k.vown(v.tensor_reduce(total[:, :], expd[:, :, :], AX.X, ALU.add))
                k.vown.wait()
                k.vown(v.reciprocal(total[:, :], total[:, :]))
                k.vown.wait()
                k.vown(v.tensor_tensor(scores[:, :, :], expd[:, :, :], spread(total), ALU.mult))
                k.vown.wait()
                for t in range(TILES):
                    k.vown(v.max(best[:, t, :], scores[:, t, :]))
                k.vown.wait()
                for t in range(TILES):
                    k.vown(v.match_replace(rest[:, t, :], best[:, t, :], scores[:, t, :], 0.0))
                k.vown(v.tensor_reduce(wsum[:, :], best[:, :, :], AX.X, ALU.add))
                k.vown.wait()
                v.tensor_tensor(dense[:, :, :], scores[:, :, :], rest[:, :, :], ALU.subtract).then_inc(dense_ready, 1)
                for t in range(TILES):
                    k.vown(v.scalar_tensor_tensor(k.x[:, t, :], k.xn[:, t, :], wsum[:, t:t + 1], k.x[:, t, :],
                                                  ALU.mult, ALU.add))
                k.vown.wait()
                for t in range(TILES):
                    v.wait_ge(mix_psum, t + 1)
                    k.vown(v.tensor_tensor(k.x[:, t, :], k.bank[4 + t][:, :], k.x[:, t, :], ALU.add))
                k.vown.wait()

            @block.scalar
            def _(a):
                norm_scalar(k, m, k.bank[0:2])
                a.wait_ge(shifted_ready, 1)
                a.activation(expd[:, :, :], shifted[:, :, :], ACT.Exp).then_inc(expd_ready, 1)
                a.wait_ge(denseT_psum, 1)
                a.copy(denseT[:, :], k.bank[3][0:E, :]).then_inc(denseT_ready, 1)



def layer3_ffn(k, dram):
    nc, n, m = k.nc, k.norms, k.turned
    k.norms += 1
    k.turned += 1
    E, R, TOP = 8, 16, 2
    SCALING = 2.0
    with ExitStack() as s:
        wb = k.sbuf("wb", [P, KT, D], F32, s)
        wra = k.sbuf("wra", [P, KT, E + E * R], F32, s)
        bm = k.sbuf("bm", [E * R, D], F32, s)
        bias = k.sbuf("bias3", [P, D], F32, s)
        lower = k.sbuf("lower", [P, E, E], F32, s)
        logits = k.sbuf("logits3", [P, TILES, E], F32, s)
        expd = k.sbuf("expd3", [P, TILES, E], F32, s)
        top = k.sbuf("top3", [P, TILES], F32, s)
        total = k.sbuf("total3", [P, TILES], F32, s)
        probs = k.sbuf("probs3", [P, TILES, E], F32, s)
        more = k.sbuf("more", [P, TILES, E, E], F32, s)
        same = k.sbuf("same", [P, TILES, E, E], F32, s)
        rank = k.sbuf("rank", [P, TILES, E], F32, s)
        weight = k.sbuf("weight3", [P, TILES, E], F32, s)
        low = k.sbuf("low", [P, TILES, E * R], F32, s)
        lowT = k.sbuf("lowT", [E * R, TILES * P], F32, s)
        loaded, lower_zeroed, lower_ready, low_psum, shifted_ready, expd_ready, low_ready, lowT_psum, lowT_ready, \
            out_psum = (k.sem(f"l3f_{x}") for x in (
                "loaded", "lower_zeroed", "lower_ready", "low_psum", "shifted_ready", "expd_ready", "low_ready",
                "lowT_psum", "lowT_ready", "out_psum"))
        with nc.Block(no_gpsimd_drain=True) as block:

            @block.sync
            def _(sp):
                sp.dma_start(bias[:, :], dram["L3_ffn_bias"].unsqueeze(0).broadcast_to([P, D])).then_inc(loaded, 16)
                sp.dma_start(wra[:, :, :], dram["wraT"].rearrange("(f p) c -> p f c", p=P)).then_inc(loaded, 16)
                sp.dma_start(wb[:, :, :], dram["wbT"].rearrange("(f p) c -> p f c", p=P)).then_inc(loaded, 16)
                sp.dma_start(bm[:, :], dram["bmT"]).then_inc(loaded, 16)

            @block.gpsimd
            def _(g):
                norm_gpsimd(k, n)
                g.memset(lower[:, :, :], 1.0).then_inc(lower_zeroed, 1)
                g.wait_ge(lower_zeroed, 1)
                g.affine_select(out=lower[:, :, :], in_=lower[:, :, :], compare_op=ALU.is_gt, fill=0.0, base=0,
                                pattern=[[1, E], [-1, E]], channel_multiplier=0).then_inc(lower_ready, 1)

            @block.tensor
            def _(pe):
                norm_tensor(k, n, m, k.bank[0:2])
                pe.wait_ge(loaded, 64)
                for t in range(TILES):
                    pe.wait_ge(k.xnT_ready, TILES * m + t + 1)
                    for f in range(KT):
                        last = pe.matmul(k.bank[2 + t // 2][:, t % 2 * 256:t % 2 * 256 + E + E * R],
                                         k.xnT[:, f, t * P:(t + 1) * P], wra[:, f, :], start=f == 0, stop=f == KT - 1)
                last.then_inc(low_psum, 1)
                for t in range(TILES):
                    for f in range(KT):
                        pe.matmul(k.bank[4 + t][:, :], k.xnT[:, f, t * P:(t + 1) * P], wb[:, f, :],
                                  start=f == 0, stop=False)
                for t in range(TILES):
                    pe.wait_ge(low_ready, t + 1)
                    last = pe.transpose(k.bank[0][:, t * P:(t + 1) * P], low[:, t, :], k.ident[:, :])
                last.then_inc(lowT_psum, 1)
                pe.wait_ge(lowT_ready, 1)
                for t in range(TILES):
                    pe.matmul(k.bank[4 + t][:, :], lowT[:, t * P:(t + 1) * P], bm[:, :],
                              start=False, stop=True).then_inc(out_psum, 1)

            @block.vector
            def _(v):
                norm_vector(k, n)
                v.wait_ge(loaded, 64)
                v.wait_ge(k.xn_ready, TILES * (n + 1))
                for t in range(TILES):
                    k.vown(v.tensor_tensor(k.x[:, t, :], k.x[:, t, :], bias[:, :], ALU.add))
                v.wait_ge(low_psum, 1)
                for h in range(2):
                    k.vown(v.tensor_copy(logits[:, 2 * h:2 * h + 2, :],
                                         k.bank[2 + h][:, :].rearrange("p (t c) -> p t c", t=2)[:, :, 0:E]))
                k.vown.wait()
                spread = lambda a: a[:, :].unsqueeze(2).broadcast_to([P, TILES, E])
                k.vown(v.tensor_reduce(top[:, :], logits[:, :, :], AX.X, ALU.max))
                k.vown.wait()
                v.tensor_tensor(logits[:, :, :], logits[:, :, :], spread(top), ALU.subtract).then_inc(shifted_ready, 1)
                v.wait_ge(expd_ready, 1)
                k.vown(v.tensor_reduce(total[:, :], expd[:, :, :], AX.X, ALU.add))
                k.vown.wait()
                k.vown(v.reciprocal(total[:, :], total[:, :]))
                k.vown.wait()
                k.vown(v.tensor_tensor(probs[:, :, :], expd[:, :, :], spread(total), ALU.mult))
                k.vown.wait()
                of_f = probs[:, :, :].unsqueeze(2).broadcast_to([P, TILES, E, E])
                of_e = probs[:, :, :].unsqueeze(3).broadcast_to([P, TILES, E, E])
                k.vown(v.tensor_tensor(more[:, :, :, :], of_f, of_e, ALU.is_gt))
                k.vown(v.tensor_tensor(same[:, :, :, :], of_f, of_e, ALU.is_equal))
                k.vown.wait()
                v.wait_ge(lower_ready, 1)
                k.vown(v.tensor_tensor(same[:, :, :, :], same[:, :, :, :],
                                       lower[:, :, :].unsqueeze(1).broadcast_to([P, TILES, E, E]), ALU.mult))
                k.vown.wait()
                k.vown(v.tensor_tensor(more[:, :, :, :], more[:, :, :, :], same[:, :, :, :], ALU.add))
                k.vown.wait()
                k.vown(v.tensor_reduce(rank[:, :, :], more[:, :, :, :], AX.X, ALU.add))
                k.vown.wait()
                k.vown(v.scalar_tensor_tensor(weight[:, :, :], rank[:, :, :], float(TOP), probs[:, :, :],
                                              ALU.is_lt, ALU.mult))
                k.vown.wait()
                k.vown(v.tensor_reduce(total[:, :], weight[:, :, :], AX.X, ALU.add))
                k.vown.wait()
                k.vown(v.reciprocal(total[:, :], total[:, :]))
                k.vown.wait()
                k.vown(v.scalar_tensor_tensor(weight[:, :, :], weight[:, :, :], SCALING, spread(total), ALU.mult, ALU.mult))
                k.vown.wait()
                for t in range(TILES):
                    h = k.bank[2 + t // 2][:, t % 2 * 256 + E:t % 2 * 256 + E + E * R]
                    v.tensor_tensor(low[:, t, :].rearrange("p (e r) -> p e r", r=R), h.rearrange("p (e r) -> p e r", r=R),
                                    weight[:, t, :].unsqueeze(2).broadcast_to([P, E, R]), ALU.mult)\
                     .then_inc(low_ready, 1)
                for t in range(TILES):
                    v.wait_ge(out_psum, t + 1)
                    k.vown(v.tensor_tensor(k.x[:, t, :], k.bank[4 + t][:, :], k.x[:, t, :], ALU.add))
                k.vown.wait()

            @block.scalar
            def _(a):
                norm_scalar(k, m, k.bank[0:2])
                a.wait_ge(shifted_ready, 1)
                a.activation(expd[:, :, :], logits[:, :, :], ACT.Exp).then_inc(expd_ready, 1)
                a.wait_ge(lowT_psum, 1)
                a.copy(lowT[:, :], k.bank[0][:, :]).then_inc(lowT_ready, 1)


def epilogue(k, out):
    nc = k.nc
    stored = k.sem("stored")
    with nc.Block(no_gpsimd_drain=True) as block:

        @block.sync
        def _(sp):
            sp.dma_start(out.rearrange("b (t p) d -> p (b t) d", p=P), k.x[:, :, :]).then_inc(stored, 16)
            sp.wait_ge(stored, 16)


LAYERS = [layer0_attention, layer0_ffn, layer1_attention, layer1_ffn, layer2_attention, layer2_ffn, layer3_attention, layer3_ffn]


def build(nc, dram, out, first=0, layers=len(LAYERS)):
    with ExitStack() as stack:
        k = Core(nc, stack)
        prologue(k, dram)
        for layer in LAYERS[first:layers]:
            k.label = layer.__name__ + "_"
            layer(k, dram)
        epilogue(k, out)


def layout(inputs):
    a = {n: np.ascontiguousarray(v) for n, v in inputs.items()}
    ctx = a.pop("ctx_4096")
    a["ctx"] = ctx
    a["ctxT"] = np.ascontiguousarray(ctx.reshape(B * CTX, D).T)
    a["wv4"] = np.ascontiguousarray(np.tile(a.pop("L1_xattn_Wv_u"), (4, 1)))
    a["wq2"] = np.ascontiguousarray(np.tile(a.pop("L1_xattn_Wq_d"), (1, 2)))
    wqk = a.pop("L1_xattn_W_qk")
    a["wqk8"] = np.ascontiguousarray(np.tile(wqk.reshape(len(wqk), 16, 1, -1), (2, 1, 4, 1)).reshape(2 * len(wqk), -1))
    a["wkv4"] = np.ascontiguousarray(np.tile(a.pop("L1_xattn_Wkv_d"), (1, 4)))
    for name, source in (("w_gateT", "L1_ffn_w_gate"), ("w_upT", "L1_ffn_w_up"), ("w_downT", "L1_ffn_w_down"),
                         ("routerT", "L2_ffn_router_weight"), ("wbT", "L3_ffn_Wb")):
        a[name] = np.ascontiguousarray(a.pop(source).T)
    G, H = 8, 128
    wkv = np.stack([a.pop("L2_xattn_k_proj_w").reshape(G, H, D), a.pop("L2_xattn_v_proj_w").reshape(G, H, D)], axis=1)
    wkv = wkv.reshape(G, 2 * H, D)
    a["wkvT"] = np.ascontiguousarray(np.concatenate([wkv, wkv[:1]]).reshape(-1, D).T)
    wq = a.pop("L2_xattn_q_proj_w").reshape(G, -1, D)
    a["wqT"] = np.ascontiguousarray(np.concatenate([wq, wq[:1]]).reshape(-1, D).T)
    wo = a.pop("L2_xattn_o_proj_w").T
    a["woT"] = np.ascontiguousarray(np.concatenate([wo, wo[:wo.shape[0] // G]]))
    low = a.pop("L3_ffn_A")
    a["wraT"] = np.ascontiguousarray(np.concatenate([a.pop("L3_ffn_Wr").T, low.reshape(-1, D).T], axis=1))
    a["bmT"] = np.ascontiguousarray(a.pop("L3_ffn_Bm").transpose(0, 2, 1).reshape(-1, D))
    return a


def kernel(**inputs):
    import numpy as _np
    import concourse.bacc as _bacc
    from concourse import mybir as _mybir
    from concourse.bass_utils import run_bass_kernel_spmd as _run

    nc = _bacc.Bacc("TRN2", target_bir_lowering=False, num_devices=1)
    arrays, dram = {}, {}
    for name, a in layout({n: _np.asarray(v) for n, v in inputs.items()}).items():
        arrays[f"in_{name}"] = a
        dram[name] = nc.dram_tensor(f"in_{name}", a.shape, _mybir.dt.from_np(a.dtype), kind="ExternalInput").ap()
    out = nc.dram_tensor("out_0_dram", (B, SEQ, D), _mybir.dt.float32, kind="ExternalOutput").ap()
    build(nc, dram, out)
    return _run(nc, [arrays], core_ids=[0]).results[0]["out_0_dram"]
```

```python
from contextlib import ExitStack

import numpy as np

import concourse.bass as bass
from concourse import mybir

F32, BF16, I32, F32R = mybir.dt.float32, mybir.dt.bfloat16, mybir.dt.int32, mybir.dt.float32r
ALU = mybir.AluOpType
ACT = mybir.ActivationFunctionType
AX = mybir.AxisListType

P = 128
B, SEQ, D = 2, 256, 512
CTX = 512
TILES = B * SEQ // P
TPB = SEQ // P
KT = D // P
CTILES = B * CTX // P
CPB = CTX // P
EPS = 1e-5
ROUND = 1.5 * 2.0 ** 23
BANKS = 8


class Own:

    def __init__(self, engine, semaphore):
        self.engine, self.semaphore, self.count = engine, semaphore, 0

    def __call__(self, instruction):
        instruction.then_inc(self.semaphore, 1)
        self.count += 1

    def wait(self):
        self.engine.wait_ge(self.semaphore, self.count)


class Core:

    def __init__(self, nc, stack):
        self.nc, self.stack, self.norms, self.turned, self.label = nc, stack, 0, 0, ""
        sb = self.sbuf
        self.x = sb("x", [P, TILES, D], F32)
        self.xn = sb("xn", [P, TILES, D], F32)
        self.xnT = sb("xnT", [P, KT, TILES * P], F32)
        self.ctxT = sb("ctxT", [P, KT, B * CTX], F32)
        self.ident = sb("ident", [P, P], F32)
        self.ident16 = sb("ident16", [P, P], BF16)
        self.ones = sb("ones", [P, P], F32)
        self.ones16 = sb("ones16", [P, 1], BF16)
        self.minus_half = sb("minus_half", [P, 8], F32)
        self.stats = sb("stats", [P, TILES, 6], F32)
        self.meanvar = sb("meanvar", [P, TILES, 2], F32)
        self.varep = sb("varep", [P, TILES], F32)
        self.rstd = sb("rstd", [P, TILES], F32)
        bisection_buffers(self)
        self.bank = [stack.enter_context(nc.psum_tensor(f"bank{i}", [P, 512], F32)) for i in range(BANKS)]
        self.vown = Own(nc.vector, self.sem("vector_own"))
        self.pown = Own(nc.gpsimd, self.sem("gpsimd_own"))
        self.aown = Own(nc.scalar, self.sem("scalar_own"))
        self.variance_ready = self.sem("variance_ready")
        self.rstd_ready = self.sem("rstd_ready")
        self.xn_ready = self.sem("xn_ready")
        self.xnT_in_psum = self.sem("xnT_in_psum")
        self.xnT_ready = self.sem("xnT_ready")
        self.x_loaded = self.sem("x_loaded")
        self.ctxT_loaded = self.sem("ctxT_loaded")

    def sbuf(self, name, shape, dtype, stack=None):
        return (stack or self.stack).enter_context(self.nc.sbuf_tensor(self.label + name, shape, dtype))

    def sem(self, name):
        return self.stack.enter_context(self.nc.semaphore(name))


def at(step, per, c):
    i, offset = step
    return per * offset + c if i is None else i * (2 * per) + (per * offset + c)


def after(step, steps=1):
    return step[0], step[1] + steps


def is_start(step):
    return step[0] is None and step[1] == 0


class StepOwn:

    def __init__(self, engine, semaphore, step, per):
        self.engine, self.semaphore, self.step, self.per, self.count = engine, semaphore, step, per, 0

    def __call__(self, instruction):
        instruction.then_inc(self.semaphore, 1)
        self.count += 1

    def wait(self):
        self.engine.wait_ge(self.semaphore, at(self.step, self.per, self.count))



def norm_vector(k, n):
    v = k.nc.vector
    for t in range(TILES):
        k.vown(v.bn_stats(k.stats[:, t, :], k.x[:, t, :]))
    k.vown.wait()
    for t in range(TILES):
        k.vown(v.bn_aggr(k.meanvar[:, t, :], k.stats[:, t, :]))
    k.vown.wait()
    v.tensor_scalar(k.varep[:, :], k.meanvar[:, :, 1], EPS, None, ALU.add).then_inc(k.variance_ready, 1)
    v.wait_ge(k.rstd_ready, n + 1)
    for t in range(TILES):
        v.tensor_scalar(k.xn[:, t, :], k.x[:, t, :], k.meanvar[:, t, 0:1], k.rstd[:, t:t + 1],
                        ALU.subtract, ALU.mult).then_inc(k.xn_ready, 1)


def norm_gpsimd(k, n):
    g = k.nc.gpsimd
    g.wait_ge(k.variance_ready, n + 1)
    g.tensor_tensor(k.rstd[:, :], k.varep[:, :], k.minus_half[:, 0:TILES], ALU.pow).then_inc(k.rstd_ready, 1)


def norm_tensor(k, n, m, banks):
    pe = k.nc.tensor
    for t in range(TILES):
        pe.wait_ge(k.xn_ready, TILES * n + t + 1)
        if t >= 2:
            pe.wait_ge(k.xnT_ready, TILES * m + t - 1)
        for f in range(KT):
            last = pe.transpose(banks[t % 2][:, f * P:(f + 1) * P], k.xn[:, t, f * P:(f + 1) * P], k.ident[:, :])
        last.then_inc(k.xnT_in_psum, 1)


def norm_scalar(k, m, banks):
    a = k.nc.scalar
    for t in range(TILES):
        a.wait_ge(k.xnT_in_psum, TILES * m + t + 1)
        a.copy(k.xnT[:, :, t * P:(t + 1) * P],
               banks[t % 2][:, :].rearrange("p (f c) -> p f c", f=KT)).then_inc(k.xnT_ready, 1)



def prologue(k, dram):
    nc = k.nc
    identity_zeroed = k.sem("identity_zeroed")
    with nc.Block(no_gpsimd_drain=True) as block:

        @block.sync
        def _(sp):
            sp.dma_start(k.x[:, :, :], dram["x"].rearrange("b (t p) d -> p (b t) d", p=P)).then_inc(k.x_loaded, 16)
            sp.wait_ge(k.x_loaded, 16)

        @block.gpsimd
        def _(g):
            g.memset(k.ident[:, :], 0.0).then_inc(identity_zeroed, 1)
            g.memset(k.ident16[:, :], 0.0).then_inc(identity_zeroed, 1)
            k.pown(g.memset(k.ones[:, :], 1.0))
            k.pown(g.memset(k.ones16[:, :], 1.0))
            k.pown(g.memset(k.minus_half[:, :], -0.5))
            g.wait_ge(identity_zeroed, 2)
            for m in (k.ident, k.ident16):
                k.pown(g.affine_select(out=m[:, :], in_=m[:, :], compare_op=ALU.not_equal, fill=1.0,
                                       base=0, pattern=[[-1, P]], channel_multiplier=1))
            k.pown.wait()



def layer0_attention(k, dram):
    nc, n = k.nc, k.norms
    k.norms += 1
    MIDDLE = 128.0
    with ExitStack() as s:
        ctx = k.sbuf("ctx", [P, CTILES, D], F32, s)
        q2 = k.sbuf("q2", [P, CTILES, D], BF16, s)
        q1 = k.sbuf("q1", [P, TILES, D], BF16, s)
        q1T = k.sbuf("q1T", [P, KT, TILES * P], BF16, s)
        t1 = k.sbuf("t1", [P, 2, D], F32, s)
        t2 = k.sbuf("t2", [P, 2, D], F32, s)
        par = k.sbuf("par", [P, 4], F32, s)
        inv = k.sbuf("inv", [P, 2], F32, s)
        off = k.sbuf("off", [P, 2], F32, s)
        s12 = k.sbuf("s12", [P, 1], F32, s)
        kd1 = k.sbuf("kd1", [P, 1], F32, s)
        d2s = k.sbuf("d2s", [P, 1], F32, s)
        rows = k.sbuf("rows", [P, TILES], F32, s)
        corr = k.sbuf("corr", [P, TILES], F32, s)
        cols = k.sbuf("cols", [1, B, D], F32, s)
        par_loaded, ctx_loaded = k.sem("par_loaded"), k.sem("ctx_loaded")
        q2_ready, q1_ready, q1T_psum, q1T_ready = (k.sem(f"l0a_{x}") for x in
                                                   ("q2_ready", "q1_ready", "q1T_psum", "q1T_ready"))
        cols_psum, cols_ready, product_psum = (k.sem(f"l0a_{x}") for x in
                                               ("cols_psum", "cols_ready", "product_psum"))
        with nc.Block(no_gpsimd_drain=True) as block:

            @block.sync
            def _(sp):
                for i, name in enumerate(("L0_xattn_x1_scale", "L0_xattn_x1_zp", "L0_xattn_x2_scale", "L0_xattn_x2_zp")):
                    sp.dma_start(par[:, i:i + 1], dram[name].unsqueeze(0).broadcast_to([P, 1])).then_inc(par_loaded, 16)
                for b in range(B):
                    sp.dma_start(ctx[:, b * CPB:(b + 1) * CPB, :],
                                 dram["ctx"][b].rearrange("(t p) d -> p t d", p=P)).then_inc(ctx_loaded, 16)
                sp.dma_start(k.ctxT[:, :, :], dram["ctxT"].rearrange("(f p) r -> p f r", p=P)).then_inc(k.ctxT_loaded, 16)

            @block.gpsimd
            def _(g):
                norm_gpsimd(k, n)

            @block.vector
            def _(v):
                norm_vector(k, n)
                v.wait_ge(par_loaded, 64)
                for i in range(2):
                    k.vown(v.reciprocal(inv[:, i:i + 1], par[:, 2 * i:2 * i + 1]))
                    k.vown(v.tensor_scalar(off[:, i:i + 1], par[:, 2 * i + 1:2 * i + 2], -1.0, MIDDLE, ALU.mult, ALU.add))
                k.vown(v.tensor_tensor(s12[:, :], par[:, 0:1], par[:, 2:3], ALU.mult))
                k.vown.wait()
                k.vown(v.tensor_scalar(kd1[:, :], off[:, 0:1], float(CTX), None, ALU.mult))
                k.vown(v.tensor_tensor(d2s[:, :], off[:, 1:2], s12[:, :], ALU.mult))

                def quantise(source, target, i, ready):
                    for j in range(2):
                        k.vown(v.tensor_scalar(t1[:, j, :], source(j), inv[:, i:i + 1], par[:, 2 * i + 1:2 * i + 2],
                                               ALU.mult, ALU.add))
                    k.vown.wait()
                    for j in range(2):
                        k.vown(v.tensor_scalar(t2[:, j, :], t1[:, j, :], 0.0, 255.0, ALU.max, ALU.min))
                    k.vown.wait()
                    for j in range(2):
                        v.tensor_scalar(target(j), t2[:, j, :], ROUND, ROUND + MIDDLE, ALU.add,
                                        ALU.subtract).then_inc(ready, 1)

                v.wait_ge(k.xn_ready, TILES * n + TILES)
                for t in range(0, TILES, 2):
                    quantise(lambda j: k.xn[:, t + j, :], lambda j: q1[:, t + j, :], 0, q1_ready)
                v.wait_ge(q1_ready, TILES)
                for t in range(TILES):
                    k.vown(v.tensor_reduce(rows[:, t:t + 1], q1[:, t, :], AX.X, ALU.add))
                v.wait_ge(ctx_loaded, 16 * B)
                for t in range(0, CTILES, 2):
                    quantise(lambda j: ctx[:, t + j, :], lambda j: q2[:, t + j, :], 1, q2_ready)
                k.vown.wait()
                k.vown(v.tensor_scalar(corr[:, :], rows[:, :], kd1[:, 0:1], d2s[:, 0:1], ALU.add, ALU.mult))
                k.vown.wait()
                for t in range(TILES):
                    k.vown(v.tensor_scalar(k.x[:, t, :], k.x[:, t, :], corr[:, t:t + 1], None, ALU.add))
                for b in range(B):
                    v.wait_ge(cols_psum, b + 1)
                    v.tensor_scalar(cols[:, b, :], k.bank[2 + b][0:1, :], off[0:1, 0:1], None,
                                    ALU.mult).then_inc(cols_ready, 1)
                k.vown.wait()
                for t in range(TILES):
                    v.wait_ge(product_psum, t + 1)
                    k.vown(v.scalar_tensor_tensor(k.x[:, t, :], k.bank[4 + t][:, :], s12[:, 0:1], k.x[:, t, :],
                                                  ALU.mult, ALU.add))
                k.vown.wait()

            @block.tensor
            def _(pe):
                for t in range(TILES):
                    pe.wait_ge(q1_ready, t + 1)
                    if t >= 2:
                        pe.wait_ge(q1T_ready, t - 1)
                    for f in range(KT):
                        last = pe.transpose(k.bank[t % 2][:, 0:256].bitcast(BF16)[:, f * P:(f + 1) * P],
                                            q1[:, t, f * P:(f + 1) * P], k.ident16[:, :])
                    last.then_inc(q1T_psum, 1)
                for b in range(B):
                    pe.wait_ge(q2_ready, CPB * (b + 1))
                    for f in range(CPB):
                        last = pe.matmul(k.bank[2 + b][0:1, :], k.ones16[:, :], q2[:, b * CPB + f, :],
                                         start=f == 0, stop=f == CPB - 1)
                    last.then_inc(cols_psum, 1)
                pe.wait_ge(q1T_ready, TILES)
                for t in range(TILES):
                    b = t // TPB
                    for f in range(CPB):
                        pe.matmul(k.bank[4 + t][:, :], q1T[:, f, t * P:(t + 1) * P], q2[:, b * CPB + f, :],
                                  start=f == 0, stop=False)
                    pe.wait_ge(cols_ready, b + 1)
                    pe.matmul(k.bank[4 + t][:, :], k.ones[0:1, :], cols[:, b, :],
                              start=False, stop=True).then_inc(product_psum, 1)

            @block.scalar
            def _(a):
                for t in range(TILES):
                    a.wait_ge(q1T_psum, t + 1)
                    a.copy(q1T[:, :, t * P:(t + 1) * P],
                           k.bank[t % 2][:, 0:256].bitcast(BF16).rearrange("p (f c) -> p f c", f=KT))\
                     .then_inc(q1T_ready, 1)



def layer0_ffn(k, dram):
    nc, n, m = k.nc, k.norms, k.turned
    k.norms += 1
    k.turned += 1
    PLANES, BITS = 4, 32
    WORDS = D // BITS
    CODES = 2 ** PLANES
    OT = D // P
    with ExitStack() as s:
        planes = k.sbuf("planes", [P, OT, PLANES * WORDS], I32, s)
        shifts = k.sbuf("shifts", [P, BITS], I32, s)
        moved = k.sbuf("moved", [P, PLANES * WORDS, BITS], I32, s)
        bits = k.sbuf("bits", [P, 2, PLANES, D], I32, s)
        lut = k.sbuf("lut", [P, OT, CODES], F32, s)
        diff = k.sbuf("diff", [P, OT, CODES // 2], F32, s)
        tree = k.sbuf("tree", [P, 2, CODES // 2, D], F32, s)
        weightT = k.sbuf("weightT", [P, KT, D], F32, s)
        bias = k.sbuf("bias", [P, D], F32, s)
        k.flags = k.sbuf("flags", [P, 2, CTX], BF16, s)
        loaded, bias_loaded, shifts_ready, diff_ready, bits_ready, leaves_ready, weight_ready, weightT_psum, \
            weightT_ready, product_psum = (k.sem(f"l0f_{x}") for x in (
                "loaded", "bias_loaded", "shifts_ready", "diff_ready", "bits_ready", "leaves_ready", "weight_ready",
                "weightT_psum", "weightT_ready", "product_psum"))
        with nc.Block(no_gpsimd_drain=True) as block:

            @block.sync
            def _(sp):
                for p in range(PLANES):
                    sp.dma_start(planes[:, :, p * WORDS:(p + 1) * WORDS],
                                 dram["L0_ffn_qweight"][p].rearrange("(t p) w -> p t w", p=P)).then_inc(loaded, 16)
                sp.dma_start(lut[:, :, :], dram["L0_ffn_lut4"].rearrange("(t p) c -> p t c", p=P)).then_inc(loaded, 16)
                sp.dma_start(bias[:, :], dram["L0_ffn_bias"].unsqueeze(0).broadcast_to([P, D])).then_inc(bias_loaded, 16)

            @block.gpsimd
            def _(g):
                g.iota(shifts[:, :], [[1, BITS]], base=0, channel_multiplier=0).then_inc(shifts_ready, 1)
                norm_gpsimd(k, n)

            @block.vector
            def _(v):
                norm_vector(k, n)
                v.wait_ge(loaded, 16 * (PLANES + 1))
                v.wait_ge(shifts_ready, 1)
                v.tensor_tensor(diff[:, :, :], lut[:, :, 1::2], lut[:, :, 0::2], ALU.subtract).then_inc(diff_ready, 1)
                v.wait_ge(bias_loaded, 16)
                v.wait_ge(k.xn_ready, TILES * (n + 1))
                for t in range(TILES):
                    k.vown(v.tensor_tensor(k.x[:, t, :], k.x[:, t, :], bias[:, :], ALU.add))

                def unpack(o):
                    if o >= 1:
                        v.wait_ge(bits_ready, o)
                    if o >= 2:
                        v.wait_ge(weight_ready, o - 1)
                        v.wait_ge(leaves_ready, o - 1)
                    k.vown(v.tensor_tensor(moved[:, :, :], planes[:, o, :].unsqueeze(2).broadcast_to([P, PLANES * WORDS, BITS]),
                                           shifts[:, :].unsqueeze(1).broadcast_to([P, PLANES * WORDS, BITS]),
                                           ALU.logical_shift_right))
                    k.vown.wait()
                    v.tensor_scalar(bits[:, o % 2, :, :].rearrange("p a (w b) -> p (a w) b", b=BITS), moved[:, :, :],
                                    1, None, ALU.bitwise_and).then_inc(bits_ready, 1)

                def choose(o):
                    v.wait_ge(leaves_ready, o + 1)
                    left = tree[:, o % 2, :, :]
                    for level in range(1, PLANES):
                        step = 2 ** (level - 1)
                        count = CODES // 2 // (2 * step)
                        mask = bits[:, o % 2, level, :].unsqueeze(1).broadcast_to([P, count, D])
                        ins = v.copy_predicated(left[:, 0::2 * step, :], mask, left[:, step::2 * step, :])
                        if level == PLANES - 1:
                            ins.then_inc(weight_ready, 1)
                        else:
                            k.vown(ins)
                            k.vown.wait()

                unpack(0)
                for o in range(OT):
                    if o + 1 < OT:
                        unpack(o + 1)
                    choose(o)
                k.vown.wait()
                v.wait_ge(k.ctxT_loaded, 16)
                bisection_start(k)
                bisection_rounds(k, 1)
                for t in range(TILES):
                    v.wait_ge(product_psum, t + 1)
                    k.vown(v.tensor_tensor(k.x[:, t, :], k.bank[4 + t][:, :], k.x[:, t, :], ALU.add))
                k.vown.wait()

            @block.scalar
            def _(a):
                def weightT_copy(o):
                    a.wait_ge(weightT_psum, o + 1)
                    a.copy(weightT[:, :, o * P:(o + 1) * P],
                                   k.bank[2 + o % 2][:, :].rearrange("p (f c) -> p f c", f=KT)).then_inc(weightT_ready, 1)

                norm_scalar(k, m, k.bank[0:2])
                a.wait_ge(diff_ready, 1)
                for o in range(OT):
                    a.wait_ge(bits_ready, o + 1)
                    if o >= 2:
                        a.wait_ge(weightT_psum, o - 1)
                    for j in range(CODES // 2):
                        ins = a.activation(tree[:, o % 2, j, :], bits[:, o % 2, 0, :], ACT.Identity,
                                           bias=lut[:, o, 2 * j:2 * j + 1], scale=diff[:, o, j:j + 1])
                    ins.then_inc(leaves_ready, 1)
                    if o >= 1:
                        weightT_copy(o - 1)
                weightT_copy(OT - 1)

            @block.tensor
            def _(pe):
                norm_tensor(k, n, m, k.bank[0:2])
                for o in range(OT):
                    pe.wait_ge(weight_ready, o + 1)
                    if o >= 2:
                        pe.wait_ge(weightT_ready, o - 1)
                    for f in range(KT):
                        last = pe.transpose(k.bank[2 + o % 2][:, f * P:(f + 1) * P],
                                            tree[:, o % 2, 0, f * P:(f + 1) * P], k.ident[:, :])
                    last.then_inc(weightT_psum, 1)
                pe.wait_ge(k.xnT_ready, TILES * (m + 1))
                pe.wait_ge(weightT_ready, OT)
                for t in range(TILES):
                    for f in range(KT):
                        last = pe.matmul(k.bank[4 + t][:, :], k.xnT[:, f, t * P:(t + 1) * P], weightT[:, f, :],
                                         start=f == 0, stop=f == KT - 1)
                    last.then_inc(product_psum, 1)



def layer1_attention(k, dram):
    nc, n, m = k.nc, k.norms, k.turned
    k.norms += 1
    k.turned += 1
    HEADS, LQ, LKV, HD = 16, D // 8, D // 16, D // 16
    COPIES = P // LKV
    QUERIES_AT = (0, 5, 9, 13)
    AHEAD = 4
    SCALE = LKV ** -0.5
    COUNTS = 8
    OWN_V = BISECT_PER_ROUND * COUNTS // 4
    with ExitStack() as s:
        ctxT = k.sbuf("ctxT_plain", [P, KT, B * CTX], F32, s)
        wq = k.sbuf("wq", [P, KT, 2 * LQ], F32, s)
        wkv = k.sbuf("wkv", [P, KT, P], F32, s)
        raw_qk = k.sbuf("raw_qk", [P, HEADS * P], F32, s)
        wqk = k.sbuf("wqk", [P, 2, HEADS * P], F32R, s)
        raw_v = k.sbuf("raw_v", [P, D], F32, s)
        wv = k.sbuf("wv", [P, D], F32R, s)
        keysT = k.sbuf("keysT", [P, B, CTX], F32R, s)
        values = k.sbuf("values", [P, CTILES, D], F32, s)
        latentT = k.sbuf("latentT", [P, TILES * P], F32R, s)
        queriesT = k.sbuf("queriesT", [P, B, HEADS, P], F32R, s)
        probs = k.sbuf("probs", [P, 4, CTX], F32, s)
        probsT = k.sbuf("probsT", [P, 4, CPB, P], F32, s)
        negmax = k.sbuf("negmax", [P, B, HEADS], F32, s)
        sums = k.sbuf("sums", [P, B, HEADS], F32, s)
        inverse = k.sbuf("inverse", [P, HEADS], F32, s)
        mixedT = k.sbuf("mixedT", [P, D], F32, s)
        mixed = k.sbuf("mixed", [P, D], F32, s)
        k.flags = k.sbuf("flags", [P, 2, CTX], BF16, s)
        names = ("operands_psum", "operands_high", "operands_low",
                 "loaded", "ctx_loaded", "wqk_low", "values_psum", "values_ready",
                 "queries_psum", "queries_high", "queries_low", "scores_psum", "negmax_ready", "probs_ready",
                 "probsT_psum", "probsT_ready", "heads_done", "mixedT_ready", "mixed_psum", "inverse_ready", "mixed_ready", "x_updated", "bisection")
        S_ = {x: k.sem(f"l1a_{x}") for x in names}
        S, T, O, Q = k.bank[0:4], k.bank[4:6], k.bank[6], k.bank[7]
        batch = lambda step: step[1] % B
        ahead = lambda step, h: (step, h + AHEAD - 1) if h + AHEAD - 1 < HEADS else (after(step), h + AHEAD - 1 - HEADS)

        def tile(step):
            i, offset = step
            return batch(step) * TPB + (offset // B if i is None else i + offset // B)

        with nc.Block(no_gpsimd_drain=True) as block:

            @block.sync
            def _(sp):
                for target, source in ((wkv[:, :, :], dram["wkv4"].rearrange("(f p) c -> p f c", p=P)),
                                       (raw_v[:, :], dram["wv4"])):
                    sp.dma_start(target, source).then_inc(S_["ctx_loaded"], 16)
                sp.dma_start(ctxT[:, :, :], dram["ctxT"].rearrange("(f p) r -> p f r", p=P)).then_inc(S_["ctx_loaded"], 16)
                for target, source in ((wq[:, :, :], dram["wq2"].rearrange("(f p) c -> p f c", p=P)),
                                       (raw_qk[:, :], dram["wqk8"])):
                    sp.dma_start(target, source).then_inc(S_["loaded"], 16)

            @block.gpsimd
            def _(g):
                norm_gpsimd(k, n)
                g.wait_ge(S_["loaded"], 32)
                k.pown(g.tensor_copy(wqk[:, 0, :], raw_qk[:, :]))
                k.pown.wait()
                g.tensor_tensor(wqk[:, 1, :], raw_qk[:, :], wqk[:, 0, :], ALU.subtract).then_inc(S_["wqk_low"], 1)

            @block.tensor
            def _(pe):
                norm_tensor(k, n, m, T)
                pe.wait_ge(S_["loaded"], 32)
                pe.wait_ge(k.xnT_ready, TILES * (m + 1))
                for f in range(KT):
                    last = pe.matmul(Q[:, :], wq[:, f, :], k.xnT[:, f, :], start=f == 0, stop=f == KT - 1)
                last.then_inc(S_["operands_psum"], 1)
                pe.wait_ge(S_["ctx_loaded"], 48)
                for b in range(B):
                    for f in range(KT):
                        last = pe.matmul(S[b][:, :], wkv[:, f, :], ctxT[:, f, b * CTX:(b + 1) * CTX],
                                         start=f == 0, stop=f == KT - 1)
                    last.then_inc(S_["operands_psum"], 1)

                def queries(step, j):
                    if not (step[0] is None and j == 0):
                        pe.wait_ge(S_["queries_low"], at(step, 4, j))
                    t = tile(step)
                    tokens = slice(t * P, (t + 1) * P) if step[0] is None else bass.ts(t, P)
                    for h in range(4 * j, 4 * j + 4):
                        for part in range(2):
                            last = pe.matmul(Q[:, h % 4 * P:(h % 4 + 1) * P], wqk[:, part, h * P:(h + 1) * P],
                                             latentT[:, tokens], start=part == 0, stop=part == 1)
                    last.then_inc(S_["queries_psum"], 1)

                def scores(step, h):
                    if step[0] is not None:
                        pe.wait_ge(S_["probs_ready"], at(step, HEADS, h - 3))
                    if h % 4 == 0:
                        pe.wait_ge(S_["queries_low"], at(step, 4, h // 4 + 1))
                    pe.matmul(S[h % 4][:, :], queriesT[:, batch(step), h, :], keysT[:, batch(step), :],
                              start=True, stop=True).then_inc(S_["scores_psum"], 1)

                def turn(step, h):
                    if h >= 2:
                        pe.wait_ge(S_["probsT_ready"], at(step, HEADS, h - 1))
                    pe.wait_ge(S_["probs_ready"], at(step, HEADS, h + 1))
                    for c in range(CPB):
                        last = pe.transpose(T[h % 2][:, c * P:(c + 1) * P], probs[:, h % 4, c * P:(c + 1) * P],
                                            k.ident[:, :])
                    last.then_inc(S_["probsT_psum"], 1)

                def mix(step, h):
                    if h == 0:
                        pe.wait_ge(S_["mixedT_ready"], at(step, 1, 1))
                    pe.wait_ge(S_["probsT_ready"], at(step, HEADS, h + 1))
                    for c in range(CPB):
                        last = pe.matmul(O[h % 4 * HD:(h % 4 + 1) * HD, h // 4 * P:(h // 4 + 1) * P],
                                         values[:, batch(step) * CPB + c, h * HD:(h + 1) * HD], probsT[:, h % 4, c, :],
                                         start=c == 0, stop=c == CPB - 1)
                    last.then_inc(S_["heads_done"], 1)

                def turn_mixed(step, c):
                    pe.wait_ge(S_["queries_low"], at(after(step, 2), 4, c))
                    pe.wait_ge(S_["mixedT_ready"], at(step, 1, 2))
                    for g in range(HEADS // 4):
                        last = pe.transpose(Q[:, g * P:(g + 1) * P], mixedT[:, g * P:(g + 1) * P], k.ident[:, :])
                    last.then_inc(S_["mixed_psum"], 1)

                pe.wait_ge(S_["operands_low"], 1)
                pe.wait_ge(S_["wqk_low"], 1)
                start = (None, 0)
                queries(start, 0)
                pe.wait_ge(S_["operands_low"], 2)
                for r in range(CTILES):
                    pe.wait_ge(S_["operands_low"], r // CPB + 3)
                    if r >= 2:
                        pe.wait_ge(S_["values_ready"], r - 1)
                    pe.matmul(S[2 + r % 2][:, :], keysT[:, r // CPB, (r % CPB) * P:(r % CPB + 1) * P], wv[:, :],
                              start=True, stop=True).then_inc(S_["values_psum"], 1)
                    if r % 2 == 1 and r < 6:
                        queries(start, r // 2 + 1)
                pe.wait_ge(S_["values_ready"], CTILES)
                for h in range(AHEAD):
                    scores(start, h)
                with pe.Fori(0, TPB) as i:
                    for b in range(B):
                        step = (i, b)
                        for h in range(HEADS):
                            if h == 3 and b == 1:
                                turn_mixed((i, 0), 1)
                            if h in QUERIES_AT:
                                if (b, h) in ((0, QUERIES_AT[0]), (1, QUERIES_AT[1])):
                                    pe.wait_ge(S_["mixed_ready"], at((i, 0), 1, b + 1))
                                queries(after(step), QUERIES_AT.index(h))
                            turn(step, h)
                            if h + AHEAD < HEADS:
                                scores(step, h + AHEAD)
                            else:
                                scores(after(step), h + AHEAD - HEADS)
                            if h >= 2:
                                mix(step, h - 2)
                        mix(step, HEADS - 2)
                        mix(step, HEADS - 1)
                    turn_mixed((i, 1), 0)

            @block.vector
            def _(v):
                own = k.vown
                norm_vector(k, n)
                v.wait_ge(S_["operands_high"], 1)
                v.scalar_tensor_tensor(latentT[LQ:P, :], Q[LQ:P, :], SCALE, latentT[LQ:P, :],
                                       ALU.mult, ALU.subtract).then_inc(S_["operands_low"], 1)
                v.wait_ge(S_["operands_high"], 2)
                v.tensor_tensor(wv[P // 2:P, :], raw_v[P // 2:P, :], wv[P // 2:P, :], ALU.subtract).then_inc(S_["operands_low"], 1)
                for b in range(B):
                    v.wait_ge(S_["operands_high"], b + 3)
                    for j in (1, 3):
                        rows = slice(j * LKV, (j + 1) * LKV)
                        last = v.tensor_tensor(keysT[rows, b, :], S[b][rows, :], keysT[rows, b, :], ALU.subtract)
                    last.then_inc(S_["operands_low"], 1)

                def queries_low(step, j):
                    v.wait_ge(S_["queries_high"], at(step, 4, j + 1))
                    now = queriesT[P // 2:P, batch(step), 4 * j:4 * j + 4, :]
                    v.tensor_tensor(now, Q[P // 2:P, :].rearrange("p (h q) -> p h q", h=4), now, ALU.subtract)\
                     .then_inc(S_["queries_low"], 1)

                start = (None, 0)
                queries_low(start, 0)
                for r in range(CTILES):
                    v.wait_ge(S_["values_psum"], r + 1)
                    v.tensor_copy(values[:, r, :], S[2 + r % 2][:, :]).then_inc(S_["values_ready"], 1)
                    if r % 2 == 1 and r < 6:
                        queries_low(start, r // 2 + 1)
                v.sem_inc(S_["mixed_ready"], 1)

                def maximum(step, h):
                    v.wait_ge(S_["scores_psum"], at(step, HEADS, h + 1))
                    v.tensor_reduce(negmax[:, batch(step), h:h + 1], S[h % 4][:, :], AX.X, ALU.max, negate=True)\
                     .then_inc(S_["negmax_ready"], 1)

                def add_mixed(step):
                    v.wait_ge(S_["probs_ready"], at(step, HEADS, HEADS))
                    v.reciprocal(inverse[:, :], sums[:, batch(step), :]).then_inc(S_["inverse_ready"], 1)
                    v.wait_ge(S_["inverse_ready"], at(step, 1, 1))
                    v.wait_ge(S_["mixed_psum"], at(step, 1, 1))
                    v.tensor_tensor(mixed[:, :].rearrange("p (h d) -> p h d", h=HEADS),
                                    Q[:, :].rearrange("p (h d) -> p h d", h=HEADS),
                                    inverse[:, :].unsqueeze(2).broadcast_to([P, HEADS, HD]), ALU.mult)\
                     .then_inc(S_["mixed_ready"], 1)
                    v.wait_ge(S_["mixed_ready"], at(step, 1, 2))
                    v.tensor_tensor(k.x[:, tile(step), :], k.x[:, tile(step), :], mixed[:, :], ALU.add)\
                     .then_inc(S_["x_updated"], 1)

                for h in range(AHEAD - 1):
                    maximum(start, h)
                with v.Fori(0, TPB) as i:
                    for b in range(B):
                        step = (i, b)
                        bisect = StepOwn(v, S_["bisection"], step, OWN_V)
                        for h in range(HEADS):
                            maximum(*ahead(step, h))
                            if h - 1 in QUERIES_AT:
                                queries_low(after(step), QUERIES_AT.index(h - 1))
                            if h == 3 and b == 1:
                                add_mixed((i, 0))
                            for c in range(COUNTS * h // HEADS, COUNTS * (h + 1) // HEADS):
                                bisection_count(k, bisect, c % 4)
                                if c % 4 == 3:
                                    bisection_update(k, bisect)
                        assert bisect.count == OWN_V
                    add_mixed((i, 1))
                v.wait_ge(S_["x_updated"], TILES)
                v.wait_ge(S_["bisection"], TILES * OWN_V)

            @block.scalar
            def _(a):
                norm_scalar(k, m, T)
                a.wait_ge(S_["operands_psum"], 1)
                a.activation(latentT[:, :], Q[:, :], ACT.Copy, scale=SCALE).then_inc(S_["operands_high"], 1)
                a.wait_ge(S_["ctx_loaded"], 48)
                a.copy(wv[:, :], raw_v[:, :]).then_inc(S_["operands_high"], 1)
                for b in range(B):
                    a.wait_ge(S_["operands_psum"], b + 2)
                    a.copy(keysT[:, b, :], S[b][:, :]).then_inc(S_["operands_high"], 1)

                def queries_high(step, j):
                    a.wait_ge(S_["queries_psum"], at(step, 4, j + 1))
                    a.copy(queriesT[:, batch(step), 4 * j:4 * j + 4, :], Q[:, :].rearrange("p (h q) -> p h q", h=4))\
                     .then_inc(S_["queries_high"], 1)

                start = (None, 0)
                queries_high(start, 0)
                for j in range(1, 4):
                    queries_high(start, j)

                def exponentials(step, h):
                    a.wait_ge(S_["negmax_ready"], at(step, HEADS, h + 1))
                    if not (is_start(step) and h < 4):
                        a.wait_ge(S_["probsT_psum"], at(step, HEADS, h - 3))
                    if h == 0 and not is_start(step):
                        a.wait_ge(S_["mixed_ready"], at(step, 1, 0))
                    a.activation(probs[:, h % 4, :], S[h % 4][:, :], ACT.Exp, bias=negmax[:, batch(step), h:h + 1],
                                 accum_out=sums[:, batch(step), h:h + 1]).then_inc(S_["probs_ready"], 1)

                def copy_turned(step, h):
                    a.wait_ge(S_["probsT_psum"], at(step, HEADS, h + 1))
                    if h >= 4:
                        a.wait_ge(S_["heads_done"], at(step, HEADS, h - 3))
                    a.copy(probsT[:, h % 4, :, :], T[h % 2][:, :].rearrange("p (c q) -> p c q", c=CPB))\
                     .then_inc(S_["probsT_ready"], 1)

                def copy_mixed(step):
                    a.wait_ge(S_["heads_done"], at(step, HEADS, HEADS))
                    a.wait_ge(S_["mixed_ready"], at(step, 1, 1))
                    a.copy(mixedT[:, :], O[:, :]).then_inc(S_["mixedT_ready"], 1)

                a.sem_inc(S_["mixedT_ready"], 1)
                for h in range(AHEAD - 1):
                    exponentials(start, h)
                with a.Fori(0, TPB) as i:
                    for b in range(B):
                        step = (i, b)
                        for h in range(HEADS):
                            copy_turned(step, h)
                            exponentials(*ahead(step, h))
                            if h - 0 in QUERIES_AT:
                                queries_high(after(step), QUERIES_AT.index(h - 0))
                            if h == 0 and b == 1:
                                copy_mixed((i, 0))
                    copy_mixed((i, 1))



def layer1_ffn(k, dram):
    nc, n = k.nc, k.norms
    k.norms += 1
    I = 1376
    IT = -(-I // P)
    TAIL = I - (IT - 1) * P
    CHUNKS = [(c, min(c + 512, I)) for c in range(0, I, 512)]
    NC = len(CHUNKS)
    SQRT7 = float(np.float32(np.sqrt(7.0)))
    GATE, UP, DOWN = range(3)
    with ExitStack() as s:
        k.flags = k.sbuf("flags", [P, 2, CTX], BF16, s)
        raw = k.sbuf("raw", [P, 2, KT, I], F32, s)
        rawd = k.sbuf("rawd", [P, IT, D], F32, s)
        wgu = k.sbuf("wgu", [P, 2, KT, I], BF16, s)
        wd = k.sbuf("wd", [P, IT, D], BF16, s)
        total = k.sbuf("total", [P, 4], F32, s)
        wmean = k.sbuf("wmean", [P, 3], F32, s)
        winv = k.sbuf("winv", [P, 3], F32, s)
        scales = k.sbuf("scales", [P, 3], F32, s)
        wscale = k.sbuf("wscale", [P, 3], F32, s)
        round_col = k.sbuf("round_col", [P, 1], F32, s)
        t1 = k.sbuf("t1", [P, TILES, D], F32, s)
        x4 = k.sbuf("x4", [P, TILES, D], BF16, s)
        x4T = k.sbuf("x4T", [P, KT, TILES * P], BF16, s)
        beta = k.sbuf("beta", [P, TILES], F32, s)
        betae = k.sbuf("betae", [P, TILES], F32, s)
        binv = k.sbuf("binv", [P, TILES], F32, s)
        gate_scale = k.sbuf("gate_scale", [P, TILES], F32, s)
        up_scale = k.sbuf("up_scale", [P, TILES], F32, s)
        relu = k.sbuf("relu", [P, 2, 512], F32, s)
        gate = k.sbuf("gate", [P, 2, 512], F32, s)
        inner = k.sbuf("inner", [P, 2, I], F32, s)
        gamma = k.sbuf("gamma", [P, TILES], F32, s)
        gammae = k.sbuf("gammae", [P, TILES], F32, s)
        ginv = k.sbuf("ginv", [P, TILES], F32, s)
        x8 = k.sbuf("x8", [P, 2, I], BF16, s)
        x8T = k.sbuf("x8T", [P, IT, TILES * P], BF16, s)
        down_scale = k.sbuf("down_scale", [P, TILES], F32, s)
        loaded = [k.sem(f"l1f_loaded_{x}") for x in ("gate", "up", "down")]
        scales_loaded, up_total_ready, total_ready, total_psum, winv_ready, rounded, clipped, weights_ready, x4_ready, \
            x4T_psum, x4T_ready, gate_psum, up_psum, relu_ready, gate_ready, inner_ready, x8_ready, x8T_psum, \
            x8T_ready, down_psum, constants = (k.sem(f"l1f_{x}") for x in (
                "scales_loaded", "up_total_ready", "total_ready", "total_psum", "winv_ready", "rounded", "clipped",
                "weights_ready", "x4_ready", "x4T_psum", "x4T_ready", "gate_psum", "up_psum", "relu_ready",
                "gate_ready", "inner_ready", "x8_ready", "x8T_psum", "x8T_ready", "down_psum", "constants"))
        G, U, T, O = k.bank[0:2], k.bank[2:4], k.bank[4:6], k.bank[6:8]
        raws = [raw[:, 0].rearrange("p f c -> p (f c)"), raw[:, 1].rearrange("p f c -> p (f c)"),
                rawd[:, :, :].rearrange("p f c -> p (f c)")]
        targets = [wgu[:, 0, :, :].rearrange("p f c -> p (f c)"), wgu[:, 1, :, :].rearrange("p f c -> p (f c)"),
                   wd[:, :, :].rearrange("p f c -> p (f c)")]
        names = ("w_gateT", "w_upT", "w_downT")
        with nc.Block(no_gpsimd_drain=True) as block:

            def load(w):
                if w == DOWN:
                    nc.sync.wait_ge(constants, 1)
                    nc.sync.dma_start(rawd[:, 0:IT - 1, :], dram["w_downT"][0:(IT - 1) * P, :]
                                      .rearrange("(f p) c -> p f c", p=P)).then_inc(loaded[w], 16)
                    nc.sync.dma_start(rawd[0:TAIL, IT - 1, :], dram["w_downT"][(IT - 1) * P:I, :])\
                      .then_inc(loaded[w], 16)
                else:
                    nc.sync.dma_start(raw[:, w], dram[names[w]].rearrange("(f p) c -> p f c", p=P))\
                      .then_inc(loaded[w], 16)

            @block.sync
            def _(sp):
                for i, name in enumerate(("s_gate", "s_up", "s_down")):
                    sp.dma_start(scales[:, i:i + 1], dram["L1_ffn_" + name].unsqueeze(0).broadcast_to([P, 1]))\
                      .then_inc(scales_loaded, 16)
                load(GATE)
                load(DOWN)
                load(UP)

            @block.gpsimd
            def _(g):
                g.memset(rawd[:, IT - 1, :], 0.0).then_inc(constants, 1)
                g.memset(round_col[:, :], ROUND).then_inc(constants, 1)
                norm_gpsimd(k, n)

            @block.scalar
            def _(a):
                a.wait_ge(constants, 2)
                for w in (GATE, DOWN):
                    a.wait_ge(loaded[w], 32 if w == DOWN else 16)
                    a.activation(targets[w], raws[w], ACT.Abs, accum_out=total[:, w:w + 1]).then_inc(total_ready, 1)
                a.wait_ge(total_ready, 2)
                for i, w in enumerate((GATE, DOWN, UP)):
                    a.wait_ge(winv_ready, i + 1)
                    a.activation(raws[w], raws[w], ACT.Identity, bias=round_col[:, 0:1],
                                 scale=winv[:, w:w + 1]).then_inc(rounded, 1)
                for t in range(TILES):
                    a.wait_ge(x4T_psum, t + 1)
                    a.copy(x4T[:, :, t * P:(t + 1) * P],
                           T[t % 2][:, 0:256].bitcast(BF16).rearrange("p (f c) -> p f c", f=KT)).then_inc(x4T_ready, 1)

                def x8T_copy(t):
                    for half, (first, last) in enumerate(((0, 8), (8, IT))):
                        a.wait_ge(x8T_psum, 2 * t + half + 1)
                        rows = P if half == 0 else TAIL
                        source = T[half][:, :].bitcast(BF16).rearrange("p (f c) -> p f c", f=8)
                        if half == 0:
                            a.copy(x8T[:, 0:8, t * P:(t + 1) * P], source).then_inc(x8T_ready, 1)
                        else:
                            k.aown(a.copy(x8T[:, 8:IT - 1, t * P:(t + 1) * P], source[:, 0:IT - 9, :]))
                            a.copy(x8T[0:TAIL, IT - 1, t * P:(t + 1) * P], source[0:TAIL, IT - 9, :])\
                             .then_inc(x8T_ready, 1)

                for t in range(TILES):
                    for c, (c0, c1) in enumerate(CHUNKS):
                        i = NC * t + c
                        a.wait_ge(gate_psum, i + 1)
                        a.activation(relu[:, i % 2, 0:c1 - c0], G[i % 2][:, 0:c1 - c0], ACT.Relu,
                                     scale=gate_scale[:, t:t + 1]).then_inc(relu_ready, 1)
                        a.wait_ge(relu_ready, i + 1)
                        if i >= 2:
                            a.wait_ge(inner_ready, i - 1)
                        a.activation(gate[:, i % 2, 0:c1 - c0], relu[:, i % 2, 0:c1 - c0], ACT.Square)\
                         .then_inc(gate_ready, 1)
                    if t >= 1:
                        x8T_copy(t - 1)
                x8T_copy(TILES - 1)

            @block.vector
            def _(v):
                norm_vector(k, n)
                v.wait_ge(scales_loaded, 48)

                def weight_scale(i, w):
                    v.wait_ge(total_psum, i + 1)
                    k.vown(v.tensor_scalar(wmean[:, w:w + 1], k.bank[6 + i % 2][:, 0:1], 1.0 / (I * D), None, ALU.mult))
                    k.vown.wait()
                    k.vown(v.tensor_scalar(winv[:, w:w + 1], wmean[:, w:w + 1], EPS, None, ALU.add))
                    k.vown(v.tensor_tensor(wscale[:, w:w + 1], wmean[:, w:w + 1], scales[:, w:w + 1], ALU.mult))
                    k.vown.wait()
                    v.reciprocal(winv[:, w:w + 1], winv[:, w:w + 1]).then_inc(winv_ready, 1)

                def weight_round(i, w):
                    v.wait_ge(rounded, i + 1)
                    v.tensor_scalar(raws[w], raws[w], ROUND, -1.0, ALU.subtract, ALU.max).then_inc(clipped, 1)
                    v.wait_ge(clipped, i + 1)
                    v.tensor_scalar(targets[w], raws[w], 1.0, None, ALU.min).then_inc(weights_ready, 1)

                bisection_rounds(k, 2)
                weight_scale(0, GATE)
                v.wait_ge(k.xn_ready, TILES * (n + 1))
                for t in range(TILES):
                    k.vown(v.tensor_reduce(beta[:, t:t + 1], k.xn[:, t, :], AX.X, ALU.add, apply_absolute_value=True))
                k.vown.wait()
                k.vown(v.tensor_scalar(beta[:, :], beta[:, :], 1.0 / D, None, ALU.mult))
                k.vown.wait()
                k.vown(v.tensor_scalar(betae[:, :], beta[:, :], EPS, None, ALU.add))
                k.vown.wait()
                k.vown(v.reciprocal(binv[:, :], betae[:, :]))
                k.vown.wait()
                for t in range(TILES):
                    k.vown(v.tensor_scalar(t1[:, t, :], k.xn[:, t, :], SQRT7, binv[:, t:t + 1], ALU.mult, ALU.mult))
                k.vown.wait()
                for t in range(TILES):
                    k.vown(v.tensor_scalar(t1[:, t, :], t1[:, t, :], ROUND, ROUND, ALU.add, ALU.subtract))
                k.vown.wait()
                for t in range(TILES):
                    v.tensor_scalar(x4[:, t, :], t1[:, t, :], -8.0, 7.0, ALU.max, ALU.min).then_inc(x4_ready, 1)
                weight_scale(1, DOWN)
                v.wait_ge(loaded[UP], 16)
                v.tensor_reduce(total[:, UP:UP + 1], raws[UP], AX.X, ALU.add, apply_absolute_value=True)\
                 .then_inc(up_total_ready, 1)
                weight_scale(2, UP)
                for i, w in enumerate((GATE, DOWN, UP)):
                    weight_round(i, w)
                k.vown(v.tensor_scalar(betae[:, :], beta[:, :], SQRT7, 1.0 / SQRT7, ALU.mult, ALU.mult))
                k.vown.wait()
                k.vown(v.tensor_scalar(up_scale[:, :], betae[:, :], wscale[:, UP:UP + 1], None, ALU.mult))
                k.vown(v.tensor_scalar(gate_scale[:, :], betae[:, :], wscale[:, GATE:GATE + 1], None, ALU.mult))
                k.vown.wait()
                v.engine_nop().then_inc(constants, 1)

                def quantise8(t):
                    k.vown(v.tensor_reduce(gamma[:, t:t + 1], inner[:, t % 2, :], AX.X, ALU.max, apply_absolute_value=True))
                    k.vown.wait()
                    k.vown(v.tensor_scalar(gammae[:, t:t + 1], gamma[:, t:t + 1], EPS, None, ALU.add))
                    k.vown.wait()
                    k.vown(v.reciprocal(ginv[:, t:t + 1], gammae[:, t:t + 1]))
                    k.vown.wait()
                    k.vown(v.tensor_scalar(inner[:, t % 2, :], inner[:, t % 2, :], 127.0, ginv[:, t:t + 1],
                                           ALU.mult, ALU.mult))
                    k.vown.wait()
                    k.vown(v.tensor_scalar(inner[:, t % 2, :], inner[:, t % 2, :], ROUND, ROUND, ALU.add, ALU.subtract))
                    k.vown.wait()
                    if t >= 2:
                        v.wait_ge(x8T_psum, 2 * (t - 1))
                    v.tensor_scalar(x8[:, t % 2, :], inner[:, t % 2, :], -128.0, 127.0, ALU.max, ALU.min)\
                     .then_inc(x8_ready, 1)

                for t in range(TILES):
                    for c, (c0, c1) in enumerate(CHUNKS):
                        i = NC * t + c
                        v.wait_ge(up_psum, i + 1)
                        v.wait_ge(gate_ready, i + 1)
                        if t >= 2:
                            v.wait_ge(x8_ready, t - 1)
                        v.scalar_tensor_tensor(inner[:, t % 2, c0:c1], U[i % 2][:, 0:c1 - c0], up_scale[:, t:t + 1],
                                               gate[:, i % 2, 0:c1 - c0], ALU.mult, ALU.mult).then_inc(inner_ready, 1)
                    v.wait_ge(inner_ready, NC * (t + 1))
                    quantise8(t)
                k.vown(v.tensor_scalar(gammae[:, :], gamma[:, :], 1.0 / 127.0, wscale[:, DOWN:DOWN + 1], ALU.mult, ALU.mult))
                k.vown.wait()
                for t in range(TILES):
                    v.wait_ge(down_psum, t + 1)
                    k.vown(v.scalar_tensor_tensor(k.x[:, t, :], O[t % 2][:, :], gammae[:, t:t + 1], k.x[:, t, :],
                                                  ALU.mult, ALU.add))
                    k.vown.wait()
                    v.engine_nop().then_inc(clipped, 1)

            @block.tensor
            def _(pe):
                for i, w in enumerate((GATE, DOWN, UP)):
                    if w == UP:
                        pe.wait_ge(up_total_ready, 1)
                    else:
                        pe.wait_ge(total_ready, i + 1)
                    if i >= 2:
                        pe.wait_ge(winv_ready, i - 1)
                    pe.matmul(k.bank[6 + i % 2][:, 0:1], k.ones[:, :], total[:, w:w + 1], start=True, stop=True)\
                      .then_inc(total_psum, 1)
                for t in range(TILES):
                    pe.wait_ge(x4_ready, t + 1)
                    if t >= 2:
                        pe.wait_ge(x4T_ready, t - 1)
                    for f in range(KT):
                        last = pe.transpose(T[t % 2][:, 0:256].bitcast(BF16)[:, f * P:(f + 1) * P],
                                            x4[:, t, f * P:(f + 1) * P], k.ident16[:, :])
                    last.then_inc(x4T_psum, 1)
                pe.wait_ge(x4T_ready, TILES)
                pe.wait_ge(weights_ready, 3)
                pe.wait_ge(constants, 3)

                def turn8(t):
                    pe.wait_ge(x8_ready, t + 1)
                    for f in range(IT):
                        rows = P if f < IT - 1 else TAIL
                        half = f // 8
                        if f % 8 == 0 and t >= 1:
                            pe.wait_ge(x8T_ready, 2 * (t - 1) + half + 1)
                        last = pe.transpose(T[half][:, :].bitcast(BF16)[0:rows, f % 8 * P:(f % 8 + 1) * P],
                                            x8[:, t % 2, f * P:f * P + rows], k.ident16[:, :])
                        if f in (7, IT - 1):
                            last.then_inc(x8T_psum, 1)

                for t in range(TILES):
                    for c, (c0, c1) in enumerate(CHUNKS):
                        i = NC * t + c
                        if i >= 2:
                            pe.wait_ge(relu_ready, i - 1)
                            pe.wait_ge(inner_ready, i - 1)
                        for w, bank, ready in ((GATE, G, gate_psum), (UP, U, up_psum)):
                            for f in range(KT):
                                last = pe.matmul(bank[i % 2][:, 0:c1 - c0], x4T[:, f, t * P:(t + 1) * P],
                                                 wgu[:, w, f, c0:c1], start=f == 0, stop=f == KT - 1)
                            last.then_inc(ready, 1)
                    if t >= 1:
                        turn8(t - 1)
                turn8(TILES - 1)
                for t in range(TILES):
                    pe.wait_ge(x8T_ready, 2 * (t + 1))
                    if t >= 2:
                        pe.wait_ge(clipped, 3 + t - 1)
                    for f in range(IT):
                        rows = P if f < IT - 1 else TAIL
                        last = pe.matmul(O[t % 2][:, :], x8T[0:rows, f, t * P:(t + 1) * P], wd[0:rows, f, :],
                                         start=f == 0, stop=f == IT - 1)
                    last.then_inc(down_psum, 1)



PARTS = ((0, 0), (0, 1), (1, 0))


def layer2_attention(k, dram):
    nc, n = k.nc, k.norms
    k.norms += 1
    HEADS, GROUPS, HD = 32, 8, 128
    REP = HEADS // GROUPS
    GW = REP * HD
    STEPS = GROUPS * B
    UNITS = REP * TPB
    PAIRS = UNITS // 2
    CHUNKS = 1 + TPB
    KV = CPB // 2
    SCALE = HD ** -0.5
    KEYS = TPB
    TURNS = (0, KEYS, 1)
    COPY_Q_AT, COPY_KV_AT, ROWS_HIGH_AT, MIX_HIGH_AT = (1, 2), (2, 4), (4, 7), (3, 5)
    VALUES_LOW_AT, ROWS_LOW_AT, MIX_LOW_AT, OUTS_AT = (3, 4), (5, 7), (4, 6), (5, 7)
    COUNTS = (1, 1, 1, 1, 0, 0, 0, 0)
    OWN_V, OWN_P = BISECT_PER_ROUND * sum(COUNTS) // 4, 2 * CHUNKS
    with ExitStack() as s:
        xnT2 = k.sbuf("xnT2", [P, 2, KT, TILES * P], F32R, s)
        ctxT2 = k.sbuf("ctxT2", [P, 2, KT, B * CTX], F32R, s)
        raw_kv = k.sbuf("raw_kv", [P, KT, 2 * HD], F32, s)
        raw_q = k.sbuf("raw_q", [P, KT, GW], F32, s)
        raw_o = k.sbuf("raw_o", [P, REP, D], F32, s)
        wq = k.sbuf("wq2", [P, 2, KT, GW], F32R, s)
        wkv = k.sbuf("wkv2", [P, 2, KT, 2 * HD], F32R, s)
        wo = k.sbuf("wo2", [P, 2, REP, D], F32R, s)
        rows = k.xn
        k.flags = k.xn[:, 3, :].bitcast(BF16).rearrange("p (j c) -> p j c", j=2)
        masked = k.xnT[:, 0:2, :]
        squares = k.xnT[:, 2:4, :]
        ssq = k.sbuf("ssq", [P, CHUNKS, REP], F32, s)
        headsT = k.sbuf("headsT", [P, 2, REP, TILES * P], F32R, s)
        keysT = k.sbuf("keysT2", [P, 2, B * CTX], F32R, s)
        values = k.sbuf("values2", [P, 2, CTILES, HD], F32R, s)
        mask = k.sbuf("mask", [P, TPB, CTX], F32, s)
        weights = k.sbuf("norm_weights", [P, 2], F32, s)
        keyscale = weights
        probs = k.sbuf("probs2", [P, 3, CTX], F32, s)
        probsT = k.sbuf("probsT2", [P, 2, 2, CPB, SEQ], F32R, s)
        statistics = k.stats[:, :, :].rearrange("p t s -> p (t s)")
        negmax, sums, inverse = (statistics[:, j * UNITS:(j + 1) * UNITS] for j in range(3))
        names = ("mask_loaded", "kv_loaded", "q_loaded", "o_loaded", "kv_weights_high", "q_weights_high", "o_weights_high",
                 "kv_weights_low", "q_weights_low", "o_weights_low", "ctx_high", "ctx_low", "xnT_psum", "xnT_high", "xnT_low",
                 "keyscale_ready", "stepped", "kv_psum", "q_psum", "rows_copied",
                 "gpsimd_steps", "rows_normed", "rowsT_psum", "rowsT_high", "rowsT_low", "values_high",
                 "values_low", "scores_psum", "max_ready", "exp_ready", "inverse_ready", "probs_ready", "probsT_psum",
                 "probsT_high", "probsT_low", "mix_psum", "mixT_high", "mixT_low", "out_psum", "out_added", "bisection")
        S_ = {x: k.sem(f"l2a_{x}") for x in names}
        S, T, V, R, J = k.bank[0:2], k.bank[2:4], k.bank[4], k.bank[5], k.bank[6:8]
        wq_dram = dram["wqT"].rearrange("(f p) (g c) -> g p f c", p=P, c=GW)
        wkv_dram = dram["wkvT"].rearrange("(f p) (g c) -> g p f c", p=P, c=2 * HD)
        wo_dram = dram["woT"].rearrange("(g h p) c -> g p h c", p=P, h=REP)
        batch = lambda step: step[1] % B

        def group(step):
            i, offset = step
            return offset // 2 if i is None else i + offset // 2

        def turned(step, c):
            b, source = batch(step), (J[0] if c == KEYS else R)[:, :]
            if c == KEYS:
                return [keysT[:, part, b * CTX:(b + 1) * CTX] for part in range(2)], source
            t = b * TPB + c
            return ([headsT[:, part, :, t * P:(t + 1) * P] for part in range(2)],
                    source.rearrange("p (h q) -> p h q", h=REP))

        with nc.Block(no_gpsimd_drain=True) as block:

            @block.sync
            def _(sp):
                def load_kv(group):
                    sp.dma_start(raw_kv[:, :, :], wkv_dram[group]).then_inc(S_["kv_loaded"], 16)

                def load_q(group):
                    sp.dma_start(raw_q[:, :, :], wq_dram[group]).then_inc(S_["q_loaded"], 16)

                def load_o(group):
                    sp.dma_start(raw_o[:, :, :], wo_dram[group]).then_inc(S_["o_loaded"], 16)

                load_q(0)
                load_kv(0)
                sp.dma_start(mask[:, :, :], dram["mask_1x1xSxS2_ff0"][0, 0].rearrange("(t p) c -> p t c", p=P))\
                  .then_inc(S_["mask_loaded"], 16)
                for i, name in enumerate(("q_norm_w", "k_norm_w")):
                    sp.dma_start(weights[:, i:i + 1], dram["L2_xattn_" + name].unsqueeze(1)).then_inc(S_["mask_loaded"], 16)
                load_o(0)
                with sp.Fori(0, GROUPS) as i:
                    sp.wait_ge(S_["q_weights_low"], i + 1)
                    load_q(i + 1)
                    sp.wait_ge(S_["kv_weights_low"], i + 1)
                    load_kv(i + 1)
                    sp.wait_ge(S_["o_weights_low"], 2 * i + 2)
                    load_o(i + 1)

            @block.gpsimd
            def _(g):
                norm_gpsimd(k, n)

                def weights_low(target, source, high, value, done):
                    g.wait_ge(high, value)
                    g.tensor_tensor(target[:, 1], source, target[:, 0], ALU.subtract).then_inc(done, 1)

                def kv_weights_low(step):
                    weights_low(wkv, raw_kv[:, :, :], S_["kv_weights_high"], group(step) + 2, S_["kv_weights_low"])

                def q_weights_low(step):
                    weights_low(wq, raw_q[:, :, :], S_["q_weights_high"], group(step) + 2, S_["q_weights_low"])

                def o_weights_low(step, half):
                    heads = slice(half * REP // 2, (half + 1) * REP // 2)
                    if half == 0:
                        g.wait_ge(S_["o_weights_high"], group(step) + 1)
                    g.tensor_tensor(wo[:, 1, heads], raw_o[:, heads], wo[:, 0, heads], ALU.subtract)\
                     .then_inc(S_["o_weights_low"], 1)

                def norm(step, own, c):
                    g.wait_ge(S_["rows_copied"], at(step, KV + TPB, TPB + KV if c == KEYS else c + 1))
                    g.sem_inc(S_["stepped"], 1)
                    own(g.tensor_scalar(ssq[:, c, :], ssq[:, c, :], 1.0 / HD, EPS, ALU.mult, ALU.add))
                    own.wait()
                    own(g.tensor_tensor(ssq[:, c, :], ssq[:, c, :], k.minus_half[:, 0:REP], ALU.pow))
                    own.wait()
                    r = rows[:, c, :].rearrange("p (h d) -> p h d", d=HD)
                    g.tensor_tensor(r, r, ssq[:, c, :].unsqueeze(2).broadcast_to([P, REP, HD]), ALU.mult)\
                     .then_inc(S_["rows_normed"], 1)

                def run(step, last=False):
                    new_o_weights = step[1] % 2 == 1 and step[1] > 0
                    if new_o_weights:
                        o_weights_low(step, 0)
                        if last:
                            o_weights_low(step, 1)
                            return
                    following = after(step)
                    own = StepOwn(g, S_["gpsimd_steps"], following, OWN_P)
                    for c in range(CHUNKS):
                        norm(following, own, c)
                        if c == 0 and new_o_weights:
                            o_weights_low(step, 1)
                        if c == 1 and step[1] % 2 == 0:
                            q_weights_low(step)
                    assert own.count == OWN_P
                    if step[1] % 2 == 0:
                        kv_weights_low(step)

                weights_low(wq, raw_q[:, :, :], S_["q_weights_high"], 1, S_["q_weights_low"])
                weights_low(wkv, raw_kv[:, :, :], S_["kv_weights_high"], 1, S_["kv_weights_low"])
                run((None, -1))
                run((None, 0))
                with g.Fori(0, STEPS // 2 - 1) as i:
                    run((i, 1))
                    run((i, 2))
                run((None, STEPS - 1), last=True)

            @block.tensor
            def _(pe):
                def product(out, stationary, moving, half=None):
                    count = len(stationary)
                    tiles = range(count) if half is None else range(count)[half * count // 2:(half + 1) * count // 2]
                    for f in tiles:
                        for x, (a, b) in enumerate(PARTS):
                            last = pe.matmul(out, stationary[f][a], moving[f][b], start=f == 0 and x == 0,
                                             stop=f == count - 1 and x == 2)
                    return last

                def project_kv(step, j):
                    pe.wait_ge(S_["rows_copied"], at(step, KV + TPB, j + 1))
                    for h in range(2):
                        r = batch(step) * CPB + 2 * j + h
                        last = product(J[j][:, h * 2 * HD:(h + 1) * 2 * HD],
                                       [[ctxT2[:, a, f, r * P:(r + 1) * P] for a in range(2)] for f in range(KT)],
                                       [[wkv[:, b, f, :] for b in range(2)] for f in range(KT)])
                    last.then_inc(S_["kv_psum"], 1)

                def project_q(step, t, half):
                    if half == 0 and t == 0 and not is_start(step):
                        pe.wait_ge(S_["rowsT_low"], at(step, CHUNKS, -1))
                    elif half == 0 and step[0] is None and step[1] == 1:
                        pe.wait_ge(S_["values_low"], t + 1)
                    elif half == 0 and not is_start(step):
                        pe.wait_ge(S_["out_added"], at(after(step, -2), TPB, t + 1))
                    token = (batch(step) * TPB + t) * P
                    last = product(J[t][:, :],
                                   [[xnT2[:, a, f, token:token + P] for a in range(2)] for f in range(KT)],
                                   [[wq[:, b, f, :] for b in range(2)] for f in range(KT)], half)
                    if half == 1:
                        last.then_inc(S_["q_psum"], 1)

                def project_out(step, t, half):
                    token = (batch(step) * TPB + t) * P
                    last = product(J[t][:, :],
                                   [[headsT[:, a, h, token:token + P] for a in range(2)] for h in range(REP)],
                                   [[wo[:, x, h, :] for x in range(2)] for h in range(REP)], half)
                    if half == 1:
                        last.then_inc(S_["out_psum"], 1)

                def turn_rows(step, c):
                    if c == KEYS and step[0] is None and step[1] < 2:
                        pe.wait_ge(S_["values_low"], at(step, KV, 1))
                    elif c == KEYS:
                        pe.wait_ge(S_["out_added"], at(step, TPB, -1))
                    elif c == 1 or not is_start(step):
                        pe.wait_ge(S_["rowsT_low"], at(step, CHUNKS, c))
                    pe.wait_ge(S_["rows_normed"], at(step, CHUNKS, c + 1))
                    for h in range(REP):
                        last = pe.transpose((J[0] if c == KEYS else R)[:, h * P:(h + 1) * P], rows[:, c, h * P:(h + 1) * P], k.ident[:, :])
                    last.then_inc(S_["rowsT_psum"], 1)

                def scores(step, u):
                    h, q = u // TPB, u % TPB
                    if not is_start(step) or u >= 2:
                        pe.wait_ge(S_["max_ready"], at(step, UNITS, u - 1))
                    if u < TPB:
                        pe.wait_ge(S_["rowsT_low"], at(step, CHUNKS, u + 2))
                    b = batch(step)
                    token = (b * TPB + q) * P
                    product(S[u % 2][:, :], [[headsT[:, a, h, token:token + P] for a in range(2)]],
                            [[keysT[:, x, b * CTX:(b + 1) * CTX] for x in range(2)]]).then_inc(S_["scores_psum"], 1)

                def turn_probs(step, u):
                    if not is_start(step) or u >= 2:
                        pe.wait_ge(S_["probsT_low"], at(step, UNITS, u - 1))
                    pe.wait_ge(S_["probs_ready"], at(step, UNITS, u + 1))
                    for c in range(CPB):
                        last = pe.transpose(T[u % 2][:, c * P:(c + 1) * P], probs[:, u % 3, c * P:(c + 1) * P],
                                            k.ident[:, :])
                    last.then_inc(S_["probsT_psum"], 1)

                def mix(step, p):
                    if not is_start(step) or p >= 1:
                        pe.wait_ge(S_["mixT_low"], at(step, PAIRS, p))
                    pe.wait_ge(S_["probsT_low"], at(step, UNITS, 2 * p + 2))
                    product(V[:, 0:SEQ],
                            [[values[:, a, batch(step) * CPB + c, :] for a in range(2)] for c in range(CPB)],
                            [[probsT[:, x, p % 2, c, :] for x in range(2)] for c in range(CPB)])\
                        .then_inc(S_["mix_psum"], 1)

                def fill(step, u, first, last):
                    following, before = after(step), after(step, -1)
                    if not last:
                        if u == 0:
                            pe.wait_ge(S_["q_weights_low"], group(following) + 1)
                        if u < TPB:
                            project_q(following, u, 0)
                            project_q(following, u, 1)
                        if u == TPB:
                            pe.wait_ge(S_["kv_weights_low"], group(following) + 1)
                        if TPB <= u < TPB + KV:
                            project_kv(following, u - TPB)
                    if not first and u in (4, 5):
                        if u == 4:
                            pe.wait_ge(S_["o_weights_low"], 2 * group(before) + 2)
                            pe.wait_ge(S_["mixT_low"], at(before, PAIRS, PAIRS))
                        if last:
                            pe.wait_ge(S_["out_added"], at(before, TPB, u - 4 + 1))
                        else:
                            pe.wait_ge(S_["values_low"], at(following, KV, u - 4 + 1))
                    if not first and u == 4:
                        project_out(before, 0, 0)
                        project_out(before, 0, 1)
                    if not first and u in (5, 6):
                        project_out(before, 1, u - 5)
                    if not last and u in (4, 6, 7):
                        turn_rows(following, TURNS[(4, 6, 7).index(u)])

                def run(step, first=False, last=False):
                    for u in range(UNITS):
                        fill(step, u, first, last)
                        turn_probs(step, u)
                        if u + 2 < UNITS:
                            scores(step, u + 2)
                        if u >= 2 and u % 2 == 0:
                            mix(step, u // 2 - 1)
                    if not last:
                        scores(after(step), 0)
                    mix(step, PAIRS - 1)
                    if not last:
                        scores(after(step), 1)

                norm_tensor_two(k, n, T, S_["xnT_psum"], S_["xnT_low"])
                pe.wait_ge(S_["xnT_low"], TILES)
                pe.wait_ge(S_["ctx_low"], CTILES)
                pe.wait_ge(S_["q_weights_low"], 1)
                start = (None, 0)
                for t in range(TPB):
                    project_q(start, t, 0)
                    project_q(start, t, 1)
                pe.wait_ge(S_["kv_weights_low"], 1)
                for j in range(KV):
                    project_kv(start, j)
                for c in TURNS:
                    turn_rows(start, c)
                scores(start, 0)
                scores(start, 1)
                run(start, first=True)
                with pe.Fori(0, STEPS // 2 - 1) as i:
                    run((i, 1))
                    run((i, 2))
                run((None, STEPS - 1), last=True)
                for t in range(TPB):
                    if t == 0:
                        pe.wait_ge(S_["mixT_low"], PAIRS * STEPS)
                    pe.wait_ge(S_["out_added"], TPB * (STEPS - 1) + t + 1)
                    project_out((None, STEPS - 1), t, 0)
                    project_out((None, STEPS - 1), t, 1)

            @block.scalar
            def _(a):
                def sum_squares(c, h, source):
                    return a.activation(squares[:, c % 2, h * HD:(h + 1) * HD], source, ACT.Square,
                                        accum_out=ssq[:, c, h:h + 1])

                def copy_kv(step, j):
                    a.wait_ge(S_["kv_psum"], at(step, KV, j + 1))
                    both = J[j][:, :].rearrange("p (r c) -> p r c", r=2)
                    a.copy(rows[:, KEYS, j * 2 * HD:(j + 1) * 2 * HD].rearrange("p (r c) -> p r c", r=2), both[:, :, 0:HD])
                    for r in range(2):
                        last = sum_squares(KEYS, 2 * j + r, both[:, r, 0:HD])
                    last.then_inc(S_["rows_copied"], 1)
                    r = batch(step) * CPB + 2 * j
                    a.copy(values[:, 0, r:r + 2, :], both[:, :, HD:2 * HD]).then_inc(S_["values_high"], 1)

                def copy_q(step, t):
                    a.wait_ge(S_["q_psum"], at(step, TPB, t + 1))
                    a.copy(rows[:, t, :], J[t][:, :])
                    for h in range(REP):
                        last = sum_squares(t, h, J[t][:, h * HD:(h + 1) * HD])
                    last.then_inc(S_["rows_copied"], 1)

                def rowsT_high(step, c):
                    a.wait_ge(S_["rowsT_psum"], at(step, CHUNKS, TURNS.index(c) + 1))
                    (high, _), source = turned(step, c)
                    if c == KEYS:
                        a.activation(high, source, ACT.Copy, scale=keyscale[:, 0:1]).then_inc(S_["rowsT_high"], 1)
                    else:
                        a.copy(high, source).then_inc(S_["rowsT_high"], 1)

                def exponentials(step, u):
                    a.wait_ge(S_["max_ready"], at(step, UNITS, u + 1))
                    if u >= 3:
                        a.wait_ge(S_["probsT_psum"], at(step, UNITS, u - 2))
                    elif not is_start(step):
                        a.wait_ge(S_["probsT_psum"], at(step, UNITS, min(u - 1, 0)))
                    a.activation(probs[:, u % 3, :], masked[:, u % 2, :], ACT.Exp, bias=negmax[:, u:u + 1],
                                 scale=-1.0, accum_out=sums[:, u:u + 1]).then_inc(S_["exp_ready"], 1)

                def divide(step, u):
                    a.wait_ge(S_["inverse_ready"], at(step, UNITS, u + 1))
                    a.activation(probs[:, u % 3, :], probs[:, u % 3, :], ACT.Copy, scale=inverse[:, u:u + 1])\
                     .then_inc(S_["probs_ready"], 1)

                def probsT_high(step, u):
                    p = u // 2
                    a.wait_ge(S_["probsT_psum"], at(step, UNITS, u + 1))
                    if not is_start(step) or p >= 2:
                        a.wait_ge(S_["mix_psum"], at(step, PAIRS, p - 1))
                    a.copy(probsT[:, 0, p % 2, :, u % 2 * P:(u % 2 + 1) * P],
                           T[u % 2][:, :].rearrange("p (c q) -> p c q", c=CPB)).then_inc(S_["probsT_high"], 1)

                def mixT_high(step, p):
                    b = batch(step)
                    a.wait_ge(S_["mix_psum"], at(step, PAIRS, p + 1))
                    a.copy(headsT[:, 0, p, b * SEQ:(b + 1) * SEQ], V[:, 0:SEQ]).then_inc(S_["mixT_high"], 1)

                def kv_weights_high(group):
                    a.wait_ge(S_["kv_loaded"], 16 * group + 16)
                    a.copy(wkv[:, 0], raw_kv[:, :, :]).then_inc(S_["kv_weights_high"], 1)

                def q_weights_high(group):
                    a.wait_ge(S_["q_loaded"], 16 * group + 16)
                    a.copy(wq[:, 0], raw_q[:, :, :]).then_inc(S_["q_weights_high"], 1)

                def o_weights_high(step):
                    a.wait_ge(S_["o_loaded"], 16 * group(step) + 16)
                    if not is_start(after(step, -1)):
                        a.wait_ge(S_["out_psum"], at(after(step, -2), TPB, TPB))
                    a.copy(wo[:, 0], raw_o[:, :, :]).then_inc(S_["o_weights_high"], 1)

                def run(step, first=False, last=False):
                    following, before = after(step), after(step, -1)
                    for u in range(UNITS):
                        divide(step, u)
                        if u:
                            probsT_high(step, u - 1)
                        if u + 1 < UNITS:
                            exponentials(step, u + 1)
                        if u == 1 and not first:
                            mixT_high(before, PAIRS - 1)
                        if u in MIX_HIGH_AT:
                            mixT_high(step, MIX_HIGH_AT.index(u))
                        if not last:
                            if u in COPY_Q_AT:
                                copy_q(following, COPY_Q_AT.index(u))
                            if u in COPY_KV_AT:
                                copy_kv(following, COPY_KV_AT.index(u))
                            if u in ROWS_HIGH_AT:
                                rowsT_high(following, TURNS[ROWS_HIGH_AT.index(u)])
                            if step[1] % 2 == 0 and u == 3:
                                q_weights_high(group(step) + 1)
                            if step[1] % 2 == 0 and u == 5:
                                kv_weights_high(group(step) + 1)
                        if step[1] % 2 == 1 and u == 0:
                            o_weights_high(step)
                    mixT_high(step, PAIRS - 2)
                    if not last:
                        rowsT_high(following, TURNS[2])
                    probsT_high(step, UNITS - 1)
                    if not last:
                        exponentials(following, 0)

                for r in range(CTILES):
                    a.activation(row_tile(ctxT2[:, 0], r), row_tile(k.ctxT, r), ACT.Copy, scale=k.sign[:, r:r + 1])\
                     .then_inc(S_["ctx_high"], 1)
                q_weights_high(0)
                for t in range(TILES):
                    a.wait_ge(S_["xnT_psum"], t + 1)
                    a.copy(xnT2[:, 0, :, t * P:(t + 1) * P], T[t % 2][:, :].rearrange("p (f c) -> p f c", f=KT))\
                     .then_inc(S_["xnT_high"], 1)
                kv_weights_high(0)
                a.wait_ge(S_["keyscale_ready"], 1)
                start = (None, 0)
                for t in range(TPB):
                    copy_q(start, t)
                for j in range(KV):
                    copy_kv(start, j)
                for c in TURNS:
                    rowsT_high(start, c)
                exponentials(start, 0)
                run(start, first=True)
                with a.Fori(0, STEPS // 2 - 1) as i:
                    run((i, 1))
                    run((i, 2))
                run((None, STEPS - 1), last=True)
                mixT_high((None, STEPS - 1), PAIRS - 1)

            @block.vector
            def _(v):
                def values_low(step, j):
                    v.wait_ge(S_["values_high"], at(step, KV, j + 1))
                    r = batch(step) * CPB + 2 * j
                    v.tensor_tensor(values[:, 1, r:r + 2, :], J[j][:, :].rearrange("p (r c) -> p r c", r=2)[:, :, HD:2 * HD],
                                    values[:, 0, r:r + 2, :], ALU.subtract).then_inc(S_["values_low"], 1)

                def rowsT_low(step, c):
                    v.wait_ge(S_["rowsT_high"], at(step, CHUNKS, TURNS.index(c) + 1))
                    (high, low), source = turned(step, c)
                    if c == KEYS:
                        v.scalar_tensor_tensor(low, source, keyscale[:, 0:1], high, ALU.mult, ALU.subtract)\
                         .then_inc(S_["rowsT_low"], 1)
                    else:
                        v.tensor_tensor(low, source, high, ALU.subtract).then_inc(S_["rowsT_low"], 1)

                def maximum(step, u):
                    v.wait_ge(S_["scores_psum"], at(step, UNITS, u + 1))
                    v.sem_inc(S_["stepped"], 1)
                    v.tensor_tensor_reduce(masked[:, u % 2, :], S[u % 2][:, :], mask[:, u % TPB, :], -1.0, 3.4e38,
                                           ALU.add, ALU.min, negmax[:, u:u + 1]).then_inc(S_["max_ready"], 1)

                def invert(step, u):
                    v.wait_ge(S_["exp_ready"], at(step, UNITS, u + 1))
                    v.reciprocal(inverse[:, u:u + 1], sums[:, u:u + 1]).then_inc(S_["inverse_ready"], 1)

                def probsT_low(step, u):
                    p = u // 2
                    v.wait_ge(S_["probsT_high"], at(step, UNITS, u + 1))
                    columns = slice(u % 2 * P, (u % 2 + 1) * P)
                    v.tensor_tensor(probsT[:, 1, p % 2, :, columns], T[u % 2][:, :].rearrange("p (c q) -> p c q", c=CPB),
                                    probsT[:, 0, p % 2, :, columns], ALU.subtract).then_inc(S_["probsT_low"], 1)

                def mixT_low(step, p):
                    b = batch(step)
                    v.wait_ge(S_["mixT_high"], at(step, PAIRS, p + 1))
                    v.tensor_tensor(headsT[:, 1, p, b * SEQ:(b + 1) * SEQ], V[:, 0:SEQ],
                                    headsT[:, 0, p, b * SEQ:(b + 1) * SEQ], ALU.subtract).then_inc(S_["mixT_low"], 1)

                def add_out(step, t):
                    v.wait_ge(S_["out_psum"], at(step, TPB, t + 1))
                    tile = batch(step) * TPB + t
                    v.tensor_tensor(k.x[:, tile, :], J[t][:, :], k.x[:, tile, :], ALU.add).then_inc(S_["out_added"], 1)

                def run(step, first=False, last=False):
                    following, before = after(step), after(step, -1)
                    own = StepOwn(v, S_["bisection"], step, OWN_V)
                    for u in range(UNITS):
                        invert(step, u)
                        if u + 1 < UNITS:
                            maximum(step, u + 1)
                        if u:
                            probsT_low(step, u - 1)
                        if u == 1 and not first:
                            mixT_low(before, PAIRS - 1)
                        if u in MIX_LOW_AT:
                            mixT_low(step, MIX_LOW_AT.index(u))
                        if not last:
                            if u in VALUES_LOW_AT:
                                values_low(following, VALUES_LOW_AT.index(u))
                            if u in ROWS_LOW_AT:
                                rowsT_low(following, TURNS[ROWS_LOW_AT.index(u)])
                        if not first and u in OUTS_AT:
                            add_out(before, OUTS_AT.index(u))
                        for c in range(sum(COUNTS[:u]), sum(COUNTS[:u + 1])):
                            bisection_count(k, own, c % 4)
                            if c % 4 == 3:
                                bisection_update(k, own)
                    mixT_low(step, PAIRS - 2)
                    if not last:
                        rowsT_low(following, TURNS[2])
                    probsT_low(step, UNITS - 1)
                    if not last:
                        maximum(following, 0)
                    assert own.count == OWN_V, own.count

                norm_vector(k, n)
                for r in range(CTILES):
                    v.wait_ge(S_["ctx_high"], r + 1)
                    v.scalar_tensor_tensor(row_tile(ctxT2[:, 1], r), row_tile(k.ctxT, r), k.sign[:, r:r + 1],
                                           row_tile(ctxT2[:, 0], r), ALU.mult, ALU.subtract).then_inc(S_["ctx_low"], 1)
                for t in range(TILES):
                    v.wait_ge(S_["xnT_high"], t + 1)
                    v.tensor_tensor(xnT2[:, 1, :, t * P:(t + 1) * P], T[t % 2][:, :].rearrange("p (f c) -> p f c", f=KT),
                                    xnT2[:, 0, :, t * P:(t + 1) * P], ALU.subtract).then_inc(S_["xnT_low"], 1)
                v.wait_ge(S_["mask_loaded"], 48)
                v.scalar_tensor_tensor(keyscale[:, 0:1], weights[:, 0:1], SCALE, weights[:, 1:2], ALU.mult, ALU.mult)\
                 .then_inc(S_["keyscale_ready"], 1)
                start = (None, 0)
                bisection_rounds(k, 2)
                for j in range(KV):
                    values_low(start, j)
                bisection_rounds(k, 2)
                for c in TURNS:
                    rowsT_low(start, c)
                maximum(start, 0)
                v.sem_inc(S_["out_added"], TPB)
                run(start, first=True)
                with v.Fori(0, STEPS // 2 - 1) as i:
                    run((i, 1))
                    run((i, 2))
                run((None, STEPS - 1), last=True)
                mixT_low((None, STEPS - 1), PAIRS - 1)
                for t in range(TPB):
                    add_out((None, STEPS - 1), t)
                v.wait_ge(S_["out_added"], TPB * (STEPS + 1))
                v.wait_ge(S_["bisection"], STEPS * OWN_V)


def norm_tensor_two(k, n, banks, in_psum, low_ready):
    pe = k.nc.tensor
    for t in range(TILES):
        pe.wait_ge(k.xn_ready, TILES * n + t + 1)
        if t >= 2:
            pe.wait_ge(low_ready, t - 1)
        for f in range(KT):
            last = pe.transpose(banks[t % 2][:, f * P:(f + 1) * P], k.xn[:, t, f * P:(f + 1) * P], k.ident[:, :])
        last.then_inc(in_psum, 1)



TOPK = 154
BISECT_PER_ROUND = 8 + 5


def bisection_buffers(k):
    k.sign = k.sbuf("sign", [P, CTILES], F32)
    k.rank = k.sbuf("rank", [P, CTILES], F32)
    k.counts = k.sbuf("counts", [P, CTILES], F32)
    k.found = k.sbuf("found", [P, CTILES], I32)
    k.candidate = k.sbuf("candidate", [P, CTILES], I32)
    k.bit = k.sbuf("bit", [P, CTILES], I32)
    k.enough = k.sbuf("enough", [P, CTILES], F32)
    k.set_bit = k.sbuf("set_bit", [P, CTILES], I32)


def row_tile(ctxT, r):
    return ctxT[:, r // B, r % B * CTX:(r % B + 1) * CTX]


def bisection_start(k):
    v, own = k.nc.vector, k.vown
    for r in range(CTILES):
        if r >= 2:
            own.wait()
        own(v.tensor_scalar(k.flags[:, r % 2], row_tile(k.ctxT, r), 0.0, 0.0, ALU.is_ge, ALU.add,
                            accum_out=k.counts[:, r:r + 1]))
    own(v.memset(k.found[:, :], 0))
    own(v.memset(k.bit[:, :], 2 ** 30))
    own(v.memset(k.candidate[:, :], 2 ** 30))
    own.wait()
    own(v.tensor_scalar(k.enough[:, :], k.counts[:, :], float(TOPK), None, ALU.is_lt))
    own.wait()
    own(v.tensor_scalar(k.sign[:, :], k.enough[:, :], -2.0, 1.0, ALU.mult, ALU.add))
    own(v.tensor_scalar(k.rank[:, :], k.enough[:, :], float(CTX + 1 - 2 * TOPK), float(TOPK), ALU.mult, ALU.add))
    own.wait()
    for r in range(CTILES):
        own(v.tensor_scalar(row_tile(k.ctxT, r), row_tile(k.ctxT, r), k.sign[:, r:r + 1], None, ALU.mult))
    own.wait()


def bisection_count(k, own, j):
    own.wait()
    for r in (2 * j, 2 * j + 1):
        own(k.nc.vector.tensor_scalar(k.flags[:, r % 2], row_tile(k.ctxT, r), k.candidate[:, r:r + 1].bitcast(F32), 0.0,
                                      ALU.is_ge, ALU.add, accum_out=k.counts[:, r:r + 1]))


def bisection_rounds(k, rounds):
    for _ in range(rounds):
        for j in range(4):
            bisection_count(k, k.vown, j)
        bisection_update(k, k.vown)
    k.vown.wait()


def bisection_update(k, own):
    v = k.nc.vector
    own.wait()
    own(v.tensor_tensor(k.enough[:, :], k.counts[:, :], k.rank[:, :], ALU.is_ge))
    own.wait()
    own(v.tensor_tensor(k.set_bit[:, :], k.enough[:, :], k.bit[:, :], ALU.mult))
    own.wait()
    own(v.tensor_tensor(k.found[:, :], k.found[:, :], k.set_bit[:, :], ALU.bitwise_or))
    own(v.tensor_scalar(k.bit[:, :], k.bit[:, :], 1, None, ALU.logical_shift_right))
    own.wait()
    own(v.tensor_tensor(k.candidate[:, :], k.found[:, :], k.bit[:, :], ALU.bitwise_or))



TAPS = 7
HALF = TAPS // 2
CHOSEN_EARLY = 8


def channel_buffers(k):
    k.conv = k.sbuf("conv", [P, 2 * TAPS], F32)
    k.distance = k.sbuf("distance", [P, 3, P], F32)
    k.band = k.sbuf("band", [P, 2, 3, P], F32)
    k.term = k.sbuf("term", [P, 2, 3, P], F32)
    k.plain = k.sbuf("plain", [P, CTILES, CTX], F32)
    k.greater = k.sbuf("greater", [P, 2, CTX], F32)
    k.equal = k.sbuf("equal", [P, 2, SEQ], F32)
    k.prefix = k.sbuf("prefix", [P, 2, SEQ], F32)
    k.zeros = k.sbuf("zeros", [P, SEQ], F32)
    k.limit = k.sbuf("limit", [P, CTILES], F32)
    k.above = k.sbuf("above", [P, CTILES], F32)
    k.left = k.sbuf("left", [P, CTILES], F32)
    k.chosen = k.sbuf("chosen", [P, KT, B, SEQ], F32)
    k.conv_loaded, k.band_ready, k.plain_ready = (k.sem(x) for x in ("conv_loaded", "band_ready", "plain_ready"))


def convolution_matrix(k):
    g = k.nc.gpsimd
    k.pown(g.iota(k.distance[:, :, :], [[P, 3], [-1, P]], base=-P, channel_multiplier=1,
           allow_small_or_imprecise_dtypes=True))
    k.pown.wait()
    g.wait_ge(k.conv_loaded, 16)
    for c in range(2):
        for tap in range(TAPS):
            w = k.conv[:, c * TAPS + tap:c * TAPS + tap + 1]
            target = k.band[:, c] if tap == 0 else k.term[:, tap % 2]
            k.pown(g.tensor_scalar(target, k.distance[:, :, :], float(tap - HALF), w, ALU.is_equal, ALU.mult))
            k.pown.wait()
            if tap:
                k.pown(g.tensor_tensor(k.band[:, c], k.band[:, c], target, ALU.add))
                k.pown.wait()
    g.engine_nop().then_inc(k.band_ready, 1)


def channel_limits(k):
    v, own = k.nc.vector, k.vown
    own(v.memset(k.zeros[:, :], 0.0))
    own(v.tensor_tensor(k.limit[:, :], k.found[:, :].bitcast(F32), k.sign[:, :], ALU.mult))
    own.wait()


def choose_channels(k, r):
    v, own, two = k.nc.vector, k.vown, (0, 1)
    v.wait_ge(k.plain_ready, r + 2)
    for j in two:
        own(v.tensor_scalar(k.greater[:, j, :], k.plain[:, r + j, :], k.limit[:, r + j:r + j + 1], 0.0,
                            ALU.is_gt, ALU.add, accum_out=k.above[:, r + j:r + j + 1]))
        own(v.tensor_scalar(k.equal[:, j, :], k.plain[:, r + j, 0:SEQ], k.limit[:, r + j:r + j + 1], None, ALU.is_equal))
    own.wait()
    for j in two:
        own(v.tensor_tensor_scan(k.prefix[:, j, :], k.equal[:, j, :], k.zeros[:, :], 0.0, ALU.add, ALU.add))
    own(v.tensor_scalar(k.left[:, r:r + 2], k.above[:, r:r + 2], -1.0, float(TOPK), ALU.mult, ALU.add))
    own.wait()
    for j in two:
        own(v.scalar_tensor_tensor(k.equal[:, j, :], k.prefix[:, j, :], k.left[:, r + j:r + j + 1], k.equal[:, j, :],
                                   ALU.is_le, ALU.mult))
    own.wait()
    for j in two:
        own(v.tensor_tensor(k.chosen[:, (r + j) // B, (r + j) % B, :], k.greater[:, j, 0:SEQ], k.equal[:, j, :], ALU.add))
    own.wait()



def layer2_ffn(k, dram):
    nc, n, m = k.nc, k.norms, k.turned
    k.norms += 1
    k.turned += 1
    E, TOP = 64, 8
    channel_buffers(k)
    with ExitStack() as s:
        router = k.sbuf("router", [P, KT, E], F32, s)
        rbias = k.sbuf("rbias", [P, E], F32, s)
        ebias = k.sbuf("ebias", [E, D], F32, s)
        logits = k.sbuf("logits", [P, TILES, E], F32, s)
        shifted = k.sbuf("shifted", [P, TILES, E], F32, s)
        expd = k.sbuf("expd", [P, TILES, E], F32, s)
        top = k.sbuf("top", [P, TILES], F32, s)
        total = k.sbuf("total", [P, TILES], F32, s)
        scores = k.sbuf("scores", [P, TILES, E], F32, s)
        rest = k.sbuf("rest", [P, TILES, E], F32, s)
        best = k.sbuf("best", [P, TILES, TOP], F32, s)
        wsum = k.sbuf("wsum", [P, TILES], F32, s)
        dense = k.sbuf("dense", [P, TILES, E], F32, s)
        denseT = k.sbuf("denseT", [E, TILES * P], F32, s)
        loaded, logits_psum, shifted_ready, expd_ready, dense_ready, denseT_psum, denseT_ready, mix_psum = (
            k.sem(f"l2f_{x}") for x in ("loaded", "logits_psum", "shifted_ready", "expd_ready", "dense_ready",
                                        "denseT_psum", "denseT_ready", "mix_psum"))
        with nc.Block(no_gpsimd_drain=True) as block:

            @block.sync
            def _(sp):
                sp.dma_start(k.conv[:, :], dram["L3_xattn_conv_w"].rearrange("a c t -> a (c t)").broadcast_to([P, 2 * TAPS]))\
                  .then_inc(k.conv_loaded, 16)
                sp.dma_start(router[:, :, :], dram["routerT"].rearrange("(f p) e -> p f e", p=P)).then_inc(loaded, 16)
                sp.dma_start(rbias[:, :], dram["L2_ffn_router_bias"].unsqueeze(0).broadcast_to([P, E])).then_inc(loaded, 16)
                sp.dma_start(ebias[:, :], dram["L2_ffn_expert_bias"]).then_inc(loaded, 16)

            @block.gpsimd
            def _(g):
                norm_gpsimd(k, n)
                convolution_matrix(k)

            @block.tensor
            def _(pe):
                norm_tensor(k, n, m, k.bank[0:2])
                pe.wait_ge(loaded, 48)
                for t in range(TILES):
                    pe.wait_ge(k.xnT_ready, TILES * m + t + 1)
                    for f in range(KT):
                        last = pe.matmul(k.bank[2][:, t * E:(t + 1) * E], k.xnT[:, f, t * P:(t + 1) * P],
                                         router[:, f, :], start=f == 0, stop=f == KT - 1)
                last.then_inc(logits_psum, 1)
                pe.wait_ge(dense_ready, 1)
                for t in range(TILES):
                    last = pe.transpose(k.bank[3][0:E, t * P:(t + 1) * P], dense[:, t, :], k.ident[:, :])
                last.then_inc(denseT_psum, 1)
                pe.wait_ge(denseT_ready, 1)
                for t in range(TILES):
                    pe.matmul(k.bank[4 + t][:, :], denseT[:, t * P:(t + 1) * P], ebias[:, :],
                              start=True, stop=True).then_inc(mix_psum, 1)

            @block.vector
            def _(v):
                norm_vector(k, n)
                channel_limits(k)
                for r in range(0, CHOSEN_EARLY, 2):
                    choose_channels(k, r)
                spread = lambda a: a[:, :].unsqueeze(2).broadcast_to([P, TILES, E])
                v.wait_ge(loaded, 48)
                v.wait_ge(logits_psum, 1)
                k.vown(v.tensor_tensor(logits[:, :, :], k.bank[2][:, 0:TILES * E].rearrange("p (t e) -> p t e", e=E),
                                       rbias[:, :].unsqueeze(1).broadcast_to([P, TILES, E]), ALU.add))
                k.vown.wait()
                k.vown(v.tensor_reduce(top[:, :], logits[:, :, :], AX.X, ALU.max))
                k.vown.wait()
                v.tensor_tensor(shifted[:, :, :], logits[:, :, :], spread(top), ALU.subtract).then_inc(shifted_ready, 1)
                v.wait_ge(expd_ready, 1)
                k.vown(v.tensor_reduce(total[:, :], expd[:, :, :], AX.X, ALU.add))
                k.vown.wait()
                k.vown(v.reciprocal(total[:, :], total[:, :]))
                k.vown.wait()
                k.vown(v.tensor_tensor(scores[:, :, :], expd[:, :, :], spread(total), ALU.mult))
                k.vown.wait()
                for t in range(TILES):
                    k.vown(v.max(best[:, t, :], scores[:, t, :]))
                k.vown.wait()
                for t in range(TILES):
                    k.vown(v.match_replace(rest[:, t, :], best[:, t, :], scores[:, t, :], 0.0))
                k.vown(v.tensor_reduce(wsum[:, :], best[:, :, :], AX.X, ALU.add))
                k.vown.wait()
                v.tensor_tensor(dense[:, :, :], scores[:, :, :], rest[:, :, :], ALU.subtract).then_inc(dense_ready, 1)
                for t in range(TILES):
                    k.vown(v.scalar_tensor_tensor(k.x[:, t, :], k.xn[:, t, :], wsum[:, t:t + 1], k.x[:, t, :],
                                                  ALU.mult, ALU.add))
                k.vown.wait()
                for t in range(TILES):
                    v.wait_ge(mix_psum, t + 1)
                    k.vown(v.tensor_tensor(k.x[:, t, :], k.bank[4 + t][:, :], k.x[:, t, :], ALU.add))
                k.vown.wait()

            @block.scalar
            def _(a):
                norm_scalar(k, m, k.bank[0:2])
                for r in range(CTILES):
                    a.activation(k.plain[:, r, :], row_tile(k.ctxT, r), ACT.Copy, scale=k.sign[:, r:r + 1])\
                     .then_inc(k.plain_ready, 1)
                a.wait_ge(shifted_ready, 1)
                a.activation(expd[:, :, :], shifted[:, :, :], ACT.Exp).then_inc(expd_ready, 1)
                a.wait_ge(denseT_psum, 1)
                a.copy(denseT[:, :], k.bank[3][0:E, :]).then_inc(denseT_ready, 1)



def layer3_attention(k, dram):
    nc, n, m = k.nc, k.norms, k.turned
    k.norms += 1
    k.turned += 1
    BRANCHES = 2
    with ExitStack() as s:
        gamma = k.sbuf("bn_gamma", [P, 1], F32, s)
        beta = k.sbuf("bn_beta", [P, 1], F32, s)
        parts = k.sbuf("parts", [P, BRANCHES, KT, B, SEQ], F32, s)
        gated = k.sbuf("gated", [P, BRANCHES, KT, B, SEQ], F32, s)
        features = k.sbuf("features", [P, 2, KT, BRANCHES, B], F32, s)
        z = k.sbuf("z", [P, KT, BRANCHES, B], F32, s)
        sq = k.sbuf("sq", [P, KT, BRANCHES, B], F32, s)
        moment = k.sbuf("moment", [P, BRANCHES], F32, s)
        rstd = k.sbuf("rstd3", [P, BRANCHES], F32, s)
        names = ("loaded", "parts_ready", "sums_ready", "features_ready", "z_psum", "z_ready", "sum_psum", "sq_ready",
                 "sumsq_psum", "var_ready", "rstd_ready", "relu_ready", "exp_ready", "crucial_gated", "gated_ready", "back_psum")
        S_ = {x: k.sem(f"l3a_{x}") for x in names}
        with nc.Block(no_gpsimd_drain=True) as block:

            @block.sync
            def _(sp):
                for target, name in ((gamma, "gamma"), (beta, "beta")):
                    sp.dma_start(target[:, :], dram["L3_xattn_bn_" + name].unsqueeze(0).broadcast_to([P, 1]))\
                      .then_inc(S_["loaded"], 16)

            @block.gpsimd
            def _(g):
                norm_gpsimd(k, n)
                g.wait_ge(S_["var_ready"], 1)
                g.tensor_tensor(rstd[:, :], moment[:, :], k.minus_half[:, 0:BRANCHES], ALU.pow).then_inc(S_["rstd_ready"], 1)

            @block.vector
            def _(v):
                norm_vector(k, n)
                own = k.vown
                for r in range(CHOSEN_EARLY, CTILES, 2):
                    choose_channels(k, r)
                own.wait()
                v.wait_ge(k.xnT_ready, TILES * (m + 1))
                flat = lambda a: a.rearrange("p f b c -> p (f b c)")
                xnT = k.xnT[:, :, :].rearrange("p f c -> p (f c)")
                v.tensor_tensor(flat(parts[:, 0]), flat(k.chosen[:, :, :, :]), xnT, ALU.mult).then_inc(S_["parts_ready"], 1)
                v.wait_ge(S_["parts_ready"], 1)
                v.tensor_tensor(flat(parts[:, 1]), xnT, flat(parts[:, 0]), ALU.subtract).then_inc(S_["parts_ready"], 1)
                v.wait_ge(S_["parts_ready"], 2)
                for branch, count in ((0, TOPK), (1, SEQ - TOPK)):
                    own(v.tensor_reduce(features[:, 0, :, branch, :], parts[:, branch], AX.X, ALU.max))
                v.wait_ge(S_["sums_ready"], BRANCHES)
                for branch, count in ((0, TOPK), (1, SEQ - TOPK)):
                    own(v.tensor_scalar(features[:, 1, :, branch, :], features[:, 1, :, branch, :], 1.0 / SEQ, SEQ / count,
                                        ALU.mult, ALU.mult))
                own.wait()
                v.engine_nop().then_inc(S_["features_ready"], 1)
                v.wait_ge(S_["z_psum"], 1)
                spread = lambda a: a.unsqueeze(1).unsqueeze(3).broadcast_to([P, KT, BRANCHES, B])
                v.tensor_copy(z[:, :, :, :].rearrange("p f r b -> p (f r b)"), k.bank[2][:, 0:16]).then_inc(S_["z_ready"], 1)
                v.wait_ge(S_["z_ready"], 1)
                v.wait_ge(S_["sum_psum"], 1)
                own(v.tensor_reduce(moment[:, :], k.bank[3][:, 0:16].rearrange("p (f r b) -> p r f b", f=KT, r=BRANCHES),
                                    AX.XY, ALU.add))
                own.wait()
                own(v.tensor_scalar(moment[:, :], moment[:, :], 1.0 / (B * D), None, ALU.mult))
                own.wait()
                own(v.tensor_tensor(z[:, :, :, :], z[:, :, :, :], spread(moment[:, :]), ALU.subtract))
                own.wait()
                v.tensor_tensor(sq[:, :, :, :], z[:, :, :, :], z[:, :, :, :], ALU.mult).then_inc(S_["sq_ready"], 1)
                v.wait_ge(S_["sumsq_psum"], 1)
                own(v.tensor_reduce(moment[:, :], k.bank[4][:, 0:16].rearrange("p (f r b) -> p r f b", f=KT, r=BRANCHES),
                                    AX.XY, ALU.add))
                own.wait()
                v.tensor_scalar(moment[:, :], moment[:, :], 1.0 / (B * D), EPS, ALU.mult, ALU.add).then_inc(S_["var_ready"], 1)
                v.wait_ge(S_["rstd_ready"], 1)
                own(v.tensor_tensor(z[:, :, :, :], z[:, :, :, :], spread(rstd[:, :]), ALU.mult))
                own.wait()
                v.wait_ge(S_["loaded"], 32)
                own(v.tensor_scalar(z[:, :, :, :], z[:, :, :, :], gamma[:, 0:1], beta[:, 0:1], ALU.mult, ALU.add))
                own.wait()
                v.tensor_scalar(z[:, :, :, :], z[:, :, :, :], 0.0, None, ALU.max).then_inc(S_["relu_ready"], 1)
                v.wait_ge(S_["exp_ready"], 1)
                own(v.tensor_scalar(sq[:, :, :, :], sq[:, :, :, :], 1.0, None, ALU.add))
                own.wait()
                v.reciprocal(z[:, :, :, :], sq[:, :, :, :]).then_inc(S_["z_ready"], 1)
                v.wait_ge(S_["z_ready"], 2)
                for j in range(KT * B):
                    f, b = j % KT, j // KT
                    v.wait_ge(S_["crucial_gated"], j + 1)
                    v.scalar_tensor_tensor(gated[:, 1, f, b, :], parts[:, 1, f, b, :], z[:, f, 1, b:b + 1],
                                           gated[:, 0, f, b, :], ALU.mult, ALU.add).then_inc(S_["gated_ready"], 1)
                for t in range(TILES):
                    v.wait_ge(S_["back_psum"], t + 1)
                    own(v.tensor_tensor(k.x[:, t, :], k.bank[4 + t][:, :], k.x[:, t, :], ALU.add))
                own.wait()

            @block.scalar
            def _(a):
                norm_scalar(k, m, k.bank[0:2])
                for branch in range(BRANCHES):
                    a.wait_ge(S_["parts_ready"], branch + 1)
                    for f in range(KT):
                        for b in range(B):
                            last = a.activation(gated[:, branch, f, b, :], parts[:, branch, f, b, :], ACT.Copy,
                                                accum_out=features[:, 1, f, branch, b:b + 1])
                    last.then_inc(S_["sums_ready"], 1)
                a.wait_ge(S_["relu_ready"], 1)
                a.activation(sq[:, :, :, :], z[:, :, :, :], ACT.Exp, scale=-1.0).then_inc(S_["exp_ready"], 1)
                a.wait_ge(S_["z_ready"], 2)
                for j in range(KT * B):
                    f, b = j % KT, j // KT
                    a.activation(gated[:, 0, f, b, :], parts[:, 0, f, b, :], ACT.Copy, scale=z[:, f, 0, b:b + 1])\
                     .then_inc(S_["crucial_gated"], 1)

            @block.tensor
            def _(pe):
                norm_tensor(k, n, m, k.bank[0:2])
                pe.wait_ge(k.band_ready, 1)
                pe.wait_ge(S_["features_ready"], 1)
                for j, (blk, c) in enumerate((blk, c) for blk in (1, 0, 2) for c in range(2)):
                    first, end = max(0, 1 - blk), min(KT, KT + 1 - blk)
                    last = pe.matmul(k.bank[2][:, first * 4:end * 4], k.band[:, c, blk, :],
                                     features[:, c, first + blk - 1:end + blk - 1].rearrange("p f r b -> p (f r b)"),
                                     start=j == 0, stop=j == 5)
                last.then_inc(S_["z_psum"], 1)
                for source, ready, bank, done in ((z, "z_ready", 3, "sum_psum"), (sq, "sq_ready", 4, "sumsq_psum")):
                    pe.wait_ge(S_[ready], 1)
                    pe.matmul(k.bank[bank][:, 0:16], k.ones[:, :], source[:, :, :, :].rearrange("p f r b -> p (f r b)"),
                              start=True, stop=True).then_inc(S_[done], 1)
                for t in range(TILES):
                    pe.wait_ge(S_["gated_ready"], KT * (t // TPB + 1))
                    for f in range(KT):
                        last = pe.transpose(k.bank[4 + t][:, f * P:(f + 1) * P],
                                            gated[:, 1, f, t // TPB, t % TPB * P:(t % TPB + 1) * P], k.ident[:, :])
                    last.then_inc(S_["back_psum"], 1)



def layer3_ffn(k, dram):
    nc, n, m = k.nc, k.norms, k.turned
    k.norms += 1
    k.turned += 1
    E, R, TOP = 8, 16, 2
    SCALING = 2.0
    with ExitStack() as s:
        wb = k.sbuf("wb", [P, KT, D], F32, s)
        wra = k.sbuf("wra", [P, KT, E + E * R], F32, s)
        bm = k.sbuf("bm", [E * R, D], F32, s)
        bias = k.sbuf("bias3", [P, D], F32, s)
        lower = k.sbuf("lower", [P, E, E], F32, s)
        logits = k.sbuf("logits3", [P, TILES, E], F32, s)
        expd = k.sbuf("expd3", [P, TILES, E], F32, s)
        top = k.sbuf("top3", [P, TILES], F32, s)
        total = k.sbuf("total3", [P, TILES], F32, s)
        probs = k.sbuf("probs3", [P, TILES, E], F32, s)
        more = k.sbuf("more", [P, TILES, E, E], F32, s)
        same = k.sbuf("same", [P, TILES, E, E], F32, s)
        rank = k.sbuf("rank", [P, TILES, E], F32, s)
        weight = k.sbuf("weight3", [P, TILES, E], F32, s)
        low = k.sbuf("low", [P, TILES, E * R], F32, s)
        lowT = k.sbuf("lowT", [E * R, TILES * P], F32, s)
        loaded, lower_zeroed, lower_ready, low_psum, shifted_ready, expd_ready, low_ready, lowT_psum, lowT_ready, \
            out_psum = (k.sem(f"l3f_{x}") for x in (
                "loaded", "lower_zeroed", "lower_ready", "low_psum", "shifted_ready", "expd_ready", "low_ready",
                "lowT_psum", "lowT_ready", "out_psum"))
        with nc.Block(no_gpsimd_drain=True) as block:

            @block.sync
            def _(sp):
                sp.dma_start(bias[:, :], dram["L3_ffn_bias"].unsqueeze(0).broadcast_to([P, D])).then_inc(loaded, 16)
                sp.dma_start(wra[:, :, :], dram["wraT"].rearrange("(f p) c -> p f c", p=P)).then_inc(loaded, 16)
                sp.dma_start(wb[:, :, :], dram["wbT"].rearrange("(f p) c -> p f c", p=P)).then_inc(loaded, 16)
                sp.dma_start(bm[:, :], dram["bmT"]).then_inc(loaded, 16)

            @block.gpsimd
            def _(g):
                norm_gpsimd(k, n)
                g.memset(lower[:, :, :], 1.0).then_inc(lower_zeroed, 1)
                g.wait_ge(lower_zeroed, 1)
                g.affine_select(out=lower[:, :, :], in_=lower[:, :, :], compare_op=ALU.is_gt, fill=0.0, base=0,
                                pattern=[[1, E], [-1, E]], channel_multiplier=0).then_inc(lower_ready, 1)

            @block.tensor
            def _(pe):
                norm_tensor(k, n, m, k.bank[0:2])
                pe.wait_ge(loaded, 64)
                for t in range(TILES):
                    pe.wait_ge(k.xnT_ready, TILES * m + t + 1)
                    for f in range(KT):
                        last = pe.matmul(k.bank[2 + t // 2][:, t % 2 * 256:t % 2 * 256 + E + E * R],
                                         k.xnT[:, f, t * P:(t + 1) * P], wra[:, f, :], start=f == 0, stop=f == KT - 1)
                last.then_inc(low_psum, 1)
                for t in range(TILES):
                    for f in range(KT):
                        pe.matmul(k.bank[4 + t][:, :], k.xnT[:, f, t * P:(t + 1) * P], wb[:, f, :],
                                  start=f == 0, stop=False)
                for t in range(TILES):
                    pe.wait_ge(low_ready, t + 1)
                    last = pe.transpose(k.bank[0][:, t * P:(t + 1) * P], low[:, t, :], k.ident[:, :])
                last.then_inc(lowT_psum, 1)
                pe.wait_ge(lowT_ready, 1)
                for t in range(TILES):
                    pe.matmul(k.bank[4 + t][:, :], lowT[:, t * P:(t + 1) * P], bm[:, :],
                              start=False, stop=True).then_inc(out_psum, 1)

            @block.vector
            def _(v):
                norm_vector(k, n)
                v.wait_ge(loaded, 64)
                v.wait_ge(k.xn_ready, TILES * (n + 1))
                for t in range(TILES):
                    k.vown(v.tensor_tensor(k.x[:, t, :], k.x[:, t, :], bias[:, :], ALU.add))
                v.wait_ge(low_psum, 1)
                for h in range(2):
                    k.vown(v.tensor_copy(logits[:, 2 * h:2 * h + 2, :],
                                         k.bank[2 + h][:, :].rearrange("p (t c) -> p t c", t=2)[:, :, 0:E]))
                k.vown.wait()
                spread = lambda a: a[:, :].unsqueeze(2).broadcast_to([P, TILES, E])
                k.vown(v.tensor_reduce(top[:, :], logits[:, :, :], AX.X, ALU.max))
                k.vown.wait()
                v.tensor_tensor(logits[:, :, :], logits[:, :, :], spread(top), ALU.subtract).then_inc(shifted_ready, 1)
                v.wait_ge(expd_ready, 1)
                k.vown(v.tensor_reduce(total[:, :], expd[:, :, :], AX.X, ALU.add))
                k.vown.wait()
                k.vown(v.reciprocal(total[:, :], total[:, :]))
                k.vown.wait()
                k.vown(v.tensor_tensor(probs[:, :, :], expd[:, :, :], spread(total), ALU.mult))
                k.vown.wait()
                of_f = probs[:, :, :].unsqueeze(2).broadcast_to([P, TILES, E, E])
                of_e = probs[:, :, :].unsqueeze(3).broadcast_to([P, TILES, E, E])
                k.vown(v.tensor_tensor(more[:, :, :, :], of_f, of_e, ALU.is_gt))
                k.vown(v.tensor_tensor(same[:, :, :, :], of_f, of_e, ALU.is_equal))
                k.vown.wait()
                v.wait_ge(lower_ready, 1)
                k.vown(v.tensor_tensor(same[:, :, :, :], same[:, :, :, :],
                                       lower[:, :, :].unsqueeze(1).broadcast_to([P, TILES, E, E]), ALU.mult))
                k.vown.wait()
                k.vown(v.tensor_tensor(more[:, :, :, :], more[:, :, :, :], same[:, :, :, :], ALU.add))
                k.vown.wait()
                k.vown(v.tensor_reduce(rank[:, :, :], more[:, :, :, :], AX.X, ALU.add))
                k.vown.wait()
                k.vown(v.scalar_tensor_tensor(weight[:, :, :], rank[:, :, :], float(TOP), probs[:, :, :],
                                              ALU.is_lt, ALU.mult))
                k.vown.wait()
                k.vown(v.tensor_reduce(total[:, :], weight[:, :, :], AX.X, ALU.add))
                k.vown.wait()
                k.vown(v.reciprocal(total[:, :], total[:, :]))
                k.vown.wait()
                k.vown(v.scalar_tensor_tensor(weight[:, :, :], weight[:, :, :], SCALING, spread(total), ALU.mult, ALU.mult))
                k.vown.wait()
                for t in range(TILES):
                    h = k.bank[2 + t // 2][:, t % 2 * 256 + E:t % 2 * 256 + E + E * R]
                    v.tensor_tensor(low[:, t, :].rearrange("p (e r) -> p e r", r=R), h.rearrange("p (e r) -> p e r", r=R),
                                    weight[:, t, :].unsqueeze(2).broadcast_to([P, E, R]), ALU.mult)\
                     .then_inc(low_ready, 1)
                for t in range(TILES):
                    v.wait_ge(out_psum, t + 1)
                    k.vown(v.tensor_tensor(k.x[:, t, :], k.bank[4 + t][:, :], k.x[:, t, :], ALU.add))
                k.vown.wait()

            @block.scalar
            def _(a):
                norm_scalar(k, m, k.bank[0:2])
                a.wait_ge(shifted_ready, 1)
                a.activation(expd[:, :, :], logits[:, :, :], ACT.Exp).then_inc(expd_ready, 1)
                a.wait_ge(lowT_psum, 1)
                a.copy(lowT[:, :], k.bank[0][:, :]).then_inc(lowT_ready, 1)


def epilogue(k, out):
    nc = k.nc
    stored = k.sem("stored")
    with nc.Block(no_gpsimd_drain=True) as block:

        @block.sync
        def _(sp):
            sp.dma_start(out.rearrange("b (t p) d -> p (b t) d", p=P), k.x[:, :, :]).then_inc(stored, 16)
            sp.wait_ge(stored, 16)


LAYERS = [layer0_attention, layer0_ffn, layer1_attention, layer1_ffn, layer2_attention, layer2_ffn, layer3_attention, layer3_ffn]


def build(nc, dram, out, first=0, layers=len(LAYERS)):
    with ExitStack() as stack:
        k = Core(nc, stack)
        prologue(k, dram)
        for layer in LAYERS[first:layers]:
            k.label = layer.__name__ + "_"
            layer(k, dram)
        epilogue(k, out)


def layout(inputs):
    a = {n: np.ascontiguousarray(v) for n, v in inputs.items()}
    ctx = a.pop("ctx_4096")
    a["ctx"] = ctx
    a["ctxT"] = np.ascontiguousarray(ctx.reshape(B * CTX, D).T)
    a["wv4"] = np.ascontiguousarray(np.tile(a.pop("L1_xattn_Wv_u"), (4, 1)))
    a["wq2"] = np.ascontiguousarray(np.tile(a.pop("L1_xattn_Wq_d"), (1, 2)))
    wqk = a.pop("L1_xattn_W_qk")
    a["wqk8"] = np.ascontiguousarray(np.tile(wqk.reshape(len(wqk), 16, 1, -1), (2, 1, 4, 1)).reshape(2 * len(wqk), -1))
    a["wkv4"] = np.ascontiguousarray(np.tile(a.pop("L1_xattn_Wkv_d"), (1, 4)))
    for name, source in (("w_gateT", "L1_ffn_w_gate"), ("w_upT", "L1_ffn_w_up"), ("w_downT", "L1_ffn_w_down"),
                         ("routerT", "L2_ffn_router_weight"), ("wbT", "L3_ffn_Wb")):
        a[name] = np.ascontiguousarray(a.pop(source).T)
    G, H = 8, 128
    wkv = np.stack([a.pop("L2_xattn_k_proj_w").reshape(G, H, D), a.pop("L2_xattn_v_proj_w").reshape(G, H, D)], axis=1)
    wkv = wkv.reshape(G, 2 * H, D)
    a["wkvT"] = np.ascontiguousarray(np.concatenate([wkv, wkv[:1]]).reshape(-1, D).T)
    wq = a.pop("L2_xattn_q_proj_w").reshape(G, -1, D)
    a["wqT"] = np.ascontiguousarray(np.concatenate([wq, wq[:1]]).reshape(-1, D).T)
    wo = a.pop("L2_xattn_o_proj_w").T
    a["woT"] = np.ascontiguousarray(np.concatenate([wo, wo[:wo.shape[0] // G]]))
    low = a.pop("L3_ffn_A")
    a["wraT"] = np.ascontiguousarray(np.concatenate([a.pop("L3_ffn_Wr").T, low.reshape(-1, D).T], axis=1))
    a["bmT"] = np.ascontiguousarray(a.pop("L3_ffn_Bm").transpose(0, 2, 1).reshape(-1, D))
    return a


def kernel(**inputs):
    import numpy as _np
    import concourse.bacc as _bacc
    from concourse import mybir as _mybir
    from concourse.bass_utils import run_bass_kernel_spmd as _run

    nc = _bacc.Bacc("TRN2", target_bir_lowering=False, num_devices=1)
    arrays, dram = {}, {}
    for name, a in layout({n: _np.asarray(v) for n, v in inputs.items()}).items():
        arrays[f"in_{name}"] = a
        dram[name] = nc.dram_tensor(f"in_{name}", a.shape, _mybir.dt.from_np(a.dtype), kind="ExternalInput").ap()
    out = nc.dram_tensor("out_0_dram", (B, SEQ, D), _mybir.dt.float32, kind="ExternalOutput").ap()
    build(nc, dram, out)
    return _run(nc, [arrays], core_ids=[0]).results[0]["out_0_dram"]
```
